# Optimizing a Trainium2 kernel written in Bass

```python
import numpy as np
import jax
import jax.numpy as jnp

def _softmax(x, axis=-1):
    return jax.nn.softmax(x, axis=axis)

def _gelu(x):
    return jax.nn.gelu(x, approximate=True)

def _silu(x):
    return jax.nn.silu(x)

def _sigmoid(x):
    return jax.nn.sigmoid(x)

def _layernorm(x, axis=-1, eps=1e-05):
    m = jnp.mean(x, axis=axis, keepdims=True)
    v = jnp.var(x, axis=axis, keepdims=True)
    return (x - m) / jnp.sqrt(v + eps)

def _scatter_add(tgt, idx, src, axis=0):
    return tgt.at[idx].add(src)

def _segment_sum(src, seg, n):
    return jax.ops.segment_sum(src, seg, n)
kernel_name = 'mk_gnn_resnorm_d4_gnn_r8_876eb9'

def setup_inputs(seed: int=0):
    np.random.seed(seed)
    _w = jnp.asarray

    def _rec_inputs():
        import jax
        import jax.numpy as jnp
        _gk = jax.random.key(seed)
        x = -0.000202 + 1 * jax.random.normal(jax.random.fold_in(_gk, 1), (12500, 64), jnp.float32)
        _s = jax.random.randint(jax.random.fold_in(_gk, 2), (100000,), 0, 12500, jnp.int32)
        _d = jax.random.randint(jax.random.fold_in(_gk, 3), (100000,), 0, 12500, jnp.int32)
        _loop = jnp.arange(12500, dtype=jnp.int32)
        src = jnp.concatenate([_s, _d, _loop])
        dst = jnp.concatenate([_d, _s, _loop])
        _o = jnp.argsort(dst, stable=True)
        src = src[_o]
        dst = dst[_o]
        edge_attr_3 = 0.00117183 + 1.0004 * jax.random.normal(jax.random.fold_in(_gk, 12), (212500, 3), jnp.float32)
        edge_attr_64 = -8.16379e-05 + 0.999858 * jax.random.normal(jax.random.fold_in(_gk, 13), (212500, 64), jnp.float32)
        edge_weight = jax.random.uniform(jax.random.fold_in(_gk, 15), (212500,), jnp.float32, 0.0, 0.999999)
        edge_weight_n2 = jax.random.uniform(jax.random.fold_in(_gk, 16), (212500,), jnp.float32, 0.0, 0.999999)
        return (x, src, dst, edge_attr_3, edge_attr_64, edge_weight, edge_weight_n2)
    x, src, dst, edge_attr_3, edge_attr_64, edge_weight, edge_weight_n2 = _rec_inputs()

    def _L0_gnn_setup():
        import jax, jax.numpy as jnp
        import numpy as np
        NUM_NODES = 12500
        NUM_HYPEREDGES = 25000
        NNZ = 150000
        IN_DIM = 64
        HID_DIM = 64
        OUT_DIM = 64

        def _hypergraph_conv(x, node_idx, edge_idx, D_inv, B_inv, W, b):
            xt = x @ W
            e = B_inv[:, None] * jax.ops.segment_sum(xt[node_idx], edge_idx, num_segments=NUM_HYPEREDGES)
            out = D_inv[:, None] * jax.ops.segment_sum(e[edge_idx], node_idx, num_segments=NUM_NODES)
            return out + b
        key = jax.random.key(seed)
        k1, k2, k3, k4, k5, k6, k7, k8 = jax.random.split(key, 8)
        x = jax.random.normal(k1, (NUM_NODES, IN_DIM), dtype=jnp.float32)
        node_idx = jax.random.randint(k2, (NNZ,), 0, NUM_NODES, dtype=jnp.int64)
        edge_idx = jax.random.randint(k3, (NNZ,), 0, NUM_HYPEREDGES, dtype=jnp.int64)
        hyperedge_index = jnp.stack([node_idx, edge_idx], axis=0)
        s1 = 1.0 / np.sqrt(IN_DIM)
        s2 = 1.0 / np.sqrt(HID_DIM)
        W1 = jax.random.uniform(k4, (IN_DIM, HID_DIM), jnp.float32, -s1, s1)
        b1 = jax.random.uniform(k5, (HID_DIM,), jnp.float32, -s1, s1)
        W2 = jax.random.uniform(k6, (HID_DIM, OUT_DIM), jnp.float32, -s2, s2)
        b2 = jax.random.uniform(k7, (OUT_DIM,), jnp.float32, -s2, s2)
        return {'x': x, 'hyperedge_index': hyperedge_index, 'W1': W1, 'b1': b1, 'W2': W2, 'b2': b2}
    _L0_gnn_all = _L0_gnn_setup()
    _L0_gnn_in = {k: v for k, v in _L0_gnn_all.items() if k in ('W1', 'b1', 'W2', 'b2')}
    del _L0_gnn_all

    def _L1_gnn_setup():
        import jax, jax.numpy as jnp
        import numpy as np
        N_NODES = 12500

        def _segment_softmax(e, dst, num_segments):
            m = jax.ops.segment_max(e, dst, num_segments=num_segments)
            m = jnp.where(jnp.isfinite(m), m, 0.0)
            ex = jnp.exp(e - m[dst])
            denom = jax.ops.segment_sum(ex, dst, num_segments=num_segments)
            return ex / denom[dst]
        key = jax.random.key(seed)
        ks = jax.random.split(key, 8)
        N, E, Din, Dout = (N_NODES, 200000, 64, 64)
        node_h = jax.random.normal(ks[0], (N, Din), jnp.float32)
        edge_h = jax.random.normal(ks[1], (E, Din), jnp.float32)
        src = jax.random.randint(ks[2], (E,), 0, N, dtype=jnp.int32)
        dst = jax.random.randint(ks[3], (E,), 0, N, dtype=jnp.int32)
        s = float(np.sqrt(2.0 / (Din + Dout)))
        W_fc = jax.random.normal(ks[4], (Dout, Din), jnp.float32) * s
        W_fcr = jax.random.normal(ks[5], (Dout, Din), jnp.float32) * s
        loop_W = jax.random.normal(ks[6], (Dout, Dout), jnp.float32) * s
        return {'node_h': node_h, 'edge_h': edge_h, 'src': src, 'dst': dst, 'W_fc': W_fc, 'W_fcr': W_fcr, 'loop_W': loop_W}
    _L1_gnn_all = _L1_gnn_setup()
    _L1_gnn_in = {k: v for k, v in _L1_gnn_all.items() if k in ('W_fc', 'W_fcr', 'loop_W')}
    del _L1_gnn_all

    def _L2_gnn_setup():
        import jax, jax.numpy as jnp
        import numpy as np
        N, E, D_IN, D_OUT = (8192, 131072, 64, 64)
        EPS = 1e-08
        key = jax.random.key(seed)
        ks = jax.random.split(key, 8)
        h = jax.random.normal(ks[0], (N, D_IN), dtype=jnp.float32)
        edge_index = jax.random.randint(ks[1], (2, E), 0, N, dtype=jnp.int64 if jax.config.jax_enable_x64 else jnp.int32)
        adj_v = jax.random.uniform(ks[2], (E,), dtype=jnp.float32)
        deg_v = jax.random.uniform(ks[3], (E,), dtype=jnp.float32)
        W = jax.random.normal(ks[4], (D_IN, D_OUT), dtype=jnp.float32) / np.sqrt(D_IN)
        b = jax.random.normal(ks[5], (D_OUT,), dtype=jnp.float32) * 0.01
        deg_coeff = jnp.array([0.5, 0.0], dtype=jnp.float32)
        coeff_param = jnp.zeros((3,), dtype=jnp.float32)
        scale_param = 2.0 * jnp.ones((1,), dtype=jnp.float32)
        return {'h': h, 'edge_index': edge_index, 'adj_v': adj_v, 'deg_v': deg_v, 'W': W, 'b': b, 'deg_coeff': deg_coeff, 'coeff_param': coeff_param, 'scale_param': scale_param}
    _L2_gnn_all = _L2_gnn_setup()
    _L2_gnn_in = {k: v for k, v in _L2_gnn_all.items() if k in ('W', 'b', 'deg_coeff', 'coeff_param', 'scale_param')}
    del _L2_gnn_all

    def _L3_gnn_setup():
        import jax, jax.numpy as jnp
        import numpy as np
        M = 6250
        E = 100000
        C_IN = 64
        C_OUT = 64
        DIM = 3
        RADIUS = 1.0
        EPS = 1e-05

        def layer_norm(x, g, b):
            mu = jnp.mean(x, axis=-1, keepdims=True)
            var = jnp.mean((x - mu) ** 2, axis=-1, keepdims=True)
            return (x - mu) * jax.lax.rsqrt(var + EPS) * g + b
        key = jax.random.key(seed)
        ks = jax.random.split(key, 12)
        inv = 1.0 / np.sqrt(C_OUT)
        return {'source': jax.random.randint(ks[0], (E,), 0, M), 'target': jax.random.randint(ks[1], (E,), 0, M), 'features': jax.random.normal(ks[2], (M, C_IN), dtype=jnp.float32), 'hood_coords': jax.random.normal(ks[3], (E, DIM), dtype=jnp.float32), 'Wd1': jax.random.normal(ks[4], (DIM, C_OUT), dtype=jnp.float32) / np.sqrt(DIM), 'bd1': jnp.zeros((C_OUT,), jnp.float32), 'g1': jnp.ones((C_OUT,), jnp.float32), 'b1': jnp.zeros((C_OUT,), jnp.float32), 'Wd2': jax.random.normal(ks[5], (C_OUT, C_OUT), dtype=jnp.float32) * inv, 'bd2': jnp.zeros((C_OUT,), jnp.float32), 'g2': jnp.ones((C_OUT,), jnp.float32), 'b2': jnp.zeros((C_OUT,), jnp.float32), 'W1': jax.random.normal(ks[6], (C_IN, C_OUT), dtype=jnp.float32) / np.sqrt(C_IN), 'W2': jax.random.normal(ks[7], (C_IN, C_OUT), dtype=jnp.float32) / np.sqrt(C_IN), 'W3': jax.random.normal(ks[8], (C_IN, C_OUT), dtype=jnp.float32) / np.sqrt(C_IN)}
    _L3_gnn_all = _L3_gnn_setup()
    _L3_gnn_in = {k: v for k, v in _L3_gnn_all.items() if k in ('Wd1', 'bd1', 'g1', 'b1', 'Wd2', 'bd2', 'g2', 'b2', 'W1', 'W2', 'W3')}
    del _L3_gnn_all
    return {'x': x, 'src': src, 'dst': dst, 'edge_attr_3': edge_attr_3, 'edge_attr_64': edge_attr_64, 'edge_weight': edge_weight, 'edge_weight_n2': edge_weight_n2, 'L0_gnn_W1': _L0_gnn_in['W1'], 'L0_gnn_b1': _L0_gnn_in['b1'], 'L0_gnn_W2': _L0_gnn_in['W2'], 'L0_gnn_b2': _L0_gnn_in['b2'], 'L1_gnn_W_fc': _L1_gnn_in['W_fc'], 'L1_gnn_W_fcr': _L1_gnn_in['W_fcr'], 'L1_gnn_loop_W': _L1_gnn_in['loop_W'], 'L2_gnn_W': _L2_gnn_in['W'], 'L2_gnn_b': _L2_gnn_in['b'], 'L2_gnn_deg_coeff': _L2_gnn_in['deg_coeff'], 'L2_gnn_coeff_param': _L2_gnn_in['coeff_param'], 'L2_gnn_scale_param': _L2_gnn_in['scale_param'], 'L3_gnn_Wd1': _L3_gnn_in['Wd1'], 'L3_gnn_bd1': _L3_gnn_in['bd1'], 'L3_gnn_g1': _L3_gnn_in['g1'], 'L3_gnn_b1': _L3_gnn_in['b1'], 'L3_gnn_Wd2': _L3_gnn_in['Wd2'], 'L3_gnn_bd2': _L3_gnn_in['bd2'], 'L3_gnn_g2': _L3_gnn_in['g2'], 'L3_gnn_b2': _L3_gnn_in['b2'], 'L3_gnn_W1': _L3_gnn_in['W1'], 'L3_gnn_W2': _L3_gnn_in['W2'], 'L3_gnn_W3': _L3_gnn_in['W3']}

def reference(x, src, dst, edge_attr_3, edge_attr_64, edge_weight, edge_weight_n2, L0_gnn_W1, L0_gnn_b1, L0_gnn_W2, L0_gnn_b2, L1_gnn_W_fc, L1_gnn_W_fcr, L1_gnn_loop_W, L2_gnn_W, L2_gnn_b, L2_gnn_deg_coeff, L2_gnn_coeff_param, L2_gnn_scale_param, L3_gnn_Wd1, L3_gnn_bd1, L3_gnn_g1, L3_gnn_b1, L3_gnn_Wd2, L3_gnn_bd2, L3_gnn_g2, L3_gnn_b2, L3_gnn_W1, L3_gnn_W2, L3_gnn_W3):
    import jax
    import jax.numpy as jnp

    def _L0_gnn_ref(x, hyperedge_index, W1, b1, W2, b2):
        import jax, jax.numpy as jnp
        import numpy as np
        NUM_NODES = 12500
        NUM_HYPEREDGES = 25000
        NNZ = 150000
        IN_DIM = 64
        HID_DIM = 64
        OUT_DIM = 64

        def _hypergraph_conv(x, node_idx, edge_idx, D_inv, B_inv, W, b):
            xt = x @ W
            e = B_inv[:, None] * jax.ops.segment_sum(xt[node_idx], edge_idx, num_segments=NUM_HYPEREDGES)
            out = D_inv[:, None] * jax.ops.segment_sum(e[edge_idx], node_idx, num_segments=NUM_NODES)
            return out + b
        node_idx = hyperedge_index[0]
        edge_idx = hyperedge_index[1]
        ones = jnp.ones((node_idx.shape[0],), dtype=x.dtype)
        D = jax.ops.segment_sum(ones, node_idx, num_segments=NUM_NODES)
        B = jax.ops.segment_sum(ones, edge_idx, num_segments=NUM_HYPEREDGES)
        D_inv = jnp.where(D > 0, 1.0 / D, 0.0)
        B_inv = jnp.where(B > 0, 1.0 / B, 0.0)
        h = jax.nn.relu(_hypergraph_conv(x, node_idx, edge_idx, D_inv, B_inv, W1, b1))
        y = _hypergraph_conv(h, node_idx, edge_idx, D_inv, B_inv, W2, b2)
        return y

    def _L1_gnn_ref(node_h, edge_h, src, dst, W_fc, W_fcr, loop_W):
        import jax, jax.numpy as jnp
        import numpy as np
        N_NODES = 12500

        def _segment_softmax(e, dst, num_segments):
            m = jax.ops.segment_max(e, dst, num_segments=num_segments)
            m = jnp.where(jnp.isfinite(m), m, 0.0)
            ex = jnp.exp(e - m[dst])
            denom = jax.ops.segment_sum(ex, dst, num_segments=num_segments)
            return ex / denom[dst]
        N = node_h.shape[0]
        h = node_h @ W_fc.T
        eh = edge_h @ W_fcr.T
        alpha = _segment_softmax(eh, dst, N)
        z = h[src]
        agg = jax.ops.segment_sum(alpha * (z + eh), dst, num_segments=N)
        deg = jax.ops.segment_sum(jnp.ones((dst.shape[0],), h.dtype), dst, num_segments=N)
        h_new = jnp.where((deg > 0)[:, None], agg + h @ loop_W, h)
        return jax.nn.relu(h_new)

    def _L2_gnn_ref(h, edge_index, adj_v, deg_v, W, b, deg_coeff, coeff_param, scale_param):
        import jax, jax.numpy as jnp
        import numpy as np
        N, E, D_IN, D_OUT = (8192, 131072, 64, 64)
        EPS = 1e-08
        n_nodes = h.shape[0]
        Wh = h @ W + b
        row, col = (edge_index[0], edge_index[1])
        sc = jax.nn.softplus(deg_coeff[0] * deg_v + deg_coeff[1])
        Wr = Wh[row]
        Wc = Wh[col]
        dot = jnp.sum(Wr * Wc, axis=-1)
        nr = jnp.sqrt(jnp.sum(Wr * Wr, axis=-1))
        nc = jnp.sqrt(jnp.sum(Wc * Wc, axis=-1))
        sim = dot / jnp.maximum(nr * nc, EPS)
        sim_pos = jax.nn.relu(sim)
        sim_neg = -jax.nn.relu(-sim)
        no_diag = (row != col).astype(Wh.dtype)
        base = adj_v * sc * no_diag
        prop_pos = jax.ops.segment_sum((base * sim_pos)[:, None] * Wc, row, num_segments=n_nodes)
        prop_neg = jax.ops.segment_sum((base * sim_neg)[:, None] * Wc, row, num_segments=n_nodes)
        coeff = jax.nn.softmax(coeff_param)
        scale = jax.nn.softplus(scale_param)
        return scale * (coeff[0] * prop_pos + coeff[1] * prop_neg + coeff[2] * Wh)

    def _L3_gnn_ref(source, target, features, hood_coords, Wd1, bd1, g1, b1, Wd2, bd2, g2, b2, W1, W2, W3):
        import jax, jax.numpy as jnp
        import numpy as np
        M = 6250
        E = 100000
        C_IN = 64
        C_OUT = 64
        DIM = 3
        RADIUS = 1.0
        EPS = 1e-05

        def layer_norm(x, g, b):
            mu = jnp.mean(x, axis=-1, keepdims=True)
            var = jnp.mean((x - mu) ** 2, axis=-1, keepdims=True)
            return (x - mu) * jax.lax.rsqrt(var + EPS) * g + b
        m = features.shape[0]
        x = hood_coords / RADIUS
        d = jax.nn.gelu(layer_norm(x @ Wd1 + bd1, g1, b1), approximate=False)
        d = jax.nn.gelu(layer_norm(d @ Wd2 + bd2, g2, b2), approximate=False)
        w1 = features @ W1
        w2 = features @ W2
        w3 = features @ W3
        logits = w1[target] - w2[source] + d
        seg_max = jax.ops.segment_max(logits, target, num_segments=m)
        seg_max = jnp.where(jnp.isfinite(seg_max), seg_max, 0.0)
        e = jnp.exp(logits - seg_max[target])
        denom = jax.ops.segment_sum(e, target, num_segments=m)
        a = e / denom[target]
        out = jax.ops.segment_sum(a * (w3[source] + d), target, num_segments=m)
        return out
    edge_index = jnp.stack([src, dst])
    x = _layernorm(x + _L0_gnn_ref(x, edge_index, L0_gnn_W1, L0_gnn_b1, L0_gnn_W2, L0_gnn_b2), axis=-1)
    x = _layernorm(x + _L1_gnn_ref(x, edge_attr_64, src, dst, L1_gnn_W_fc, L1_gnn_W_fcr, L1_gnn_loop_W), axis=-1)
    x = _layernorm(x + _L2_gnn_ref(x, edge_index, edge_weight, edge_weight_n2, L2_gnn_W, L2_gnn_b, L2_gnn_deg_coeff, L2_gnn_coeff_param, L2_gnn_scale_param), axis=-1)
    x = _layernorm(x + _L3_gnn_ref(src, dst, x, edge_attr_3, L3_gnn_Wd1, L3_gnn_bd1, L3_gnn_g1, L3_gnn_b1, L3_gnn_Wd2, L3_gnn_bd2, L3_gnn_g2, L3_gnn_b2, L3_gnn_W1, L3_gnn_W2, L3_gnn_W3), axis=-1)
    return x

_drawn_inputs = setup_inputs


def setup_inputs(seed=0):
    import zlib

    import numpy as np

    out = dict(_drawn_inputs(seed))
    spreads = {'L2_gnn_coeff_param': (0.0, 0.409),
     'L3_gnn_bd1': (0.0, 0.1),
     'L3_gnn_g1': (1.0, 0.2),
     'L3_gnn_b1': (0.0, 0.1),
     'L3_gnn_bd2': (0.0, 0.1),
     'L3_gnn_g2': (1.0, 0.2),
     'L3_gnn_b2': (0.0, 0.1)}
    factors = {'edge_weight_n2': 3.66, 'L0_gnn_W1': 8.0, 'L2_gnn_b': 7.056, 'L3_gnn_W1': 8.0}
    for name, (base, spread) in spreads.items():
        noise = np.random.default_rng([zlib.crc32(name.encode()), seed]).standard_normal(out[name].shape)
        drawn = base * np.exp(spread * noise) if base else spread * noise
        out[name] = jnp.asarray(drawn.astype(out[name].dtype))
    for name, factor in factors.items():
        out[name] = (out[name] * factor).astype(out[name].dtype)
    return out
```

```python
import concourse.bass as bass
from concourse import mybir
from contextlib import ExitStack

F32 = mybir.dt.float32
I32 = mybir.dt.int32
BF16 = mybir.dt.bfloat16
ALU = mybir.AluOpType
ACT = mybir.ActivationFunctionType
AX = mybir.AxisListType

P = 128
F = 64
N = 12500
E = 212500
NJ = -(-(N + 1) // P)
NP = NJ * P
HI = NJ
T = 64
NT = -(-E // (P * 2 * T)) * 2 * T
NCH = NT // T
EP = P * NT
ROWS = EP + 1
BIG = 1.0e38
NOROW = float(1 << 21)
EPS = 1e-5
G = 14
NG = NJ // G


class Counter:

    def __init__(self, sem):
        self.sem, self.base = sem, 0


def gnn_resnorm(nc, x_in, src_in, dst_in, attr3_in, attr64_in, w_in, w2_in, W, out):
    top = ExitStack()

    unique = [0]

    def alloc(ctx, name, shape, dt=F32):
        unique[0] += 1
        return ctx.enter_context(nc.sbuf_tensor(f"{name}_{unique[0]}", shape, dt))

    def ps(ctx, name, shape, dt=F32):
        unique[0] += 1
        return ctx.enter_context(nc.psum_tensor(f"{name}_{unique[0]}", shape, dt))

    phase_sems = []

    def lasting(name):
        return top.enter_context(nc.semaphore(name))

    def sem(name):
        phase_sems.append(nc.alloc_semaphore(name=name))
        return phase_sems[-1]

    def phase(build):
        def run(*args, **kw):
            build(*args, **kw)
            nc.clear_and_free_semaphores(list(phase_sems))
            phase_sems.clear()
            nc.all_engine_barrier()
        return run

    def dram(name, shape, dt=F32):
        return nc.dram_tensor(name, shape, dt).ap()

    tab = dram("tab", [NP, F])
    tab65 = dram("tab65", [NP, F + 1])
    tab128 = dram("tab128", [NP, 2 * F])
    sums = dram("sums", [ROWS, F])
    sums2 = dram("sums2", [ROWS, 2 * F])
    maxes = dram("maxes", [EP, F])
    dists = dram("dists", [EP, F])
    spread = dram("spread", [EP, F + 1])
    rec1 = dram("rec1", [EP, 4], I32)
    rec2 = dram("rec2", [EP, 4], I32)
    skey = dram("skey", [EP + 2], I32)
    sdst = dram("sdst", [EP], I32)
    sbase = dram("sbase", [EP])
    flat = {n: dram(n, [NP], I32) for n in ("end_d", "end_s", "start_s")}
    flatf = {n: dram(n, [NP]) for n in ("cnt_d", "cnt_s")}

    def cols(ap, c, w=T, first=0):
        if len(ap.shape) == 1:
            return ap.rearrange("(p t) -> p t", p=P)[:, bass.ds(c * w + first, w)]
        return ap.rearrange("(p t) f -> p t f", p=P)[:, bass.ds(c * w + first, w), :]

    X = alloc(top, "X", [P, NJ, F])
    ident = alloc(top, "ident", [P, P])
    keep = {o: alloc(top, f"keep_{o}", [P, NT]) for o in "ds"}
    neg = alloc(top, "neg_d", [P, NT])
    fk = {o: alloc(top, f"fk_{o}", [P, 1]) for o in "ds"}
    aT = {o: alloc(top, f"aT_{o}", [F, P]) for o in "ds"}
    end0 = {o: alloc(top, f"end0_{o}", [P, 1], I32) for o in "ds"}
    endp = {o: alloc(top, f"endp_{o}", [P, NJ], I32) for o in "ds"}
    startp = alloc(top, "startp", [P, NJ], I32)
    inv = {o: alloc(top, f"inv_{o}", [P, NJ]) for o in "ds"}
    co = alloc(top, "co", [P, 16])
    zero = alloc(top, "zero", [P, 1])
    bd = {n: alloc(top, f"bd_{n}", [P, P]) for n in ("a1", "a2", "fc", "fcr", "loop", "w2l", "d2", "q1", "q2", "q3")}

    chain = {e: Counter(lasting(f"chain_{e}")) for e in ("dve", "act", "pool", "pe")}

    def linker(eng, which):
        k = chain[which]

        def link(ins):
            k.base += 1
            ins.then_inc(k.sem, 1)
            eng.wait_ge(k.sem, k.base)
        return link

    @phase
    def constants():
        loaded, made = sem("w_loaded"), sem("ident_made")
        zeroed = sem("bd_zeroed")
        tr_ready, tr_done = sem("wt_ready"), sem("wt_done")
        order = {"a1": "L0_gnn_W1", "a2": "L0_gnn_W2", "fc": "L1_gnn_W_fc", "fcr": "L1_gnn_W_fcr",
                 "loop": "L1_gnn_loop_W", "w2l": "L2_gnn_W", "d2": "L3_gnn_Wd2",
                 "q1": "L3_gnn_W1", "q2": "L3_gnn_W2", "q3": "L3_gnn_W3"}
        with ExitStack() as c, nc.Block() as block:
            tp = ps(c, "wt_ps", [P, P])
            mean = alloc(c, "mean_d2", [P, 1])
            st = alloc(c, "soft", [P, 8])

            @block.gpsimd
            def _(pool):
                pool.memset(ident[:, :], 0.0).then_inc(made, 1)
                pool.wait_ge(made, 1)
                pool.affine_select(out=ident[:, :], in_=ident[:, :], compare_op=ALU.not_equal, fill=1.0, base=0,
                                   pattern=[[-1, P]], channel_multiplier=1).then_inc(made, 1)

            @block.sync
            def _(sp):
                sp.wait_ge(zeroed, len(order) + 2)
                for n, full in order.items():
                    for h in (0, F):
                        sp.dma_start(bd[n][h:h + F, h:h + F], W[full]).then_inc(loaded, 16)
                sp.dma_start(X[:, :, :], x_in.rearrange("(p j) f -> p j f", p=P)).then_inc(loaded, 16)
                for k, (n, w) in enumerate((("L2_gnn_deg_coeff", 2), ("L2_gnn_coeff_param", 3), ("L2_gnn_scale_param", 1))):
                    v = W[n].rearrange("(a n) -> a n", a=1).to_broadcast([P, w])
                    sp.dma_start(co[:, 4 * k:4 * k + w], v).then_inc(loaded, 16)

            @block.vector
            def _(dve):
                link = linker(dve, "dve")
                for n in order:
                    dve.memset(bd[n][:, :], 0.0).then_inc(zeroed, 1)
                dve.memset(co[:, :], 0.0).then_inc(zeroed, 1)
                dve.memset(zero[:, :], 0.0).then_inc(zeroed, 1)
                dve.wait_ge(loaded, 16 * (2 * len(order) + 4))
                for k, n in enumerate(("fc", "fcr")):
                    dve.wait_ge(tr_ready, k + 1)
                    dve.tensor_copy(bd[n][:, :], tp[:, :]).then_inc(tr_done, 1)
                link(dve.reduce_sum(mean[:, :], bd["d2"][:, :], axis=AX.X))
                link(dve.tensor_scalar(mean[:, :], mean[:, :], 1.0 / F, None, ALU.mult))
                for h in (0, F):
                    link(dve.tensor_scalar(bd["d2"][h:h + F, h:h + F], bd["d2"][h:h + F, h:h + F],
                                           mean[h:h + F, 0:1], None, ALU.subtract))
                link(dve.reduce_max(st[:, 0:1], co[:, 4:7], axis=AX.X))
                link(dve.tensor_scalar(co[:, 4:7], co[:, 4:7], st[:, 0:1], None, ALU.subtract))
                dve.tensor_scalar(st[:, 1:2], co[:, 8:9], -1.0, None, ALU.mult).then_inc(chain["dve"].sem, 1)
                chain["dve"].base += 1
                dve.wait_ge(chain["dve"].sem, chain["dve"].base)
                link(dve.tensor_tensor(st[:, 1:2], st[:, 1:2], co[:, 8:9], ALU.min))
                dve.sem_inc(tr_done, 1)
                dve.wait_ge(tr_ready, 3)
                link(dve.reduce_sum(st[:, 2:3], co[:, 4:7], axis=AX.X))
                link(dve.reciprocal(st[:, 3:4], st[:, 2:3]))
                link(dve.tensor_scalar(co[:, 4:7], co[:, 4:7], st[:, 3:4], None, ALU.mult))
                link(dve.tensor_scalar(st[:, 4:5], co[:, 8:9], 0.0, None, ALU.max))
                link(dve.tensor_tensor(co[:, 8:9], st[:, 4:5], st[:, 1:2], ALU.add))
                link(dve.tensor_scalar(co[:, 4:7], co[:, 4:7], co[:, 8:9], None, ALU.mult))

            @block.scalar
            def _(act):
                link = linker(act, "act")
                act.wait_ge(tr_done, 3)
                link(act.activation(co[:, 4:7], co[:, 4:7], ACT.Exp))
                link(act.activation(st[:, 1:2], st[:, 1:2], ACT.Exp))
                act.activation(st[:, 1:2], st[:, 1:2], ACT.Ln, bias=1.0).then_inc(tr_ready, 1)

            @block.tensor
            def _(pe):
                pe.wait_ge(made, 2)
                pe.wait_ge(loaded, 16 * (2 * len(order) + 4))
                for k, n in enumerate(("fc", "fcr")):
                    if k:
                        pe.wait_ge(tr_done, k)
                    pe.transpose(tp[:, :], bd[n][:, :], ident[:, :]).then_inc(tr_ready, 1)

    @phase
    def counts(hist_bases):
        K = 16
        NK = NT // K
        keys_in, digits = sem("keys_in"), sem("digits_ready")
        oh_ready, oh_used = sem("onehot_ready"), sem("onehot_used")
        hist, post, pre = sem("hist_ready"), sem("hist_sums"), sem("hist_copied")
        stored, back = sem("ptr_stored"), sem("ptr_back")
        with ExitStack() as c, nc.Block() as block:
            ki = alloc(c, "ki", [P, NT], I32)
            kj = alloc(c, "kj", [P, NT], I32)
            dig = {d: alloc(c, f"dig_{d}", [P, NT], BF16) for d in ("dl", "dh", "sl", "sh")}
            oh = [{d: alloc(c, f"oh_{d}{b}", [P, K, P], BF16) for d in dig} for b in range(2)]
            iota_i = alloc(c, "iota_i", [P, P], I32)
            iota = alloc(c, "iota", [P, P], BF16)
            zb = alloc(c, "zb", [P, P], BF16)
            ones = alloc(c, "ones_c", [P, P])
            upper = alloc(c, "upper_c", [P, P])
            Hd, Hs, HsT = ps(c, "Hd", [P, P]), ps(c, "Hs", [P, P]), ps(c, "HsT", [P, P])
            pre_d, pre_s = ps(c, "pre_d", [P, 1]), ps(c, "pre_s", [P, 1])
            bl, bh = ps(c, "bl", [P, P]), ps(c, "bh", [P, P])
            h = {o: alloc(c, f"h_{o}", [P, P]) for o in "ds"}
            hT = alloc(c, "hT", [P, P])
            cum = {o: alloc(c, f"cum_{o}", [P, P]) for o in "ds"}
            tmp = alloc(c, "tmp_c", [P, P])
            pi = {n: alloc(c, f"pi_{n}", [P, P], I32) for n in flat}
            cb = {o: alloc(c, f"cb_{o}", [P, NJ]) for o in "ds"}
            cm = alloc(c, "cm", [P, NJ])
            const = sem("count_consts")
            hT2 = alloc(c, "hT2", [P, P])

            @block.gpsimd
            def _(pool):
                pool.memset(ones[:, :], 1.0).then_inc(const, 1)
                pool.memset(zb[:, :], 0.0).then_inc(const, 1)
                pool.iota(iota_i[:, :], pattern=[[1, P]], base=0, channel_multiplier=0).then_inc(const, 1)
                pool.wait_ge(const, 3)
                pool.affine_select(out=upper[:, :], in_=ones[:, :], compare_op=ALU.is_gt, fill=0.0, base=0,
                                   pattern=[[1, P]], channel_multiplier=-1).then_inc(const, 1)

            @block.sync
            def _(sp):
                sp.dma_start(ki[:, :], dst_in[1:EP + 1].rearrange("(p t) -> p t", p=P)).then_inc(keys_in, 16)
                sp.dma_start(kj[:, :], src_in.rearrange("(p t) -> p t", p=P)).then_inc(keys_in, 16)
                sp.wait_ge(post, 2)
                for o in "ds":
                    sp.dma_start(flatf[f"cnt_{o}"].rearrange("(h l) -> h l", l=P), h[o][0:HI, :]).then_inc(stored, 16)
                for n in flat:
                    sp.dma_start(flat[n].rearrange("(h l) -> h l", l=P), pi[n][0:HI, :]).then_inc(stored, 16)
                sp.wait_ge(stored, 80)
                for o in "ds":
                    sp.dma_start(cb[o][:, :], flatf[f"cnt_{o}"].rearrange("(p j) -> p j", p=P)).then_inc(back, 16)
                    sp.dma_start(endp[o][:, :], flat[f"end_{o}"].rearrange("(p j) -> p j", p=P)).then_inc(back, 16)
                sp.dma_start(startp[:, :], flat["start_s"].rearrange("(p j) -> p j", p=P)).then_inc(back, 16)

            @block.vector
            def _(dve):
                link = linker(dve, "dve")
                dve.wait_ge(const, 4)
                dve.wait_ge(keys_in, 32)
                dve.tensor_copy(iota[:, :], iota_i[:, :]).then_inc(digits, 1)
                for k, (keys, l, hh) in enumerate(((ki, "dl", "dh"), (kj, "sl", "sh"))):
                    sc = oh[0]["dl"][:, :, :].rearrange("p a b -> p (a b)").bitcast(I32)
                    half = K * P // 2
                    for a in range(0, NT, half):
                        n = min(half, NT - a)
                        link(dve.tensor_scalar(sc[:, 0:n], keys[:, a:a + n], P - 1, None, ALU.bitwise_and))
                        link(dve.tensor_copy(dig[l][:, a:a + n], sc[:, 0:n]))
                        link(dve.tensor_scalar(sc[:, 0:n], keys[:, a:a + n], 7, None, ALU.logical_shift_right))
                        link(dve.tensor_copy(dig[hh][:, a:a + n], sc[:, 0:n]))
                dve.wait_ge(digits, 1)

                def onehots(i, b):
                    if not isinstance(i, int) or i:
                        dve.wait_ge(oh_used, i * 2 + b - 1)
                    for d in dig:
                        v = dig[d][:, bass.ds((i * 2 + b) * K, K)].unsqueeze(2).to_broadcast([P, K, P])
                        w = iota[:, :].unsqueeze(1).to_broadcast([P, K, P])
                        dve.tensor_tensor(oh[b][d][:, :, :], v, w, ALU.is_equal).then_inc(oh_ready, 1)
                onehots(0, 0)
                onehots(0, 1)
                with dve.Fori(1, NK // 2) as i:
                    onehots(i, 0)
                    onehots(i, 1)
                dve.wait_ge(hist, 1)
                link(dve.tensor_copy(h["d"][:, :], Hd[:, :]))
                link(dve.tensor_copy(h["s"][:, :], Hs[:, :]))
                link(dve.tensor_copy(hT[:, :], HsT[:, :]))
                for o in "ds":
                    link(dve.tensor_tensor_scan(cum[o][:, :], ones[:, :], h[o][:, :], 0.0, ALU.mult, ALU.add))
                dve.sem_inc(pre, 1)
                dve.wait_ge(post, 1)
                for o, pp in (("d", pre_d), ("s", pre_s)):
                    link(dve.tensor_scalar(cum[o][:, :], cum[o][:, :], pp[:, 0:1], None, ALU.add))
                    link(dve.tensor_scalar(tmp[:, :], h[o][:, :], 1.0, None, ALU.min))
                    if o == "s":
                        link(dve.tensor_tensor(hT2[:, :], cum[o][:, :], h[o][:, :], ALU.subtract))
                        link(dve.tensor_scalar(hT2[:, :], hT2[:, :], -NOROW, None, ALU.add))
                        link(dve.tensor_tensor(hT2[:, :], hT2[:, :], tmp[:, :], ALU.mult))
                        link(dve.tensor_scalar(hT2[:, :], hT2[:, :], NOROW, None, ALU.add))
                        link(dve.tensor_copy(pi["start_s"][:, :], hT2[:, :]))
                    link(dve.tensor_scalar(cum[o][:, :], cum[o][:, :], -1.0 - EP, None, ALU.add))
                    link(dve.tensor_tensor(cum[o][:, :], cum[o][:, :], tmp[:, :], ALU.mult))
                    link(dve.tensor_scalar(cum[o][:, :], cum[o][:, :], float(EP), None, ALU.add))
                    link(dve.tensor_copy(pi[f"end_{o}"][:, :], cum[o][:, :]))
                for dst_t, sp_t in ((hist_bases[0], bl), (hist_bases[1], bh)):
                    link(dve.tensor_copy(tmp[:, :], sp_t[:, :]))
                    link(dve.tensor_tensor_scan(dst_t[:, :], ones[:, :], tmp[:, :], 0.0, ALU.mult, ALU.add))
                    link(dve.tensor_tensor(dst_t[:, :], dst_t[:, :], tmp[:, :], ALU.subtract))
                dve.sem_inc(post, 1)
                dve.wait_ge(back, 80)
                for o in "ds":
                    link(dve.tensor_scalar(cm[:, :], cb[o][:, :], 1.0, None, ALU.max))
                    link(dve.reciprocal(inv[o][:, :], cm[:, :]))
                    link(dve.tensor_scalar(cm[:, :], cb[o][:, :], 1.0, None, ALU.min))
                    link(dve.tensor_tensor(inv[o][:, :], inv[o][:, :], cm[:, :], ALU.mult))

            @block.tensor
            def _(pe):
                pe.wait_ge(const, 4)
                for acc in (Hd, Hs, HsT):
                    pe.matmul(acc[:, :], zb[:, :], zb[:, :], start=True, stop=False)

                def tile_counts(i, b):
                    pe.wait_ge(oh_ready, (i * 2 + b + 1) * 4)
                    for k in range(K):
                        o = oh[b]
                        pe.matmul(Hd[:, :], o["dh"][:, k, :], o["dl"][:, k, :], start=False, stop=False)
                        pe.matmul(Hs[:, :], o["sh"][:, k, :], o["sl"][:, k, :], start=False, stop=False)
                        last = pe.matmul(HsT[:, :], o["sl"][:, k, :], o["sh"][:, k, :], start=False, stop=False)
                    last.then_inc(oh_used, 1)
                with pe.Fori(0, NK // 2) as i:
                    tile_counts(i, 0)
                    tile_counts(i, 1)
                for acc in (Hd, Hs, HsT):
                    last = pe.matmul(acc[:, :], zb[:, :], zb[:, :], start=False, stop=True)
                last.then_inc(hist, 1)
                pe.wait_ge(pre, 1)
                pe.matmul(pre_d[:, :], upper[:, :], cum["d"][:, P - 1:P], start=True, stop=True)
                pe.matmul(pre_s[:, :], upper[:, :], cum["s"][:, P - 1:P], start=True, stop=True)
                pe.matmul(bl[:, :], ones[:, :], h["s"][:, :], start=True, stop=True)
                pe.matmul(bh[:, :], ones[:, :], hT[:, :], start=True, stop=True).then_inc(post, 1)

    @phase
    def sort_pass(k, base):
        rec_out = rec1 if k == 0 else rec2
        K = 16
        loaded = [sem(f"sort{k}_in{b}") for b in range(2)]
        moved = [sem(f"sort{k}_out{b}") for b in range(2)]
        packed, dig_r, oh_r = sem(f"sort{k}_packed"), sem(f"sort{k}_digits"), sem(f"sort{k}_onehots")
        started = sem(f"sort{k}_started")
        packed4, before_ready = sem(f"sort{k}_columns"), sem(f"sort{k}_before")
        ranked, counted, idx_r, const = sem(f"sort{k}_ranked"), sem(f"sort{k}_counted"), sem(f"sort{k}_idx"), sem(f"sort{k}_consts")
        with ExitStack() as c, nc.Block() as block:
            recs = [alloc(c, f"recs{b}", [P, T, 4], I32) for b in range(2)]
            raw = [alloc(c, f"raw{b}", [P, 4, T], I32) for b in range(2)]
            di = alloc(c, "di", [P, T], I32)
            db = alloc(c, "db", [P, T], BF16)
            ohs = alloc(c, "ohs", [P, T, P], BF16)
            junk = alloc(c, "junk", [P, P])
            pos = alloc(c, "pos", [P, T])
            pi = alloc(c, "posi", [P, T], I32)
            pl = alloc(c, "posl", [P, T], I32)
            idx = [alloc(c, f"sidx{b}", [P, T], I32) for b in range(2)]
            iota_i = alloc(c, "iota_i", [P, P], I32)
            iota = alloc(c, "iota", [P, P], BF16)
            ones_b = alloc(c, "ones_b", [P, P], BF16)
            ones_f = alloc(c, "ones_f", [P, P])
            before = alloc(c, "before", [P, P], BF16)
            rest = alloc(c, "rest", [P, P], BF16)
            acc = ps(c, "acc", [P, P])

            @block.sync
            def _(sp):
                def load(i, b):
                    if not isinstance(i, int) or i:
                        sp.wait_ge(moved[b], i * 16 * T)
                        sp.wait_ge(packed, i * 2 + b - 1)
                    ch = i * 2 + b
                    if k == 0:
                        for q, a in enumerate((src_in, dst_in[1:EP + 1], w_in, w2_in)):
                            d = raw[b][:, q, :]
                            sp.dma_start(d if q < 2 else d.bitcast(F32), cols(a, ch)).then_inc(loaded[b], 16)
                    else:
                        sp.dma_start(recs[b][:, :, :], cols(rec1, ch)).then_inc(loaded[b], 16)
                load(0, 0)
                load(0, 1)
                with sp.Fori(1, NCH // 2) as i:
                    load(i, 0)
                    load(i, 1)

            nl = 64 if k == 0 else 16

            @block.scalar
            def _(act):
                def pack(i, b):
                    act.wait_ge(loaded[b], (i + 1) * nl)
                    if not isinstance(i, int) or i:
                        act.wait_ge(moved[b], i * 16 * T)
                    for q in range(4):
                        s, d = raw[b][:, q, :], recs[b][:, :, q]
                        if q >= 2:
                            s, d = s.bitcast(F32), d.bitcast(F32)
                        act.activation(d, s, ACT.Copy).then_inc(packed4, 1)
                    act.wait_ge(packed4, (i * 2 + b + 1) * 4)
                    act.sem_inc(packed, 1)
                if k == 0:
                    pack(0, 0)
                    pack(0, 1)
                    with act.Fori(1, NCH // 2) as i:
                        pack(i, 0)
                        pack(i, 1)
                else:
                    def fwd(i, b):
                        act.wait_ge(loaded[b], (i + 1) * nl)
                        act.sem_inc(packed, 1)
                    with act.Fori(0, NCH // 2) as i:
                        fwd(i, 0)
                        fwd(i, 1)

            @block.gpsimd
            def _(pool):
                pool.memset(ones_b[:, :], 1.0).then_inc(const, 1)
                pool.memset(ones_f[:, :], 1.0).then_inc(const, 1)
                pool.iota(iota_i[:, :], pattern=[[1, P]], base=0, channel_multiplier=0).then_inc(const, 1)
                pool.wait_ge(const, 3)
                pool.affine_select(out=before[:, :], in_=ones_b[:, :], compare_op=ALU.is_gt, fill=0.0, base=0,
                                   pattern=[[1, P]], channel_multiplier=-1).then_inc(const, 1)
                pool.affine_select(out=rest[:, :], in_=ones_b[:, :], compare_op=ALU.is_ge, fill=0.0, base=0,
                                   pattern=[[-1, P]], channel_multiplier=1).then_inc(const, 1)

                def scatter(i, b):
                    pool.wait_ge(idx_r, i * 2 + b + 1)
                    pool.sem_inc(started, 1)
                    for j in range(T):
                        pool.indirect_dma_start(rec_out, bass.IndirectOffsetOnAxis(ap=idx[b][:, j:j + 1], axis=0),
                                                recs[b][:, j, :], None).then_inc(moved[b], 16)
                with pool.Fori(0, NCH // 2) as i:
                    scatter(i, 0)
                    scatter(i, 1)
                for b in range(2):
                    pool.wait_ge(moved[b], NCH // 2 * 16 * T)

            @block.vector
            def _(dve):
                dve.wait_ge(const, 5)
                dve.tensor_copy(iota[:, :], iota_i[:, :]).then_inc(dig_r, 1)
                dve.wait_ge(dig_r, 1)
                ndig = 1

                def rank(i, b):
                    ch = i * 2 + b
                    dve.wait_ge(packed, ch + 1)
                    if k == 0:
                        dve.tensor_scalar(di[:, :], recs[b][:, :, 0], P - 1, None, ALU.bitwise_and).then_inc(dig_r, 1)
                    else:
                        dve.tensor_scalar(di[:, :], recs[b][:, :, 0], 7, None, ALU.logical_shift_right).then_inc(dig_r, 1)
                    dve.wait_ge(dig_r, ch * 5 + 2)
                    dve.tensor_copy(db[:, :], di[:, :]).then_inc(dig_r, 1)
                    dve.wait_ge(dig_r, ch * 5 + 3)
                    if not isinstance(i, int) or i or b:
                        dve.wait_ge(counted, ch * T)
                    for q in range(T // K):
                        v = db[:, q * K:q * K + K].unsqueeze(2).to_broadcast([P, K, P])
                        w = iota[:, :].unsqueeze(1).to_broadcast([P, K, P])
                        dve.tensor_tensor(ohs[:, q * K:q * K + K, :], v, w, ALU.is_equal).then_inc(oh_r, 1)
                    dve.wait_ge(oh_r, (ch + 1) * (T // K))
                    for t in range(T):
                        dve.wait_ge(before_ready, ch * T + t + 1)
                        dve.tensor_tensor_reduce(out=junk[:, :], in0=acc[:, :], in1=ohs[:, t, :], scale=1.0, scalar=0.0,
                                                 op0=ALU.mult, op1=ALU.add, accum_out=pos[:, t:t + 1]).then_inc(ranked, 1)
                        dve.wait_ge(ranked, ch * T + t + 1)
                    dve.tensor_copy(pi[:, :], pos[:, :]).then_inc(dig_r, 1)
                    dve.wait_ge(dig_r, ch * 5 + 4)
                    if not isinstance(i, int) or i:
                        dve.wait_ge(moved[b], i * 16 * T)
                    if k == 0:
                        dve.tensor_scalar(pl[:, :], pi[:, :], P - 1, None, ALU.bitwise_and).then_inc(dig_r, 1)
                        dve.tensor_scalar(di[:, :], pi[:, :], 7, None, ALU.logical_shift_right).then_inc(dig_r, 1)
                        dve.wait_ge(dig_r, ch * 5 + 6)
                        dve.scalar_tensor_tensor(idx[b][:, :], pl[:, :], float(NT), di[:, :], ALU.mult, ALU.add).then_inc(idx_r, 1)
                    else:
                        dve.tensor_copy(pl[:, :], pi[:, :]).then_inc(dig_r, 1)
                        dve.tensor_copy(di[:, :], pi[:, :]).then_inc(dig_r, 1)
                        dve.tensor_copy(idx[b][:, :], pi[:, :]).then_inc(idx_r, 1)
                    dve.wait_ge(idx_r, ch + 1)
                    dve.wait_ge(dig_r, ch * 5 + 6)
                rank(0, 0)
                rank(0, 1)
                with dve.Fori(1, NCH // 2) as i:
                    rank(i, 0)
                    rank(i, 1)

            @block.tensor
            def _(pe):
                pe.wait_ge(const, 5)
                pe.matmul(acc[:, :], ones_f[0:1, :], base[0:1, :], start=True, stop=True)

                def count(i, b):
                    ch = i * 2 + b
                    pe.wait_ge(oh_r, (ch + 1) * (T // K))
                    for t in range(T):
                        pe.matmul(acc[:, :], before[:, :], ohs[:, t, :], start=False, stop=True,
                                  skip_group_check=True).then_inc(before_ready, 1)
                        pe.wait_ge(ranked, ch * T + t + 1)
                        pe.matmul(acc[:, :], rest[:, :], ohs[:, t, :], start=False, stop=False,
                                  skip_group_check=True).then_inc(counted, 1)
                with pe.Fori(0, NCH // 2) as i:
                    count(i, 0)
                    count(i, 1)

    @phase
    def unpack_sorted():
        ld, pr, wr, ax = sem("rec_loaded"), sem("rec_ready"), sem("rec_written"), sem("softplus_ready")
        with ExitStack() as c, nc.Block() as block:
            r = alloc(c, "r", [P, NT, 4], I32)
            s_c, d_c = alloc(c, "s_c", [P, NT], I32), alloc(c, "d_c", [P, NT], I32)
            w_c, v = alloc(c, "w_c", [P, NT]), alloc(c, "v", [P, NT])
            a, b = alloc(c, "a", [P, NT]), alloc(c, "b", [P, NT])
            end = alloc(c, "end", [1, 2], I32)

            @block.sync
            def _(sp):
                sp.dma_start(r[:, :, :], rec2.rearrange("(p t) f -> p t f", p=P)).then_inc(ld, 16)
                sp.wait_ge(pr, 1)
                sp.dma_start(skey[1:EP + 1].rearrange("(p t) -> p t", p=P), s_c[:, :]).then_inc(wr, 16)
                sp.dma_start(skey[0:1].rearrange("(a n) -> a n", a=1), end[:, 0:1]).then_inc(wr, 16)
                sp.dma_start(skey[EP + 1:EP + 2].rearrange("(a n) -> a n", a=1), end[:, 1:2]).then_inc(wr, 16)
                sp.dma_start(sdst.rearrange("(p t) -> p t", p=P), d_c[:, :]).then_inc(wr, 16)
                sp.wait_ge(pr, 2)
                sp.dma_start(sbase.rearrange("(p t) -> p t", p=P), w_c[:, :]).then_inc(wr, 16)
                sp.wait_ge(wr, 80)

            @block.vector
            def _(dve):
                link = linker(dve, "dve")
                dve.wait_ge(ld, 16)
                link(dve.memset(end[:, :], -1))
                link(dve.tensor_copy(s_c[:, :], r[:, :, 0]))
                link(dve.tensor_copy(d_c[:, :], r[:, :, 1]))
                dve.sem_inc(pr, 1)
                link(dve.tensor_copy(v[:, :], r[:, :, 3].bitcast(F32)))
                link(dve.tensor_scalar(v[:, :], v[:, :], co[:, 0:1], co[:, 1:2], ALU.mult, ALU.add))
                link(dve.tensor_scalar(a[:, :], v[:, :], -1.0, None, ALU.mult))
                link(dve.tensor_tensor(a[:, :], a[:, :], v[:, :], ALU.min))
                dve.sem_inc(ax, 1)
                link(dve.tensor_scalar(b[:, :], v[:, :], 0.0, None, ALU.max))
                dve.wait_ge(ax, 2)
                link(dve.tensor_tensor(b[:, :], b[:, :], a[:, :], ALU.add))
                link(dve.tensor_tensor(v[:, :], s_c[:, :], d_c[:, :], ALU.not_equal))
                link(dve.tensor_tensor(b[:, :], b[:, :], v[:, :], ALU.mult))
                link(dve.tensor_tensor(w_c[:, :], b[:, :], r[:, :, 2].bitcast(F32), ALU.mult))
                dve.sem_inc(pr, 1)

            @block.scalar
            def _(act):
                link = linker(act, "act")
                act.wait_ge(ax, 1)
                link(act.activation(a[:, :], a[:, :], ACT.Exp))
                link(act.activation(a[:, :], a[:, :], ACT.Ln, bias=1.0))
                act.sem_inc(ax, 1)

    @phase
    def masks(o, keys):
        ld, tr, bc = sem(f"mask_{o}_in"), sem(f"mask_{o}_T"), sem(f"mask_{o}_b")
        with ExitStack() as c, nc.Block() as block:
            k = [alloc(c, f"k{n}", [P, NT], I32) for n in range(3)]
            nx, col = alloc(c, "nx", [P, NT]), alloc(c, "col", [P, NT], I32)
            colf = alloc(c, "colf", [P, NT])
            rowb, rowf = alloc(c, "rowb", [P, 1], I32), alloc(c, "rowf", [P, 1])
            m = alloc(c, "m", [P, 1])
            ab = alloc(c, "ab", [P, F])
            pt = ps(c, "pt", [F, P])
            io = sem(f"mask_{o}_iota")

            @block.sync
            def _(sp):
                for n in range(3):
                    sp.dma_start(k[n][:, :], keys[n:n + EP].rearrange("(p t) -> p t", p=P)).then_inc(ld, 16)

            @block.gpsimd
            def _(pool):
                pool.iota(col[:, :], pattern=[[1, NT]], base=0, channel_multiplier=0).then_inc(io, 1)
                pool.iota(rowb[:, :], pattern=[[0, 1]], base=0, channel_multiplier=NT).then_inc(io, 1)

            @block.vector
            def _(dve):
                link = linker(dve, "dve")
                dve.wait_ge(ld, 48)
                dve.wait_ge(io, 2)
                kp = keep[o]
                link(dve.tensor_tensor(kp[:, :], k[1][:, :], k[0][:, :], ALU.is_equal))
                link(dve.tensor_tensor(nx[:, :], k[1][:, :], k[2][:, :], ALU.is_equal))
                link(dve.tensor_copy(fk[o][:, :], kp[:, 0:1]))
                link(dve.tensor_reduce(out=m[:, :], in_=kp[:, :], op=ALU.min, axis=AX.X))
                link(dve.memset(ab[:, :], 0.0))
                link(dve.tensor_scalar(ab[:, :], ab[:, :], m[:, 0:1], None, ALU.add))
                dve.sem_inc(bc, 1)
                link(dve.memset(kp[:, 0:1], 0.0))
                if o == "d":
                    link(dve.tensor_scalar(neg[:, :], nx[:, :], 1.0, BIG, ALU.subtract, ALU.mult))
                link(dve.tensor_copy(colf[:, :], col[:, :]))
                link(dve.tensor_scalar(nx[:, :], nx[:, :], NOROW, None, ALU.mult))
                link(dve.tensor_tensor(nx[:, :], nx[:, :], colf[:, :], ALU.add))
                link(dve.tensor_reduce(out=m[:, :], in_=nx[:, :], op=ALU.min, axis=AX.X))
                link(dve.tensor_copy(rowf[:, :], rowb[:, :]))
                link(dve.tensor_tensor(m[:, :], m[:, :], rowf[:, :], ALU.add))
                link(dve.tensor_copy(end0[o][:, :], m[:, :]))
                dve.wait_ge(tr, 1)
                link(dve.tensor_copy(aT[o][:, :], pt[:, :]))

            @block.tensor
            def _(pe):
                pe.wait_ge(bc, 1)
                pe.transpose(pt[:, :], ab[:, :], ident[:, :]).then_inc(tr, 1)

    def gathers(pool, table, idx, rows, idx_in, rows_in, free, go, w, n):
        def gather(i, b):
            if not isinstance(i, int) or i:
                free(pool, i, b)
            pool.wait_ge(idx_in[b], (i + 1) * 16)
            pool.sem_inc(go, 1)
            for j in range(w):
                pool.indirect_dma_start(rows[b][:, j, :], None, table,
                                        bass.IndirectOffsetOnAxis(ap=idx[b][:, j:j + 1], axis=0)).then_inc(rows_in[b], 16)
        pairs(pool, gather, n)

    def pairs(eng, step, n=NCH):
        step(0, 0)
        step(0, 1)
        with eng.Fori(1, n // 2) as i:
            step(i, 0)
            step(i, 1)

    DW = 16
    QUARTER = NT // 4
    dist_w = alloc(top, "dist_w", [F + 1, DW * F])
    dist_b2 = alloc(top, "dist_b2", [1, 4 * P])
    dist_v = {n: alloc(top, f"dist_{n}", [P, F]) for n in ("g1", "b1", "g2", "b2")}
    ones_row = alloc(top, "ones_row", [1, P])

    class Distances:

        def __init__(self, c, q):
            S = lambda n: sem(f"dist{q}_{n}")
            self.first = q * QUARTER
            self.a3_in, self.a3_T, self.a3_s, self.y1, self.y1_s = S("a3_in"), S("a3_T"), S("a3_s"), S("y1"), S("y1_s")
            self.sq, self.ln, self.ge, self.tr, self.ts, self.y2, self.y2_s = (S(n) for n in ("sq", "ln", "ge", "tr", "ts", "y2", "y2_s"))
            self.k, self.stored, self.var, self.sd = S("dve"), S("stored"), S("var"), S("sd")
            self.a3 = alloc(c, "a3", [P, P])
            self.a3T = alloc(c, "a3T", [F + 1, P])
            self.Y, self.SQ = alloc(c, "Y", [P, DW, F]), alloc(c, "SQ", [P, DW, F])
            self.yT = alloc(c, "yT", [P, 4, P])
            self.ss = alloc(c, "ss", [P, DW])
            self.pa, self.p1 = ps(c, "pa", [P, P]), ps(c, "p1", [P, DW, F])
            self.pt, self.p2 = ps(c, "pt", [P, 4, P]), ps(c, "p2", [P, 4, P])

        def start(self, dve):
            dve.memset(self.a3[:, :], 0.0).then_inc(self.k, 1)
            dve.memset(self.a3T[:, :], 1.0).then_inc(self.k, 1)

        def load(self, sp, i, b):
            ch = i * 2 + b
            if isinstance(ch, int) and ch == 0:
                sp.wait_ge(self.k, 2)
            else:
                sp.wait_ge(self.a3_T, ch)
            src = attr3_in.rearrange("(p t) f -> p (t f)", p=P)[:, bass.ds(ch * DW * 3 + self.first * 3, DW * 3)]
            sp.dma_start(self.a3[:, 0:DW * 3], src).then_inc(self.a3_in, 16)

        def store(self, sp, i, b):
            ch = i * 2 + b
            sp.wait_ge(self.ge, ch * 2 + 2)
            sp.dma_start(cols(dists, ch, DW, self.first), self.Y[:, :, :]).then_inc(self.stored, 16)

        def pe(self, pe, i, b):
            ch = i * 2 + b
            first = isinstance(ch, int) and ch == 0
            pe.wait_ge(self.a3_in, ch * 16 + 16)
            pe.transpose(self.pa[:, :], self.a3[:, :], ident[:, :]).then_inc(self.a3_T, 1)
            pe.wait_ge(self.a3_s, ch + 1)
            for h in range(2):
                t = pe.matmul(self.p1[:, 8 * h:8 * h + 8, :].rearrange("p a f -> p (a f)"), self.a3T[:, :],
                              dist_w[:, h * 512:(h + 1) * 512], start=True, stop=True)
            t.then_inc(self.y1, 1)
            pe.wait_ge(self.ge, ch * 2 + 1)
            for g in range(2):
                for h in range(4):
                    r = self.Y[:, 8 * g + 2 * h:8 * g + 2 * h + 2, :].rearrange("p a f -> p (a f)")
                    t = pe.transpose(self.pt[:, h, :], r, ident[:, :])
                t.then_inc(self.tr, 1)
                pe.wait_ge(self.ts, ch * 2 + g + 1)
                if g or not first:
                    pe.wait_ge(self.y2_s, ch * 2 + g)
                pe.matmul(self.p2[:, :, :].rearrange("p a f -> p (a f)"), ones_row[:, :], dist_b2[:, :], start=True, stop=False)
                for h in range(4):
                    t = pe.matmul(self.p2[:, h, :], self.yT[:, h, :], bd["d2"][:, :], start=False, stop=h == 3)
                t.then_inc(self.y2, 1)

        def act(self, act, i, b):
            ch = i * 2 + b
            act.wait_ge(self.a3_T, ch + 1)
            act.activation(self.a3T[0:F, :], self.pa[0:F, :], ACT.Copy).then_inc(self.a3_s, 1)
            act.wait_ge(self.y1, ch + 1)
            if not (isinstance(ch, int) and ch == 0):
                act.wait_ge(self.stored, ch * 16)
            flat_ = lambda t: t[:, :, :].rearrange("p a f -> p (a f)")
            act.activation(flat_(self.Y), flat_(self.p1), ACT.Copy).then_inc(self.y1_s, 1)
            act.wait_ge(self.y1_s, ch + 1)
            act.activation(self.SQ[:, :, :], self.Y[:, :, :], ACT.Square).then_inc(self.sq, 1)
            act.wait_ge(self.var, ch * 2 + 1)
            act.activation(self.ss[:, :], self.ss[:, :], ACT.Sqrt).then_inc(self.sd, 1)
            act.wait_ge(self.ln, ch * 2 + 1)
            act.activation(self.Y[:, :, :], self.Y[:, :, :], ACT.Gelu).then_inc(self.ge, 1)
            for g in range(2):
                act.wait_ge(self.tr, ch * 2 + g + 1)
                act.activation(self.yT[:, :, :], self.pt[:, :, :], ACT.Copy).then_inc(self.ts, 1)
                act.wait_ge(self.y2, ch * 2 + g + 1)
                act.activation(self.Y[:, 8 * g:8 * g + 8, :].rearrange("p a f -> p (a f)"),
                               self.p2[:, :, :].rearrange("p a f -> p (a f)"), ACT.Copy).then_inc(self.y2_s, 1)
            act.wait_ge(self.y2_s, ch * 2 + 2)
            act.activation(self.SQ[:, :, :], self.Y[:, :, :], ACT.Square).then_inc(self.sq, 1)
            act.wait_ge(self.var, ch * 2 + 2)
            act.activation(self.ss[:, :], self.ss[:, :], ACT.Sqrt).then_inc(self.sd, 1)
            act.wait_ge(self.ln, ch * 2 + 2)
            act.activation(self.Y[:, :, :], self.Y[:, :, :], ACT.Gelu).then_inc(self.ge, 1)

        def dve(self, dve, i, b, h):
            ch = i * 2 + b
            k = [ch * 12 + 6 * h + 2]

            def link(ins):
                ins.then_inc(self.k, 1)
                k[0] = k[0] + 1
                dve.wait_ge(self.k, k[0])
            Y, ss = self.Y, self.ss
            dve.wait_ge(self.sq, ch * 2 + h + 1)
            link(dve.reduce_sum(ss[:, :], self.SQ[:, :, :], axis=AX.X))
            link(dve.tensor_scalar(ss[:, :], ss[:, :], 1.0 / F, EPS, ALU.mult, ALU.add))
            dve.sem_inc(self.var, 1)
            dve.wait_ge(self.sd, ch * 2 + h + 1)
            link(dve.reciprocal(ss[:, :], ss[:, :]))
            link(dve.tensor_tensor(Y[:, :, :], Y[:, :, :], ss[:, :].unsqueeze(2).to_broadcast([P, DW, F]), ALU.mult))
            g, bb = dist_v[f"g{h + 1}"], dist_v[f"b{h + 1}"]
            link(dve.tensor_tensor(Y[:, :, :], Y[:, :, :], g[:, :].unsqueeze(1).to_broadcast([P, DW, F]), ALU.mult))
            link(dve.tensor_tensor(Y[:, :, :], Y[:, :, :], bb[:, :].unsqueeze(1).to_broadcast([P, DW, F]), ALU.add))
            dve.sem_inc(self.ln, 1)

    @phase
    def sum_pass(name, o, idx_arr, table, last, quarter):
        S = lambda n: [sem(f"{name}_{n}{b}") for b in range(2)]
        idx_in, rows_in, stored = S("idx"), S("rows"), S("stored")
        scanned, carried, go = sem(f"{name}_scanned"), sem(f"{name}_carried"), sem(f"{name}_go")
        with ExitStack() as c, nc.Block() as block:
            idx = [alloc(c, f"idx{b}", [P, T], I32) for b in range(2)]
            rows = [alloc(c, f"rows{b}", [P, T, F]) for b in range(2)]
            dist = Distances(c, quarter)

            @block.sync
            def _(sp):
                def load(i, b):
                    if not isinstance(i, int) or i:
                        sp.wait_ge(rows_in[b], i * 16 * T)
                    sp.dma_start(idx[b][:, :], cols(idx_arr, i * 2 + b)).then_inc(idx_in[b], 16)
                    dist.load(sp, i, b)

                def step(i, b):
                    load(i, b)
                    if not isinstance(i, int) or i or b:
                        bb, ii = (1, i - 1) if b == 0 else (0, i)
                        store(ii, bb)

                def store(i, b):
                    sp.wait_ge(scanned, (i * 2 + b + 1) * F)
                    sp.dma_start(cols(sums[0:EP, :], i * 2 + b), rows[b][:, :, :]).then_inc(stored[b], 16)
                    dist.store(sp, i, b)
                pairs(sp, step)
                store(NCH // 2 - 1, 1)
                for b in range(2):
                    sp.wait_ge(stored[b], NCH // 2 * 16)
                sp.wait_ge(dist.stored, NCH * 16)

            @block.gpsimd
            def _(pool):
                gathers(pool, table, idx, rows, idx_in, rows_in, lambda e, i, b: e.wait_ge(stored[b], i * 16), go, T, NCH)

            @block.tensor
            def _(pe):
                pairs(pe, lambda i, b: dist.pe(pe, i, b))

            @block.scalar
            def _(act):
                pairs(act, lambda i, b: dist.act(act, i, b))

            @block.vector
            def _(dve):
                dist.start(dve)
                dve.memset(last[:, :], 0.0).then_inc(carried, 1)

                def scan(i, b):
                    ch = i * 2 + b
                    dist.dve(dve, i, b, 0)
                    dve.wait_ge(rows_in[b], (i + 1) * 16 * T)
                    dve.wait_ge(carried, ch + 1)
                    k = keep[o][:, bass.ds(ch * T, T)]
                    for f in range(F):
                        dve.tensor_tensor_scan(rows[b][:, :, f], k, rows[b][:, :, f], last[:, f:f + 1],
                                               ALU.mult, ALU.add).then_inc(scanned, 1)
                    dve.wait_ge(scanned, (ch + 1) * F)
                    dve.tensor_copy(last[:, :], rows[b][:, T - 1, :]).then_inc(carried, 1)
                    dist.dve(dve, i, b, 1)
                pairs(dve, scan)

    TS = 52

    @phase
    def softmax_pass(name, idx_arr, table, last, lastmax):
        NC = NT // TS
        one = name == "L1"
        W_ = F if one else 2 * F
        S = lambda n: [sem(f"{name}_{n}{b}") for b in range(2)]
        q = lambda n: sem(f"{name}_{n}")
        idx_in, rows_in = S("idx"), S("rows")
        go, side_in, maxed, dk, faded, valued, summed, carried, mstored, sstored = (q(n) for n in (
            "go", "side_in", "maxed", "steps", "faded", "valued", "summed", "carried", "mstored", "sstored"))
        hs, ml, ml2, cp = q("hscan"), q("logit"), q("weighted"), q("copy")
        tr, ts, lg, ls, t1 = q("tr"), q("ts"), q("lg"), q("ls"), q("act")
        GR = [(4 * g, min(4, TS // 2 - 4 * g)) for g in range(-(-TS // 8))]
        NGR = len(GR)
        with ExitStack() as c, nc.Block() as block:
            idx = [alloc(c, f"idx{b}", [P, TS], I32) for b in range(2)]
            rows = [alloc(c, f"rows{b}", [P, TS, W_]) for b in range(2)]
            side = alloc(c, "side", [P, TS, F])
            L1b = alloc(c, "logits", [P, TS, F]) if one else None
            Hh = alloc(c, "H", [P, TS + 1, F])
            XB, PB = alloc(c, "XB", [P, TS, F]), alloc(c, "PB", [P, TS, F])
            DN = alloc(c, "DN", [P, TS, 2 * F])
            if one:
                aT_ = [alloc(c, f"attrT{n}", [P, 4, P]) for n in range(2)]
                pt = [ps(c, f"pt{n}", [P, 4, P]) for n in range(2)]
                pl = [ps(c, f"pl{n}", [P, 4, P]) for n in range(2)]

            def lg_of(b):
                return L1b[:, :, :] if one else rows[b][:, :, 0:F]

            def val_of(b):
                return rows[b][:, :, :] if one else rows[b][:, :, F:2 * F]

            @block.sync
            def _(sp):
                def step(i, b):
                    ch = i * 2 + b
                    if not isinstance(i, int) or i:
                        sp.wait_ge(rows_in[b], i * 16 * TS)
                    sp.dma_start(idx[b][:, :], cols(idx_arr, ch, TS)).then_inc(idx_in[b], 16)
                    if not isinstance(i, int) or i or b:
                        if one:
                            sp.wait_ge(tr, ch * NGR)
                        else:
                            sp.wait_ge(valued, ch)
                    sp.dma_start(side[:, :, :], cols(attr64_in if one else dists, ch, TS)).then_inc(side_in, 16)
                    if not isinstance(i, int) or i or b:
                        store(ch - 1)

                def store(ch):
                    sp.wait_ge(maxed, ch + 1)
                    sp.dma_start(cols(maxes, ch, TS), Hh[:, 0:TS, :]).then_inc(mstored, 16)
                    sp.wait_ge(summed, (ch + 1) * 2 * F)
                    sp.dma_start(cols(sums2[0:EP, :], ch, TS), DN[:, :, :]).then_inc(sstored, 16)
                pairs(sp, step, NC)
                store(NC - 1)
                sp.wait_ge(mstored, NC * 16)
                sp.wait_ge(sstored, NC * 16)

            @block.gpsimd
            def _(pool):
                gathers(pool, table, idx, rows, idx_in, rows_in,
                        lambda e, i, b: e.wait_ge(summed, (i * 2 + b - 1) * 2 * F), go, TS, NC)

            @block.tensor
            def _(pe):
                def step(i, b):
                    ch = i * 2 + b
                    pe.wait_ge(side_in, ch * 16 + 16)
                    for g, (h0, n) in enumerate(GR):
                        z = (b * NGR + g) % 2
                        first = (isinstance(i, int) and i == 0) and b * NGR + g < 2
                        if not first:
                            pe.wait_ge(ts, ch * NGR + g - 1)
                        for h in range(n):
                            r = side[:, 2 * (h0 + h):2 * (h0 + h) + 2, :].rearrange("p a f -> p (a f)")
                            t = pe.transpose(pt[z][:, h, :], r, ident[:, :])
                        t.then_inc(tr, 1)
                        pe.wait_ge(ts, ch * NGR + g + 1)
                        if not first:
                            pe.wait_ge(ls, ch * NGR + g - 1)
                        for h in range(n):
                            t = pe.matmul(pl[z][:, h, :], aT_[z][:, h, :], bd["fcr"][:, :], start=True, stop=True)
                        t.then_inc(lg, 1)
                if one:
                    pairs(pe, step, NC)

            @block.scalar
            def _(act):
                def logits(i, b):
                    ch = i * 2 + b
                    for g, (h0, n) in enumerate(GR):
                        z = (b * NGR + g) % 2
                        act.wait_ge(tr, ch * NGR + g + 1)
                        if not ((isinstance(i, int) and i == 0) and b * NGR + g < 2):
                            act.wait_ge(lg, ch * NGR + g - 1)
                        act.activation(aT_[z][:, 0:n, :], pt[z][:, 0:n, :], ACT.Copy).then_inc(ts, 1)
                        act.wait_ge(lg, ch * NGR + g + 1)
                        if g == 0 and not (isinstance(i, int) and i == 0 and b == 0):
                            act.wait_ge(valued, ch)
                        act.activation(L1b[:, 2 * h0:2 * (h0 + n), :].rearrange("p a f -> p (a f)"),
                                       pl[z][:, 0:n, :].rearrange("p a f -> p (a f)"), ACT.Copy).then_inc(ls, 1)

                def fades(i, b):
                    ch = i * 2 + b
                    act.wait_ge(dk, ch + 1)
                    if not (isinstance(i, int) and i == 0 and b == 0):
                        act.wait_ge(summed, ch * 2 * F)
                    act.activation(PB[:, :, :], XB[:, :, :], ACT.Relu, scale=-1.0).then_inc(t1, 1)
                    act.wait_ge(t1, ch * 2 + 1)
                    act.activation(XB[:, :, :], XB[:, :, :], ACT.Relu).then_inc(t1, 1)
                    act.activation(PB[:, :, :], PB[:, :, :], ACT.Exp, scale=-1.0).then_inc(faded, 1)
                    act.wait_ge(t1, ch * 2 + 2)
                    act.activation(XB[:, :, :], XB[:, :, :], ACT.Exp, scale=-1.0).then_inc(faded, 1)
                if one:
                    logits(0, 0)
                    fades(0, 0)
                    logits(0, 1)
                    fades(0, 1)
                    with act.Fori(1, NC // 2) as i:
                        logits(i, 0)
                        fades(i, 0)
                        logits(i, 1)
                        fades(i, 1)
                else:
                    pairs(act, fades, NC)

            @block.vector
            def _(dve):
                dve.memset(last[:, :], 0.0).then_inc(carried, 1)
                dve.memset(Hh[:, TS, :], -BIG).then_inc(cp, 1)

                def step(i, b):
                    ch = i * 2 + b
                    first = isinstance(i, int) and i == 0 and b == 0
                    l, v = lg_of(b), val_of(b)
                    dve.wait_ge(cp, ch * 2 + 1)
                    if not first:
                        dve.wait_ge(mstored, ch * 16)
                    dve.tensor_copy(Hh[:, 0, :], Hh[:, TS, :]).then_inc(cp, 1)
                    if one:
                        dve.wait_ge(ls, (ch + 1) * NGR)
                    else:
                        dve.wait_ge(side_in, ch * 16 + 16)
                        dve.wait_ge(rows_in[b], (i + 1) * 16 * TS)
                        dve.tensor_tensor(l, side[:, :, :], l, ALU.subtract).then_inc(ml, 1)
                        dve.wait_ge(ml, ch + 1)
                    dve.wait_ge(cp, ch * 2 + 2)
                    k = neg[:, bass.ds(ch * TS, TS)]
                    for f in range(F):
                        dve.tensor_tensor_scan(Hh[:, 1:TS + 1, f], l[:, :, f], k, Hh[:, 0, f:f + 1],
                                               ALU.max, ALU.add).then_inc(hs, 1)
                    dve.wait_ge(hs, (ch + 1) * F)
                    if not first:
                        dve.wait_ge(summed, ch * 2 * F)
                    dve.tensor_tensor(XB[:, :, :], l, Hh[:, 0:TS, :], ALU.subtract).then_inc(dk, 1)
                    dve.wait_ge(dk, ch + 1)
                    dve.tensor_tensor(Hh[:, 0:TS, :], Hh[:, 0:TS, :], l, ALU.max).then_inc(maxed, 1)
                    if one:
                        dve.wait_ge(rows_in[b], (i + 1) * 16 * TS)
                        dve.tensor_tensor(v, v, l, ALU.add).then_inc(valued, 1)
                    else:
                        dve.tensor_tensor(v, v, side[:, :, :], ALU.add).then_inc(valued, 1)
                    dve.wait_ge(valued, ch + 1)
                    dve.wait_ge(maxed, ch + 1)
                    dve.tensor_copy(lastmax[:, :], Hh[:, TS - 1, :]).then_inc(cp, 1)
                    dve.wait_ge(faded, ch * 2 + 2)
                    dve.tensor_tensor(v, v, PB[:, :, :], ALU.mult).then_inc(ml2, 1)
                    dve.wait_ge(ml2, ch + 1)
                    dve.wait_ge(carried, ch + 1)
                    if not first:
                        dve.wait_ge(sstored, ch * 16)
                    for s_, a in enumerate((PB[:, :, :], v)):
                        for f in range(F):
                            dve.tensor_tensor_scan(DN[:, :, s_ * F + f], XB[:, :, f], a[:, :, f],
                                                   last[:, s_ * F + f:s_ * F + f + 1], ALU.mult, ALU.add).then_inc(summed, 1)
                    dve.wait_ge(summed, (ch + 1) * 2 * F)
                    dve.tensor_copy(last[:, :], DN[:, TS - 1, :]).then_inc(carried, 1)
                pairs(dve, step, NC)

    @phase
    def fix_and_fetch(name, o, src, last, lastmax, node_rows):
        W_ = 2 * F if lastmax is not None else F
        soft = lastmax is not None
        tr, tb, up, fx = sem(f"{name}_T"), sem(f"{name}_carryT"), sem(f"{name}_carry"), sem(f"{name}_first")
        f_in, f_out, n_in = sem(f"{name}_first_in"), sem(f"{name}_first_out"), sem(f"{name}_nodes")
        ex = sem(f"{name}_exps")
        nk = 3 if soft else 1
        with ExitStack() as c, nc.Block() as block:
            pT = [ps(c, f"pT{n}", [F, P]) for n in range(nk)]
            pB = [ps(c, f"pB{n}", [P, F]) for n in range(nk)]
            lT = [alloc(c, f"lT{n}", [F, P]) for n in range(nk)]
            cT = [alloc(c, f"cT{n}", [F, P + 1]) for n in range(nk)]
            nT, dT, eT = (alloc(c, f"xT{n}", [F, P]) for n in range(3))
            cin = alloc(c, "cin", [P, nk * F])
            row, mrow = alloc(c, "row", [P, W_]), alloc(c, "mrow", [P, F])
            M, e1, e2 = (alloc(c, f"e{n}", [P, F]) for n in range(3))
            parts = [lastmax[:, :], last[:, 0:F], last[:, F:2 * F]] if soft else [last[:, :]]

            @block.tensor
            def _(pe):
                for n, part in enumerate(parts):
                    t = pe.transpose(pT[n][:, :], part, ident[:, :])
                t.then_inc(tr, 1)
                pe.wait_ge(tb, 1)
                for n in range(nk):
                    t = pe.transpose(pB[n][:, :], cT[n][:, 0:P], ident[0:F, 0:F])
                t.then_inc(up, 1)

            @block.scalar
            def _(act):
                if soft:
                    link = linker(act, "act")
                    for k in (1, 3):
                        act.wait_ge(ex, k)
                        a, b_ = (dT, eT) if k == 1 else (e1, e2)
                        link(act.activation(a[:, :], a[:, :], ACT.Exp))
                        link(act.activation(b_[:, :], b_[:, :], ACT.Exp))
                        act.sem_inc(ex, 1)

            @block.vector
            def _(dve):
                link = linker(dve, "dve")
                dve.wait_ge(tr, 1)
                for n in range(nk):
                    link(dve.tensor_copy(lT[n][:, :], pT[n][:, :]))
                    link(dve.memset(cT[n][:, :], -BIG if soft and n == 0 else 0.0))
                if soft:
                    link(dve.tensor_scalar(nT[:, :], aT[o][:, :], 1.0, BIG, ALU.subtract, ALU.mult))
                    link(dve.tensor_tensor_scan(cT[0][:, 1:P + 1], nT[:, :], lT[0][:, :], -BIG, ALU.add, ALU.max))
                    link(dve.tensor_tensor(dT[:, :], cT[0][:, 0:P], cT[0][:, 1:P + 1], ALU.subtract))
                    link(dve.tensor_scalar(dT[:, :], dT[:, :], 0.0, None, ALU.min))
                    link(dve.tensor_tensor(eT[:, :], lT[0][:, :], cT[0][:, 1:P + 1], ALU.subtract))
                    dve.sem_inc(ex, 1)
                    dve.wait_ge(ex, 2)
                    link(dve.tensor_tensor(dT[:, :], dT[:, :], aT[o][:, :], ALU.mult))
                    for n in (1, 2):
                        link(dve.tensor_tensor(lT[n][:, :], lT[n][:, :], eT[:, :], ALU.mult))
                        link(dve.tensor_tensor_scan(cT[n][:, 1:P + 1], dT[:, :], lT[n][:, :], 0.0, ALU.mult, ALU.add))
                else:
                    link(dve.tensor_tensor_scan(cT[0][:, 1:P + 1], aT[o][:, :], lT[0][:, :], 0.0, ALU.mult, ALU.add))
                dve.sem_inc(tb, 1)
                dve.wait_ge(up, 1)
                for n in range(nk):
                    link(dve.tensor_copy(cin[:, n * F:(n + 1) * F], pB[n][:, :]))
                dve.wait_ge(f_in, (2 if soft else 1) * 16)
                if soft:
                    link(dve.tensor_scalar(cin[:, 0:3 * F], cin[:, 0:3 * F], fk[o][:, 0:1], None, ALU.mult))
                    link(dve.tensor_scalar(M[:, 0:1], fk[o][:, 0:1], 1.0, BIG, ALU.subtract, ALU.mult))
                    link(dve.tensor_scalar(e1[:, :], cin[:, 0:F], M[:, 0:1], None, ALU.add))
                    link(dve.tensor_tensor(M[:, :], e1[:, :], mrow[:, :], ALU.max))
                    link(dve.tensor_tensor(e1[:, :], e1[:, :], M[:, :], ALU.subtract))
                    link(dve.tensor_tensor(e2[:, :], mrow[:, :], M[:, :], ALU.subtract))
                    dve.sem_inc(ex, 1)
                    dve.wait_ge(ex, 4)
                    for n in range(2):
                        a, b_ = row[:, n * F:(n + 1) * F], cin[:, (n + 1) * F:(n + 2) * F]
                        link(dve.tensor_tensor(a, a, e2[:, :], ALU.mult))
                        link(dve.tensor_tensor(b_, b_, e1[:, :], ALU.mult))
                        link(dve.tensor_tensor(a, a, b_, ALU.add))
                else:
                    link(dve.scalar_tensor_tensor(row[:, :], cin[:, :], fk[o][:, 0:1], row[:, :], ALU.mult, ALU.add))
                dve.sem_inc(fx, 1)

            @block.gpsimd
            def _(pool):
                link = linker(pool, "pool")
                link(pool.memset(row[:, :], 0.0))
                link(pool.memset(mrow[:, :], 0.0))
                off = lambda: bass.IndirectOffsetOnAxis(ap=end0[o][:, 0:1], axis=0)
                pool.indirect_dma_start(row[:, :], None, src[0:EP, :], off(), bounds_check=EP - 1, oob_is_err=False).then_inc(f_in, 16)
                if soft:
                    pool.indirect_dma_start(mrow[:, :], None, maxes, off(), bounds_check=EP - 1, oob_is_err=False).then_inc(f_in, 16)
                pool.wait_ge(fx, 1)
                pool.indirect_dma_start(src[0:EP, :], off(), row[:, :], None, bounds_check=EP - 1, oob_is_err=False).then_inc(f_out, 16)
                pool.wait_ge(f_out, 16)
                for j in range(NJ):
                    pool.indirect_dma_start(node_rows[:, j, 0:W_], None, src,
                                            bass.IndirectOffsetOnAxis(ap=endp[o][:, j:j + 1], axis=0)).then_inc(n_in, 16)
                pool.wait_ge(n_in, 16 * NJ)

    pj = [Counter(lasting(n)) for n in ("proj_in", "proj_T", "proj_lhs", "proj_out", "proj_stored")]

    def project(src, weight, dst):
        s_in, s_T, s_l, s_o, s_d = pj
        B = [s.base for s in pj]
        with ExitStack() as c, nc.Block() as block:
            xin, xT = alloc(c, "xin", [P, G, F]), alloc(c, "xT", [P, G // 2, P])
            pT, pO = ps(c, "pTp", [P, 8, P]), ps(c, "pOp", [P, 8, P])
            H = G // 2

            @block.vector
            def _(dve):
                with dve.Fori(0, NG) as i:
                    dve.wait_ge(s_o.sem, i + B[3])
                    dve.tensor_copy(xin[:, :, :], src[:, bass.ds(i * G, G), :]).then_inc(s_in.sem, 1)
                    dve.wait_ge(s_o.sem, i + B[3] + 1)
                    dve.tensor_copy(dst[:, bass.ds(i * G, G), :],
                                    pO[:, 0:H, :].rearrange("p h (a f) -> p (h a) f", f=F)).then_inc(s_d.sem, 1)

            @block.tensor
            def _(pe):
                with pe.Fori(0, NG) as i:
                    pe.wait_ge(s_in.sem, i + B[0] + 1)
                    for h in range(H):
                        t = pe.transpose(pT[:, h, :], xin[:, 2 * h:2 * h + 2, :].rearrange("p a f -> p (a f)"), ident[:, :])
                    t.then_inc(s_T.sem, 1)
                    pe.wait_ge(s_l.sem, i + B[2] + 1)
                    pe.wait_ge(s_d.sem, i + B[4])
                    for h in range(H):
                        t = pe.matmul(pO[:, h, :], xT[:, h, :], weight[:, :], start=True, stop=True)
                    t.then_inc(s_o.sem, 1)

            @block.scalar
            def _(act):
                with act.Fori(0, NG) as i:
                    act.wait_ge(s_T.sem, i + B[1] + 1)
                    act.activation(xT[:, :, :], pT[:, 0:H, :], ACT.Copy).then_inc(s_l.sem, 1)
        for s in pj:
            s.base += NG

    def bias_tile(c, n, vec):
        t = alloc(c, f"bias_{n}", [P, F])
        return t, vec.rearrange("(a n) -> a n", a=1).to_broadcast([P, F])

    def bc(t):
        return t[:, :].unsqueeze(1).to_broadcast([P, NJ, F])

    def pc(t):
        return t.unsqueeze(2).to_broadcast([P, NJ, F])

    nd = {n: lasting(n) for n in ("vec_in", "table_out")}
    ndb = {"vec_in": 0, "table_out": 0}

    def nodes(dve_work, vectors=(), tables=(), act_work=None):
        done = Counter_done
        with ExitStack() as c, nc.Block() as block:
            vt = [alloc(c, f"vec{n}", [P, F]) for n in range(len(vectors))]
            tmp = alloc(c, "tmp_n", [P, NJ, F])
            small = [alloc(c, f"small{n}", [P, NJ]) for n in range(3)]
            b_in, b_out, b_done = ndb["vec_in"], ndb["table_out"], done.base

            @block.sync
            def _(sp):
                for t, v in zip(vt, vectors):
                    sp.dma_start(t[:, :], v.rearrange("(a n) -> a n", a=1).to_broadcast([P, F])).then_inc(nd["vec_in"], 16)
                if tables:
                    sp.wait_ge(done.sem, b_done + 1)
                    for dst, s in tables:
                        sp.dma_start(dst.rearrange("(p j) f -> p j f", p=P), s).then_inc(nd["table_out"], 16)
                    sp.wait_ge(nd["table_out"], b_out + 16 * len(tables))

            @block.vector
            def _(dve):
                if vectors:
                    dve.wait_ge(nd["vec_in"], b_in + 16 * len(vectors))
                dve_work(dve, linker(dve, "dve"), vt, tmp, small)
                dve.sem_inc(done.sem, 1)

            @block.scalar
            def _(act):
                for t in pending:
                    act.wait_ge(root_in.sem, root_in.base)
                    act.activation(t[:, :], t[:, :], ACT.Sqrt).then_inc(root_out.sem, 1)
                pending.clear()
            ndb["vec_in"] += 16 * len(vectors)
            ndb["table_out"] += 16 * len(tables)
            done.base += 1
    root_in, root_out = Counter(lasting("root_in")), Counter(lasting("root_out"))

    def roots(dve, t):
        root_in.base += 1
        root_out.base += 1
        pending.append(t)
        dve.sem_inc(root_in.sem, 1)
        dve.wait_ge(root_out.sem, root_out.base)
    pending = []

    Counter_done = Counter(lasting("nodes_done"))

    def layernorm(dve, link, x, tmp, small):
        mean, var = small[0], small[1]
        link(dve.reduce_sum(mean[:, :], x[:, :, :], axis=AX.X))
        link(dve.tensor_scalar(mean[:, :], mean[:, :], 1.0 / F, None, ALU.mult))
        link(dve.tensor_tensor(x[:, :, :], x[:, :, :], pc(mean[:, :]), ALU.subtract))
        link(dve.tensor_tensor(tmp[:, :, :], x[:, :, :], x[:, :, :], ALU.mult))
        link(dve.reduce_sum(var[:, :], tmp[:, :, :], axis=AX.X))
        link(dve.tensor_scalar(var[:, :], var[:, :], 1.0 / F, EPS, ALU.mult, ALU.add))
        roots(dve, var)
        link(dve.reciprocal(var[:, :], var[:, :]))
        link(dve.tensor_tensor(x[:, :, :], x[:, :, :], pc(var[:, :]), ALU.mult))

    @phase
    def similarity_pass(last):
        W_ = F + 1
        S = lambda n: [sem(f"L2_{n}{b}") for b in range(2)]
        q = lambda n: sem(f"L2_{n}")
        idx_in, rows_in, side_in = S("idx"), S("rows"), S("side")
        go, filled, prod, steps, msg, scanned, carried, stored = (q(n) for n in (
            "go", "filled", "prod", "steps", "msg", "scanned", "carried", "stored"))
        with ExitStack() as c, nc.Block() as block:
            idx = [alloc(c, f"idx{b}", [P, T], I32) for b in range(2)]
            rows = [alloc(c, f"rows{b}", [P, T, W_]) for b in range(2)]
            own = [alloc(c, f"own{b}", [P, T, W_]) for b in range(2)]
            base = [alloc(c, f"base{b}", [P, T]) for b in range(2)]
            tmp = alloc(c, "tmp", [P, T, F])
            lastu = alloc(c, "lastu", [P, W_])
            dot, nn, a, b2 = (alloc(c, f"s{n}", [P, T]) for n in range(4))

            @block.sync
            def _(sp):
                def step(i, b):
                    ch = i * 2 + b
                    if not isinstance(i, int) or i:
                        sp.wait_ge(rows_in[b], i * 16 * T)
                        sp.wait_ge(msg, ch - 1)
                    sp.dma_start(idx[b][:, :], cols(sdst, ch)).then_inc(idx_in[b], 16)
                    sp.dma_start(own[b][:, :, :], cols(spread, ch)).then_inc(side_in[b], 16)
                    sp.dma_start(base[b][:, :], cols(sbase, ch)).then_inc(side_in[b], 16)
                    if not isinstance(i, int) or i or b:
                        store(ch - 1)

                def store(ch):
                    sp.wait_ge(scanned, (ch + 1) * F)
                    sp.dma_start(cols(sums[0:EP, :], ch), tmp[:, :, :]).then_inc(stored, 16)
                pairs(sp, step)
                store(NCH - 1)
                sp.wait_ge(stored, NCH * 16)

            @block.gpsimd
            def _(pool):
                gathers(pool, tab65, idx, rows, idx_in, rows_in, lambda e, i, b: e.wait_ge(msg, i * 2 + b - 1), go, T, NCH)

            @block.vector
            def _(dve):
                dve.memset(last[:, :], 0.0).then_inc(carried, 1)
                dve.memset(lastu[:, :], 0.0).then_inc(carried, 1)
                NS = 10

                def step(i, b):
                    ch = i * 2 + b
                    first = isinstance(i, int) and i == 0 and b == 0
                    k = keep["s"][:, bass.ds(ch * T, T)]
                    dve.wait_ge(side_in[b], (i + 1) * 32)
                    dve.wait_ge(carried, ch * 2 + 2)
                    u, g = own[b], rows[b]
                    for f in range(W_):
                        dve.tensor_tensor_scan(u[:, :, f], k, u[:, :, f], lastu[:, f:f + 1], ALU.mult, ALU.add).then_inc(filled, 1)
                    dve.wait_ge(filled, (ch + 1) * W_)
                    dve.tensor_copy(lastu[:, :], u[:, T - 1, :]).then_inc(carried, 1)
                    dve.wait_ge(rows_in[b], (i + 1) * 16 * T)
                    if not first:
                        dve.wait_ge(stored, ch * 16)
                    n = [0]

                    def link(ins):
                        n[0] += 1
                        ins.then_inc(steps, 1)
                        dve.wait_ge(steps, ch * NS + n[0])
                    link(dve.tensor_tensor(tmp[:, :, :], u[:, :, 0:F], g[:, :, 0:F], ALU.mult))
                    link(dve.reduce_sum(dot[:, :], tmp[:, :, :], axis=AX.X))
                    link(dve.tensor_tensor(nn[:, :], u[:, :, F], g[:, :, F], ALU.mult))
                    link(dve.tensor_scalar(nn[:, :], nn[:, :], 1e-8, None, ALU.max))
                    link(dve.reciprocal(a[:, :], nn[:, :]))
                    link(dve.tensor_tensor(dot[:, :], dot[:, :], a[:, :], ALU.mult))
                    link(dve.tensor_scalar(a[:, :], dot[:, :], 0.0, co[:, 4:5], ALU.max, ALU.mult))
                    link(dve.tensor_scalar(b2[:, :], dot[:, :], 0.0, co[:, 5:6], ALU.min, ALU.mult))
                    link(dve.tensor_tensor(a[:, :], a[:, :], b2[:, :], ALU.add))
                    link(dve.tensor_tensor(a[:, :], a[:, :], base[b][:, :], ALU.mult))
                    dve.tensor_tensor(tmp[:, :, :], g[:, :, 0:F], a[:, :].unsqueeze(2).to_broadcast([P, T, F]), ALU.mult).then_inc(msg, 1)
                    dve.wait_ge(msg, ch + 1)
                    for f in range(F):
                        dve.tensor_tensor_scan(tmp[:, :, f], k, tmp[:, :, f], last[:, f:f + 1], ALU.mult, ALU.add).then_inc(scanned, 1)
                    dve.wait_ge(scanned, (ch + 1) * F)
                    dve.tensor_copy(last[:, :], tmp[:, T - 1, :]).then_inc(carried, 1)
                pairs(dve, step)

    @phase
    def spread_rows(wh):
        sc, kin, fin, fst = sem("spread_nodes"), sem("spread_key"), sem("spread_first_in"), sem("spread_first")
        with ExitStack() as c, nc.Block() as block:
            key0 = alloc(c, "key0", [P, 2], I32)
            row = alloc(c, "row0", [P, F + 1])

            @block.sync
            def _(sp):
                sp.dma_start(key0[:, :], skey[1:EP + 1].rearrange("(p t) -> p t", p=P)[:, 0:2]).then_inc(kin, 16)
                sp.wait_ge(fin, 16)
                sp.wait_ge(sc, 16 * NJ)
                sp.dma_start(spread.rearrange("(p t) f -> p t f", p=P)[:, 0, :], row[:, :]).then_inc(fst, 16)
                sp.wait_ge(fst, 16)

            @block.gpsimd
            def _(pool):
                pool.wait_ge(kin, 16)
                pool.indirect_dma_start(row[:, :], None, tab65, bass.IndirectOffsetOnAxis(ap=key0[:, 0:1], axis=0)).then_inc(fin, 16)
                for j in range(NJ):
                    pool.indirect_dma_start(spread, bass.IndirectOffsetOnAxis(ap=startp[:, j:j + 1], axis=0),
                                            wh[:, j, :], None, bounds_check=EP - 1, oob_is_err=False).then_inc(sc, 16)
                pool.wait_ge(sc, 16 * NJ)

    @phase
    def zero_scratch():
        z, zd = sem("zeros"), sem("zeroed")
        with ExitStack() as c, nc.Block() as block:
            zt = alloc(c, "zt", [P, 2 * T, F + 1])

            @block.vector
            def _(dve):
                dve.memset(zt[:, :, :], 0.0).then_inc(z, 1)

            @block.sync
            def _(sp):
                sp.wait_ge(z, 1)
                with sp.Fori(0, NCH // 2) as i:
                    sp.dma_start(cols(spread, i, 2 * T), zt[:, :, :]).then_inc(zd, 16)
                sp.dma_start(sums[EP:ROWS, :], zt[0:1, 0, 0:F]).then_inc(zd, 16)
                sp.dma_start(sums2[EP:ROWS, :], zt[0:1, 0:2, 0:F]).then_inc(zd, 16)
                sp.wait_ge(zd, 16 * (NCH // 2 + 2))

    @phase
    def distance_weights():
        ld, ce, st, rd = sem("dw_loaded"), sem("dw_centred"), sem("dw_stored"), sem("dw_back")
        centred = dram("centred", [5, F])
        with ExitStack() as c, nc.Block() as block:
            w = alloc(c, "w5", [5, F])
            m = alloc(c, "m5", [5, 1])
            zs = sem("dw_zeroed")

            @block.sync
            def _(sp):
                sp.dma_start(w[0:3, :], W["L3_gnn_Wd1"]).then_inc(ld, 16)
                sp.dma_start(w[3:4, :], W["L3_gnn_bd1"].rearrange("(a n) -> a n", a=1)).then_inc(ld, 16)
                sp.dma_start(w[4:5, :], W["L3_gnn_bd2"].rearrange("(a n) -> a n", a=1)).then_inc(ld, 16)
                for n in ("g1", "b1", "g2", "b2"):
                    sp.dma_start(dist_v[n][:, :], W[f"L3_gnn_{n}"].rearrange("(a n) -> a n", a=1).to_broadcast([P, F])).then_inc(ld, 16)
                sp.wait_ge(ce, 1)
                sp.dma_start(centred, w[:, :]).then_inc(st, 16)
                sp.wait_ge(st, 16)
                sp.wait_ge(zs, 2)
                for t in range(DW):
                    sp.dma_start(dist_w[3 * t:3 * t + 3, t * F:(t + 1) * F], centred[0:3, :]).then_inc(rd, 16)
                    sp.dma_start(dist_w[F:F + 1, t * F:(t + 1) * F], centred[3:4, :]).then_inc(rd, 16)
                for t in range(8):
                    sp.dma_start(dist_b2[:, t * F:(t + 1) * F], centred[4:5, :]).then_inc(rd, 16)
                sp.wait_ge(rd, 16 * (2 * DW + 8))

            @block.vector
            def _(dve):
                link = linker(dve, "dve")
                dve.memset(dist_w[:, :], 0.0).then_inc(zs, 1)
                dve.memset(ones_row[:, :], 1.0).then_inc(zs, 1)
                dve.sem_inc(pj[3].sem, 1)
                dve.sem_inc(pj[4].sem, 1)
                pj[3].base = pj[4].base = 1
                dve.wait_ge(ld, 16 * 7)
                link(dve.reduce_sum(m[:, :], w[:, :], axis=AX.X))
                link(dve.tensor_scalar(m[:, :], m[:, :], 1.0 / F, None, ALU.mult))
                link(dve.tensor_scalar(w[:, :], w[:, :], m[:, 0:1], None, ALU.subtract))
                dve.sem_inc(ce, 1)

    constants()
    distance_weights()
    with ExitStack() as srt:
        bases = [alloc(srt, f"digit_base{n}", [P, P]) for n in range(2)]
        counts(bases)
        sort_pass(0, bases[0])
        sort_pass(1, bases[1])
    zero_scratch()
    unpack_sorted()
    masks("d", dst_in)
    masks("s", skey)

    dst_keys = dst_in[1:EP + 1]
    with ExitStack() as c:
        A = alloc(c, "A", [P, NJ, F])
        project(X, bd["a1"], A)
        nodes(lambda dve, link, v, tmp, small: None, tables=[(tab, A[:, :, :])])
    quarter = 0
    for conv, (bias, nxt) in enumerate((("L0_gnn_b1", "a2"), ("L0_gnn_b2", None))):
        for o, keys in (("d", src_in), ("s", sdst)):
            with ExitStack() as c:
                last = alloc(c, "last", [P, F])
                sum_pass(f"conv{conv}{o}", o, keys, tab, last, quarter)
                quarter += 1
                R = alloc(c, "node_rows", [P, NJ, F])
                fix_and_fetch(f"conv{conv}{o}", o, sums, last, None, R)
                if o == "d":
                    nodes(lambda dve, link, v, tmp, small:
                          link(dve.tensor_tensor(R[:, :, :], R[:, :, :], pc(inv["d"][:, :]), ALU.mult)), tables=[(tab, R[:, :, :])])
                    continue

                def finish(dve, link, v, tmp, small):
                    link(dve.tensor_tensor(R[:, :, :], R[:, :, :], pc(inv["s"][:, :]), ALU.mult))
                    link(dve.tensor_tensor(R[:, :, :], R[:, :, :], bc(v[0]), ALU.add))
                    if conv == 0:
                        link(dve.tensor_scalar(R[:, :, :], R[:, :, :], 0.0, None, ALU.max))
                    else:
                        link(dve.tensor_tensor(X[:, :, :], X[:, :, :], R[:, :, :], ALU.add))
                        layernorm(dve, link, X, tmp, small)
                nodes(finish, vectors=[W[bias]])
                if nxt:
                    A = alloc(c, "A", [P, NJ, F])
                    project(R, bd[nxt], A)
                    nodes(lambda dve, link, v, tmp, small: None, tables=[(tab, A[:, :, :])])

    with ExitStack() as c:
        A = alloc(c, "A", [P, NJ, F])
        project(X, bd["fc"], A)
        nodes(lambda dve, link, v, tmp, small: None, tables=[(tab, A[:, :, :])])
    with ExitStack() as c:
        last, lastmax = alloc(c, "last", [P, 2 * F]), alloc(c, "lastmax", [P, F])
        softmax_pass("L1", src_in, tab, last, lastmax)
        R = alloc(c, "node_rows", [P, NJ, 2 * F])
        fix_and_fetch("L1", "d", sums2, last, lastmax, R)
        Hn = alloc(c, "Hn", [P, NJ, F])
        B_ = R[:, :, 0:F]
        num = R[:, :, F:2 * F]

        def attend(dve, link, v, tmp, small):
            link(dve.tensor_scalar(B_, B_, 1e-30, None, ALU.max))
            link(dve.reciprocal(tmp[:, :, :], B_))
            link(dve.tensor_tensor(num, num, tmp[:, :, :], ALU.mult))
        nodes(attend)
        project(X, bd["fc"], Hn)
        L_ = R[:, :, 0:F]
        project(Hn, bd["loop"], L_)

        def merge(dve, link, v, tmp, small):
            has = small[2]
            link(dve.tensor_scalar(has[:, :], inv["d"][:, :], 0.0, None, ALU.is_gt))
            link(dve.tensor_tensor(num, num, L_, ALU.add))
            link(dve.tensor_tensor(num, num, pc(has[:, :]), ALU.mult))
            link(dve.tensor_scalar(has[:, :], has[:, :], -1.0, 1.0, ALU.mult, ALU.add))
            link(dve.tensor_tensor(Hn[:, :, :], Hn[:, :, :], pc(has[:, :]), ALU.mult))
            link(dve.tensor_tensor(num, num, Hn[:, :, :], ALU.add))
            link(dve.tensor_scalar(num, num, 0.0, None, ALU.max))
            link(dve.tensor_tensor(X[:, :, :], X[:, :, :], num, ALU.add))
            layernorm(dve, link, X, tmp, small)
        nodes(merge)

    with ExitStack() as c:
        WH = alloc(c, "WH", [P, NJ, F + 1])
        project(X, bd["w2l"], WH[:, :, 0:F])

        def norms(dve, link, v, tmp, small):
            wh = WH[:, :, 0:F]
            link(dve.tensor_tensor(wh, wh, bc(v[0]), ALU.add))
            link(dve.tensor_tensor(tmp[:, :, :], wh, wh, ALU.mult))
            link(dve.reduce_sum(small[0][:, :], tmp[:, :, :], axis=AX.X))
            roots(dve, small[0])
            link(dve.tensor_copy(WH[:, :, F], small[0][:, :]))
        nodes(norms, vectors=[W["L2_gnn_b"]], tables=[(tab65, WH[:, :, :])])
        spread_rows(WH)
    with ExitStack() as c:
        last = alloc(c, "last", [P, F])
        similarity_pass(last)
        R = alloc(c, "node_rows", [P, NJ, F])
        fix_and_fetch("L2", "s", sums, last, None, R)
        A = alloc(c, "A", [P, NJ, F])
        project(X, bd["w2l"], A)

        def propagate(dve, link, v, tmp, small):
            link(dve.tensor_tensor(A[:, :, :], A[:, :, :], bc(v[0]), ALU.add))
            link(dve.tensor_scalar(A[:, :, :], A[:, :, :], co[:, 6:7], None, ALU.mult))
            link(dve.tensor_tensor(R[:, :, :], R[:, :, :], A[:, :, :], ALU.add))
            link(dve.tensor_tensor(X[:, :, :], X[:, :, :], R[:, :, :], ALU.add))
            layernorm(dve, link, X, tmp, small)
        nodes(propagate, vectors=[W["L2_gnn_b"]])

    with ExitStack() as c:
        Q = alloc(c, "Q", [P, NJ, 2 * F])
        project(X, bd["q2"], Q[:, :, 0:F])
        project(X, bd["q3"], Q[:, :, F:2 * F])
        nodes(lambda dve, link, v, tmp, small: None, tables=[(tab128, Q[:, :, :])])
    with ExitStack() as c:
        last, lastmax = alloc(c, "last", [P, 2 * F]), alloc(c, "lastmax", [P, F])
        softmax_pass("L3", src_in, tab128, last, lastmax)
        R = alloc(c, "node_rows", [P, NJ, 2 * F])
        fix_and_fetch("L3", "d", sums2, last, lastmax, R)
        B_ = R[:, :, 0:F]
        num = R[:, :, F:2 * F]

        def final(dve, link, v, tmp, small):
            link(dve.tensor_scalar(B_, B_, 1e-30, None, ALU.max))
            link(dve.reciprocal(tmp[:, :, :], B_))
            link(dve.tensor_tensor(num, num, tmp[:, :, :], ALU.mult))
            link(dve.tensor_tensor(X[:, :, :], X[:, :, :], num, ALU.add))
            layernorm(dve, link, X, tmp, small)
        nodes(final, tables=[(out, X[:, :, :])])
    top.close()


_WEIGHTS = ["L0_gnn_W1", "L0_gnn_b1", "L0_gnn_W2", "L0_gnn_b2", "L1_gnn_W_fc", "L1_gnn_W_fcr", "L1_gnn_loop_W",
            "L2_gnn_W", "L2_gnn_b", "L2_gnn_deg_coeff", "L2_gnn_coeff_param", "L2_gnn_scale_param",
            "L3_gnn_Wd1", "L3_gnn_bd1", "L3_gnn_g1", "L3_gnn_b1", "L3_gnn_Wd2", "L3_gnn_bd2", "L3_gnn_g2", "L3_gnn_b2",
            "L3_gnn_W1", "L3_gnn_W2", "L3_gnn_W3"]


def kernel(**inputs):
    import numpy as _np
    import concourse.bacc as _bacc
    from concourse import mybir as _mybir
    from concourse.bass_utils import run_bass_kernel_spmd as _run

    def padded(a, n, value=0, before=0):
        a = _np.asarray(a)
        o = _np.full((n,) + a.shape[1:], value, a.dtype)
        o[before:before + a.shape[0]] = a
        return o

    arrays = {
        "x": padded(inputs["x"], NP),
        "src": padded(inputs["src"], EP, N),
        "dst": _np.concatenate([_np.full(1, -1, _np.int32), padded(inputs["dst"], EP, N), _np.full(1, -1, _np.int32)]),
        "attr3": padded(inputs["edge_attr_3"], EP),
        "attr64": padded(inputs["edge_attr_64"], EP),
        "w": padded(inputs["edge_weight"], EP),
        "w2": padded(inputs["edge_weight_n2"], EP),
    }
    for name in _WEIGHTS:
        arrays[name] = _np.ascontiguousarray(inputs[name])
    nc = _bacc.Bacc("TRN2", target_bir_lowering=False, num_devices=1)
    arrays = {f"in_{k}": _np.ascontiguousarray(v) for k, v in arrays.items()}
    ap = {k: nc.dram_tensor(k, v.shape, _mybir.dt.from_np(v.dtype), kind="ExternalInput").ap() for k, v in arrays.items()}
    out = nc.dram_tensor("out_0", (NP, F), _mybir.dt.float32, kind="ExternalOutput").ap()
    gnn_resnorm(nc, ap["in_x"], ap["in_src"], ap["in_dst"], ap["in_attr3"], ap["in_attr64"], ap["in_w"], ap["in_w2"],
                {n: ap[f"in_{n}"] for n in _WEIGHTS}, out)
    r = _run(nc, [arrays], core_ids=[0])
    return r.results[0]["out_0"][:N]
```

```python
import concourse.bass as bass
from concourse import mybir
from contextlib import ExitStack

F32 = mybir.dt.float32
I32 = mybir.dt.int32
BF16 = mybir.dt.bfloat16
ALU = mybir.AluOpType
ACT = mybir.ActivationFunctionType
AX = mybir.AxisListType

P = 128
F = 64
N = 12500
E = 212500
NJ = -(-(N + 1) // P)
NP = NJ * P
HI = NJ
T = 64
NT = -(-E // (P * 2 * T)) * 2 * T
NCH = NT // T
EP = P * NT
ROWS = EP + 1
BIG = 1.0e38
NOROW = float(1 << 21)
EPS = 1e-5
G = 14
NG = NJ // G


class Counter:

    def __init__(self, sem):
        self.sem, self.base = sem, 0


def gnn_resnorm(nc, x_in, src_in, dst_in, attr3_in, attr64_in, w_in, w2_in, W, out):
    top = ExitStack()

    unique = [0]

    def alloc(ctx, name, shape, dt=F32):
        unique[0] += 1
        return ctx.enter_context(nc.sbuf_tensor(f"{name}_{unique[0]}", shape, dt))

    def ps(ctx, name, shape, dt=F32):
        unique[0] += 1
        return ctx.enter_context(nc.psum_tensor(f"{name}_{unique[0]}", shape, dt))

    phase_sems = []

    def lasting(name):
        return top.enter_context(nc.semaphore(name))

    def sem(name):
        phase_sems.append(nc.alloc_semaphore(name=name))
        return phase_sems[-1]

    def phase(build):
        def run(*args, **kw):
            build(*args, **kw)
            nc.clear_and_free_semaphores(list(phase_sems))
            phase_sems.clear()
            nc.all_engine_barrier()
        return run

    def dram(name, shape, dt=F32):
        return nc.dram_tensor(name, shape, dt).ap()

    tab = dram("tab", [NP, F])
    tab65 = dram("tab65", [NP, F + 1])
    tab128 = dram("tab128", [NP, 2 * F])
    sums = dram("sums", [ROWS, F])
    sums2 = dram("sums2", [ROWS, 2 * F])
    maxes = dram("maxes", [EP, F])
    dists = dram("dists", [EP, F])
    spread = dram("spread", [EP, F + 1])
    rec = dram("rec", [EP, 3], I32)
    base_in = dram("base", [EP])
    skey = dram("skey", [EP + 2], I32)
    sdst = dram("sdst", [EP], I32)
    sbase = dram("sbase", [EP])
    flat = {n: dram(n, [NP], I32) for n in ("end_d", "end_s", "start_s")}
    flatf = {n: dram(n, [NP]) for n in ("cnt_d", "cnt_s")}

    def cols(ap, c, w=T, first=0):
        if len(ap.shape) == 1:
            return ap.rearrange("(p t) -> p t", p=P)[:, bass.ds(c * w + first, w)]
        return ap.rearrange("(p t) f -> p t f", p=P)[:, bass.ds(c * w + first, w), :]

    X = alloc(top, "X", [P, NJ, F])
    ident = alloc(top, "ident", [P, P])
    keep = {o: alloc(top, f"keep_{o}", [P, NT]) for o in "ds"}
    neg = alloc(top, "neg_d", [P, NT])
    fk = {o: alloc(top, f"fk_{o}", [P, 1]) for o in "ds"}
    aT = {o: alloc(top, f"aT_{o}", [F, P]) for o in "ds"}
    end0 = {o: alloc(top, f"end0_{o}", [P, 1], I32) for o in "ds"}
    endp = {o: alloc(top, f"endp_{o}", [P, NJ], I32) for o in "ds"}
    startp = alloc(top, "startp", [P, NJ], I32)
    inv = {o: alloc(top, f"inv_{o}", [P, NJ]) for o in "ds"}
    co = alloc(top, "co", [P, 16])
    zero = alloc(top, "zero", [P, 1])
    bd = {n: alloc(top, f"bd_{n}", [P, P]) for n in ("a1", "a2", "fc", "fcr", "loop", "w2l", "d2", "q1", "q2", "q3")}

    chain = {e: Counter(lasting(f"chain_{e}")) for e in ("dve", "act", "pool", "pe")}

    def linker(eng, which):
        k = chain[which]

        def link(ins):
            k.base += 1
            ins.then_inc(k.sem, 1)
            eng.wait_ge(k.sem, k.base)
        return link

    @phase
    def constants():
        loaded, made = sem("w_loaded"), sem("ident_made")
        zeroed = sem("bd_zeroed")
        tr_ready, tr_done = sem("wt_ready"), sem("wt_done")
        order = {"a1": "L0_gnn_W1", "a2": "L0_gnn_W2", "fc": "L1_gnn_W_fc", "fcr": "L1_gnn_W_fcr",
                 "loop": "L1_gnn_loop_W", "w2l": "L2_gnn_W", "d2": "L3_gnn_Wd2",
                 "q1": "L3_gnn_W1", "q2": "L3_gnn_W2", "q3": "L3_gnn_W3"}
        with ExitStack() as c, nc.Block() as block:
            tp = ps(c, "wt_ps", [P, P])
            mean = alloc(c, "mean_d2", [P, 1])
            st = alloc(c, "soft", [P, 8])

            @block.gpsimd
            def _(pool):
                pool.memset(ident[:, :], 0.0).then_inc(made, 1)
                pool.wait_ge(made, 1)
                pool.affine_select(out=ident[:, :], in_=ident[:, :], compare_op=ALU.not_equal, fill=1.0, base=0,
                                   pattern=[[-1, P]], channel_multiplier=1).then_inc(made, 1)

            @block.sync
            def _(sp):
                sp.wait_ge(zeroed, len(order) + 2)
                for n, full in order.items():
                    for h in (0, F):
                        sp.dma_start(bd[n][h:h + F, h:h + F], W[full]).then_inc(loaded, 16)
                sp.dma_start(X[:, :, :], x_in.rearrange("(p j) f -> p j f", p=P)).then_inc(loaded, 16)
                for k, (n, w) in enumerate((("L2_gnn_deg_coeff", 2), ("L2_gnn_coeff_param", 3), ("L2_gnn_scale_param", 1))):
                    v = W[n].rearrange("(a n) -> a n", a=1).to_broadcast([P, w])
                    sp.dma_start(co[:, 4 * k:4 * k + w], v).then_inc(loaded, 16)

            @block.vector
            def _(dve):
                link = linker(dve, "dve")
                for n in order:
                    dve.memset(bd[n][:, :], 0.0).then_inc(zeroed, 1)
                dve.memset(co[:, :], 0.0).then_inc(zeroed, 1)
                dve.memset(zero[:, :], 0.0).then_inc(zeroed, 1)
                dve.wait_ge(loaded, 16 * (2 * len(order) + 4))
                for k, n in enumerate(("fc", "fcr")):
                    dve.wait_ge(tr_ready, k + 1)
                    dve.tensor_copy(bd[n][:, :], tp[:, :]).then_inc(tr_done, 1)
                link(dve.reduce_sum(mean[:, :], bd["d2"][:, :], axis=AX.X))
                link(dve.tensor_scalar(mean[:, :], mean[:, :], 1.0 / F, None, ALU.mult))
                for h in (0, F):
                    link(dve.tensor_scalar(bd["d2"][h:h + F, h:h + F], bd["d2"][h:h + F, h:h + F],
                                           mean[h:h + F, 0:1], None, ALU.subtract))
                link(dve.reduce_max(st[:, 0:1], co[:, 4:7], axis=AX.X))
                link(dve.tensor_scalar(co[:, 4:7], co[:, 4:7], st[:, 0:1], None, ALU.subtract))
                dve.tensor_scalar(st[:, 1:2], co[:, 8:9], -1.0, None, ALU.mult).then_inc(chain["dve"].sem, 1)
                chain["dve"].base += 1
                dve.wait_ge(chain["dve"].sem, chain["dve"].base)
                link(dve.tensor_tensor(st[:, 1:2], st[:, 1:2], co[:, 8:9], ALU.min))
                dve.sem_inc(tr_done, 1)
                dve.wait_ge(tr_ready, 3)
                link(dve.reduce_sum(st[:, 2:3], co[:, 4:7], axis=AX.X))
                link(dve.reciprocal(st[:, 3:4], st[:, 2:3]))
                link(dve.tensor_scalar(co[:, 4:7], co[:, 4:7], st[:, 3:4], None, ALU.mult))
                link(dve.tensor_scalar(st[:, 4:5], co[:, 8:9], 0.0, None, ALU.max))
                link(dve.tensor_tensor(co[:, 8:9], st[:, 4:5], st[:, 1:2], ALU.add))
                link(dve.tensor_scalar(co[:, 4:7], co[:, 4:7], co[:, 8:9], None, ALU.mult))

            @block.scalar
            def _(act):
                link = linker(act, "act")
                act.wait_ge(tr_done, 3)
                link(act.activation(co[:, 4:7], co[:, 4:7], ACT.Exp))
                link(act.activation(st[:, 1:2], st[:, 1:2], ACT.Exp))
                act.activation(st[:, 1:2], st[:, 1:2], ACT.Ln, bias=1.0).then_inc(tr_ready, 1)

            @block.tensor
            def _(pe):
                pe.wait_ge(made, 2)
                pe.wait_ge(loaded, 16 * (2 * len(order) + 4))
                for k, n in enumerate(("fc", "fcr")):
                    if k:
                        pe.wait_ge(tr_done, k)
                    pe.transpose(tp[:, :], bd[n][:, :], ident[:, :]).then_inc(tr_ready, 1)

    KC = 16

    class Counting:

        def __init__(self, c, hist):
            self.keys_in, self.const, self.dig_s = sem("keys_in"), sem("count_consts"), sem("digits")
            self.ready, self.used, self.done, self.out = sem("onehots"), sem("onehots_used"), sem("counted"), sem("hist_out")
            self.hist = hist
            self.raw = {o: alloc(c, f"keys_{o}", [P, NT], I32) for o in "ds"}
            self.tmp = alloc(c, "key_tmp", [P, NT], I32)
            self.dig = {d: alloc(c, f"dig_{d}", [P, NT], BF16) for d in ("dl", "dh", "sl", "sh")}
            self.oh = {d: alloc(c, f"oh_{d}", [P, KC, P if d[1] == "l" else HI], BF16) for d in self.dig}
            self.iota_i, self.iota = alloc(c, "iota_i", [P, P], I32), alloc(c, "iota", [P, P], BF16)
            self.H = {o: ps(c, f"H_{o}", [P, P]) for o in "ds"}
            self.zb = alloc(c, "zb", [P, P], BF16)

        def load(self, sp):
            sp.dma_start(self.raw["d"][:, :], dst_in[1:EP + 1].rearrange("(p t) -> p t", p=P)).then_inc(self.keys_in, 16)
            sp.dma_start(self.raw["s"][:, :], src_in.rearrange("(p t) -> p t", p=P)).then_inc(self.keys_in, 16)

        def consts(self, pool):
            pool.memset(self.zb[:, :], 0.0).then_inc(self.const, 1)
            pool.iota(self.iota_i[:, :], pattern=[[1, P]], base=0, channel_multiplier=0).then_inc(self.const, 1)

        def digits(self, dve, link):
            dve.wait_ge(self.const, 2)
            dve.wait_ge(self.keys_in, 32)
            link(dve.tensor_copy(self.iota[:, :], self.iota_i[:, :]))
            for o in "ds":
                link(dve.tensor_scalar(self.tmp[:, :], self.raw[o][:, :], P - 1, None, ALU.bitwise_and))
                link(dve.tensor_copy(self.dig[o + "l"][:, :], self.tmp[:, :]))
                link(dve.tensor_scalar(self.tmp[:, :], self.raw[o][:, :], 7, None, ALU.logical_shift_right))
                link(dve.tensor_copy(self.dig[o + "h"][:, :], self.tmp[:, :]))

        def dve(self, dve, i, b):
            for k in range(T // KC):
                n = (i * 2 + b) * (T // KC) + k
                if not (isinstance(n, int) and n == 0):
                    dve.wait_ge(self.used, n)
                for d, oh in self.oh.items():
                    w = oh.shape[2]
                    v = self.dig[d][:, bass.ds(n * KC, KC)].unsqueeze(2).to_broadcast([P, KC, w])
                    u = self.iota[:, 0:w].unsqueeze(1).to_broadcast([P, KC, w])
                    dve.tensor_tensor(oh[:, :, :], v, u, ALU.is_equal).then_inc(self.ready, 1)

        def pe_begin(self, pe):
            pe.wait_ge(self.const, 2)
            for o in "ds":
                pe.matmul(self.H[o][:, :], self.zb[:, :], self.zb[:, :], start=True, stop=False)

        def pe(self, pe, i, b):
            for k in range(T // KC):
                n = (i * 2 + b) * (T // KC) + k
                pe.wait_ge(self.ready, (n + 1) * 4)
                for t in range(KC):
                    for o in "ds":
                        last = pe.matmul(self.H[o][0:HI, :], self.oh[o + "h"][:, t, :], self.oh[o + "l"][:, t, :],
                                         start=False, stop=False)
                last.then_inc(self.used, 1)

        def pe_end(self, pe):
            for o in "ds":
                last = pe.matmul(self.H[o][:, :], self.zb[:, :], self.zb[:, :], start=False, stop=True)
            last.then_inc(self.done, 1)

        def dve_end(self, dve, link):
            dve.wait_ge(self.done, 1)
            for o in "ds":
                link(dve.tensor_copy(self.hist[o][:, :], self.H[o][:, :]))

    @phase
    def pointers(hist, first_row):
        post, pre, const = sem("hist_sums"), sem("hist_scanned"), sem("ptr_consts")
        stored, back = sem("ptr_stored"), sem("ptr_back")
        with ExitStack() as c, nc.Block() as block:
            ones = alloc(c, "ones_c", [P, P])
            upper = alloc(c, "upper_c", [P, P])
            before = {o: ps(c, f"before_{o}", [P, 1]) for o in "ds"}
            cum = {o: alloc(c, f"cum_{o}", [P, P]) for o in "ds"}
            has, tmp = alloc(c, "has", [P, P]), alloc(c, "tmp_c", [P, P])
            pi = {n: alloc(c, f"pi_{n}", [P, P], I32) for n in flat}
            cb = {o: alloc(c, f"cb_{o}", [P, NJ]) for o in "ds"}
            cm = alloc(c, "cm", [P, NJ])

            @block.gpsimd
            def _(pool):
                pool.memset(ones[:, :], 1.0).then_inc(const, 1)
                pool.wait_ge(const, 1)
                pool.affine_select(out=upper[:, :], in_=ones[:, :], compare_op=ALU.is_gt, fill=0.0, base=0,
                                   pattern=[[1, P]], channel_multiplier=-1).then_inc(const, 1)

            @block.sync
            def _(sp):
                for o in "ds":
                    sp.dma_start(flatf[f"cnt_{o}"].rearrange("(h l) -> h l", l=P), hist[o][0:HI, :]).then_inc(stored, 16)
                sp.wait_ge(post, 2)
                for n in flat:
                    sp.dma_start(flat[n].rearrange("(h l) -> h l", l=P), pi[n][0:HI, :]).then_inc(stored, 16)
                sp.wait_ge(stored, 80)
                for o in "ds":
                    sp.dma_start(cb[o][:, :], flatf[f"cnt_{o}"].rearrange("(p j) -> p j", p=P)).then_inc(back, 16)
                    sp.dma_start(endp[o][:, :], flat[f"end_{o}"].rearrange("(p j) -> p j", p=P)).then_inc(back, 16)
                sp.dma_start(startp[:, :], flat["start_s"].rearrange("(p j) -> p j", p=P)).then_inc(back, 16)

            @block.tensor
            def _(pe):
                pe.wait_ge(const, 2)
                pe.wait_ge(pre, 1)
                for o in "ds":
                    last = pe.matmul(before[o][:, :], upper[:, :], cum[o][:, P - 1:P], start=True, stop=True)
                last.then_inc(post, 1)

            @block.vector
            def _(dve):
                link = linker(dve, "dve")
                dve.wait_ge(const, 2)
                for o in "ds":
                    link(dve.tensor_tensor_scan(cum[o][:, :], ones[:, :], hist[o][:, :], 0.0, ALU.mult, ALU.add))
                dve.sem_inc(pre, 1)
                dve.wait_ge(post, 1)
                for o in "ds":
                    link(dve.tensor_scalar(cum[o][:, :], cum[o][:, :], before[o][:, 0:1], None, ALU.add))
                    link(dve.tensor_scalar(has[:, :], hist[o][:, :], 1.0, None, ALU.min))
                    if o == "s":
                        link(dve.tensor_tensor(first_row[:, :], cum[o][:, :], hist[o][:, :], ALU.subtract))
                        link(dve.tensor_scalar(tmp[:, :], first_row[:, :], -NOROW, None, ALU.add))
                        link(dve.tensor_tensor(tmp[:, :], tmp[:, :], has[:, :], ALU.mult))
                        link(dve.tensor_scalar(tmp[:, :], tmp[:, :], NOROW, None, ALU.add))
                        link(dve.tensor_copy(pi["start_s"][:, :], tmp[:, :]))
                    link(dve.tensor_scalar(cum[o][:, :], cum[o][:, :], -1.0 - EP, None, ALU.add))
                    link(dve.tensor_tensor(cum[o][:, :], cum[o][:, :], has[:, :], ALU.mult))
                    link(dve.tensor_scalar(cum[o][:, :], cum[o][:, :], float(EP), None, ALU.add))
                    link(dve.tensor_copy(pi[f"end_{o}"][:, :], cum[o][:, :]))
                dve.sem_inc(post, 1)
                dve.wait_ge(back, 80)
                for o in "ds":
                    link(dve.tensor_scalar(cm[:, :], cb[o][:, :], 1.0, None, ALU.max))
                    link(dve.reciprocal(inv[o][:, :], cm[:, :]))
                    link(dve.tensor_scalar(cm[:, :], cb[o][:, :], 1.0, None, ALU.min))
                    link(dve.tensor_tensor(inv[o][:, :], inv[o][:, :], cm[:, :], ALU.mult))

    @phase
    def sort_edges(first_row):
        NP2 = T // 2
        NGP = T // 4
        loaded = [sem(f"sort_in{b}") for b in range(2)]
        moved = [sem(f"sort_out{b}") for b in range(2)]
        q = lambda n: sem(f"sort_{n}")
        const, started, copied, packed, dg, ohr, idx_r = (q(n) for n in (
            "consts", "started", "columns", "packed", "digits", "onehots", "idx"))
        tr, tev, eqr, msk, look, placed, pev, rk = (q(n) for n in (
            "turned", "turned_copied", "same", "masked", "looked_up", "placed", "place_copied", "ranked"))
        with ExitStack() as c, nc.Block() as block:
            recs = [alloc(c, f"recs{b}", [P, T, 3], I32) for b in range(2)]
            raw = [alloc(c, f"raw{b}", [P, 3, T], I32) for b in range(2)]
            di, lo, hi = alloc(c, "di", [P, 2, T], I32), alloc(c, "lo", [P, T], BF16), alloc(c, "hi", [P, T], BF16)
            ohl = [alloc(c, f"ohl{b}", [P, T, P], BF16) for b in range(2)]
            ohh = [alloc(c, f"ohh{b}", [P, T, HI], BF16) for b in range(2)]
            ohT = [alloc(c, f"ohT{z}", [P, 4, P]) for z in range(2)]
            same = [[alloc(c, f"same{z}{h}", [P, 3, P], BF16) for h in range(2)] for z in range(2)]
            mask = alloc(c, "mask", [P, 3, P])
            place = alloc(c, "place", [P, HI])
            junk = alloc(c, "junk", [P, HI])
            pos = alloc(c, "pos", [P, T])
            idx = [alloc(c, f"sidx{b}", [P, T], I32) for b in range(2)]
            iota_i, iota = alloc(c, "iota_i", [P, P], I32), alloc(c, "iota", [P, P], BF16)
            identb = alloc(c, "identb", [P, P], BF16)
            pT = [ps(c, f"pT{z}", [P, 4, P], BF16) for z in range(2)]
            pE = [ps(c, f"pE{h}", [P, 3, P]) for h in range(2)]
            pV = [ps(c, f"pV{h}", [P, 2, P]) for h in range(2)]
            pP = ps(c, "pP", [P, HI])

            def zero(n):
                return isinstance(n, int) and n == 0

            @block.sync
            def _(sp):
                def load(i, b):
                    if not zero(i):
                        sp.wait_ge(packed, i * 2 + b - 1)
                    for n, a in enumerate((src_in, dst_in[1:EP + 1], base_in)):
                        d = raw[b][:, n, :]
                        sp.dma_start(d if n < 2 else d.bitcast(F32), cols(a, i * 2 + b)).then_inc(loaded[b], 16)
                pairs(sp, load)

            @block.gpsimd
            def _(pool):
                pool.iota(iota_i[:, :], pattern=[[1, P]], base=0, channel_multiplier=0).then_inc(const, 1)
                pool.memset(mask[:, :, :], 1.0).then_inc(const, 1)
                pool.wait_ge(const, 2)
                for n in (0, 2):
                    pool.affine_select(out=mask[:, n, :], in_=mask[:, n, :], compare_op=ALU.is_gt, fill=0.0, base=0,
                                       pattern=[[1, P]], channel_multiplier=-1).then_inc(const, 1)

                def scatter(i, b):
                    pool.wait_ge(packed, i * 2 + b + 1)
                    pool.wait_ge(idx_r, i * 2 + b + 1)
                    pool.sem_inc(started, 1)
                    for j in range(T):
                        pool.indirect_dma_start(rec, bass.IndirectOffsetOnAxis(ap=idx[b][:, j:j + 1], axis=0),
                                                recs[b][:, j, :], None).then_inc(moved[b], 16)
                with pool.Fori(0, NCH // 2) as i:
                    scatter(i, 0)
                    scatter(i, 1)
                for b in range(2):
                    pool.wait_ge(moved[b], NCH // 2 * 16 * T)

            @block.scalar
            def _(act):
                def pack(i, b):
                    act.wait_ge(loaded[b], (i + 1) * 48)
                    if not zero(i):
                        act.wait_ge(moved[b], i * 16 * T)
                    for n in range(3):
                        s, d = raw[b][:, n, :], recs[b][:, :, n]
                        if n == 2:
                            s, d = s.bitcast(F32), d.bitcast(F32)
                        act.activation(d, s, ACT.Copy).then_inc(copied, 1)
                    act.wait_ge(copied, (i * 2 + b + 1) * 3)
                    act.sem_inc(packed, 1)

                def turned(ch, g, z):
                    act.wait_ge(tr, ch * NGP + g + 1)
                    if not (zero(ch) and g < 2):
                        act.wait_ge(look, ch * NP2 + 2 * g - 2)
                    act.activation(ohT[z][:, :, :], pT[z][:, :, :], ACT.Copy).then_inc(tev, 1)

                def step(i, b):
                    ch = i * 2 + b
                    turned(ch, 0, 0)
                    for g in range(NGP):
                        if g + 1 < NGP:
                            turned(ch, g + 1, (g + 1) % 2)
                        for h in range(2):
                            act.wait_ge(placed, ch * NP2 + 2 * g + h + 2)
                            act.activation(place[:, :], pP[:, :], ACT.Copy).then_inc(pev, 1)
                        if g == 3 * NGP // 4:
                            pack(i, b)
                act.wait_ge(placed, 1)
                act.activation(place[:, :], pP[:, :], ACT.Copy).then_inc(pev, 1)
                pairs(act, step)

            @block.vector
            def _(dve):
                link = linker(dve, "dve")
                dve.wait_ge(const, 4)
                link(dve.tensor_copy(iota[:, :], iota_i[:, :]))
                link(dve.tensor_copy(identb[:, :], ident[:, :]))
                dve.sem_inc(const, 1)

                def digits(i, b):
                    ch = i * 2 + b
                    dve.wait_ge(loaded[b], (i + 1) * 48)
                    if not zero(ch):
                        dve.wait_ge(ohr, ch * 2 * NGP)
                    dve.tensor_scalar(di[:, 0, :], raw[b][:, 0, :], P - 1, None, ALU.bitwise_and).then_inc(dg, 1)
                    dve.tensor_scalar(di[:, 1, :], raw[b][:, 0, :], 7, None, ALU.logical_shift_right).then_inc(dg, 1)
                    dve.wait_ge(dg, ch * 4 + 2)
                    dve.tensor_copy(lo[:, :], di[:, 0, :]).then_inc(dg, 1)
                    dve.tensor_copy(hi[:, :], di[:, 1, :]).then_inc(dg, 1)
                    dve.wait_ge(dg, ch * 4 + 4)

                def onehots(ch, b, g):
                    for src, dst, w in ((lo, ohl, P), (hi, ohh, HI)):
                        v = src[:, 4 * g:4 * g + 4].unsqueeze(2).to_broadcast([P, 4, w])
                        u = iota[:, 0:w].unsqueeze(1).to_broadcast([P, 4, w])
                        dve.tensor_tensor(dst[b][:, 4 * g:4 * g + 4, :], v, u, ALU.is_equal).then_inc(ohr, 1)

                def masks_(ch, g):
                    for h in range(2):
                        dve.wait_ge(eqr, ch * NP2 + 2 * g + h + 1)
                        if not (zero(ch) and g < 2):
                            dve.wait_ge(look, ch * NP2 + 2 * g + h - 3)
                        dve.tensor_tensor(same[g % 2][h][:, :, :], pE[h][:, :, :], mask[:, :, :], ALU.mult).then_inc(msk, 1)

                def ranks(ch, g, h, b):
                    dve.wait_ge(look, ch * NP2 + 2 * g + h + 1)
                    for k in range(2):
                        t = 4 * g + 2 * h + k
                        if not (zero(ch) and t == 0):
                            dve.wait_ge(rk, ch * T + t)
                        dve.tensor_tensor_reduce(out=junk[:, :], in0=pV[h][:, k, 0:HI], in1=ohh[b][:, t, :], scale=1.0, scalar=0.0,
                                                 op0=ALU.mult, op1=ALU.add, accum_out=pos[:, t:t + 1]).then_inc(rk, 1)

                def step(i, b, last=False):
                    ch = i * 2 + b
                    if not last:
                        digits(*((i, 1) if b == 0 else (i + 1, 0)))
                    masks_(ch, 0)
                    for g in range(NGP):
                        ranks(ch, g, 0, b)
                        if g + 1 < NGP:
                            masks_(ch, g + 1)
                        ranks(ch, g, 1, b)
                        if not last:
                            onehots(ch + 1, 1 - b, g)
                    dve.wait_ge(rk, (ch + 1) * T)
                    if not zero(i):
                        dve.wait_ge(moved[b], i * 16 * T)
                    dve.tensor_copy(idx[b][:, :], pos[:, :]).then_inc(idx_r, 1)
                    dve.wait_ge(idx_r, ch + 1)
                digits(0, 0)
                for g in range(NGP):
                    onehots(0, 0, g)
                step(0, 0)
                step(0, 1)
                with dve.Fori(1, NCH // 2 - 1) as i:
                    step(i, 0)
                    step(i, 1)
                step(NCH // 2 - 1, 0)
                step(NCH // 2 - 1, 1, last=True)

            @block.tensor
            def _(pe):
                pe.wait_ge(const, 5)
                pe.matmul(pP[:, :], first_row[:, :], ident[:, 0:HI], start=True, stop=True).then_inc(placed, 1)

                def turn(ch, g, b):
                    if not (zero(ch) and g < 2):
                        pe.wait_ge(tev, ch * NGP + g - 1)
                    pe.wait_ge(ohr, (ch * NGP + g + 1) * 2)
                    for t in range(4):
                        last = pe.transpose(pT[g % 2][:, t, :], ohl[b][:, 4 * g + t, :], identb[:, :])
                    last.then_inc(tr, 1)

                def equal(ch, g):
                    pe.wait_ge(tev, ch * NGP + g + 1)
                    o = ohT[g % 2]
                    for h in range(2):
                        if not (zero(ch) and g == 0):
                            pe.wait_ge(msk, ch * NP2 + 2 * g + h - 1)
                        pe.matmul(pE[h][:, 0:2, :].rearrange("p a e -> p (a e)"), o[:, 2 * h, :],
                                  o[:, 2 * h:2 * h + 2, :].rearrange("p a e -> p (a e)"), start=True, stop=True)
                        pe.matmul(pE[h][:, 2, :], o[:, 2 * h + 1, :], o[:, 2 * h + 1, :],
                                  start=True, stop=True).then_inc(eqr, 1)

                def rows_of(ch, g, h, b):
                    n = ch * NP2 + 2 * g + h
                    o, s, t = ohT[g % 2], same[g % 2][h], 4 * g + 2 * h
                    pe.wait_ge(msk, n + 1)
                    pe.wait_ge(pev, n + 1)
                    if not (zero(ch) and g == 0):
                        pe.wait_ge(rk, 2 * n - 2)
                    pe.matmul(pV[h][:, 0, 0:HI], o[:, 2 * h, :], place[:, :], start=True, stop=False)
                    pe.matmul(pV[h][:, 0, 0:HI], s[:, 0, :], ohh[b][:, t, :], start=False, stop=True)
                    pe.matmul(pV[h][:, 1, 0:HI], o[:, 2 * h + 1, :], place[:, :], start=True, stop=False)
                    pe.matmul(pV[h][:, 1, 0:HI], s[:, 1, :], ohh[b][:, t, :], start=False, stop=False)
                    pe.matmul(pV[h][:, 1, 0:HI], s[:, 2, :], ohh[b][:, t + 1, :], start=False, stop=True).then_inc(look, 1)
                    for k in range(2):
                        last = pe.matmul(pP[:, :], ohl[b][:, t + k, :], ohh[b][:, t + k, :], start=False, stop=k == 1,
                                         skip_group_check=True)
                    last.then_inc(placed, 1)

                def step(i, b):
                    ch = i * 2 + b
                    turn(ch, 0, b)
                    equal(ch, 0)
                    for g in range(NGP):
                        if g + 1 < NGP:
                            turn(ch, g + 1, b)
                        rows_of(ch, g, 0, b)
                        if g + 1 < NGP:
                            equal(ch, g + 1)
                        rows_of(ch, g, 1, b)
                pairs(pe, step)

    @phase
    def edge_weights():
        ld, pr, wr, ax = sem("weights_loaded"), sem("weights_ready"), sem("weights_written"), sem("softplus_ready")
        with ExitStack() as c, nc.Block() as block:
            s_c, d_c = alloc(c, "s_c", [P, NT], I32), alloc(c, "d_c", [P, NT], I32)
            w_c, v = alloc(c, "w_c", [P, NT]), alloc(c, "v", [P, NT])
            a, b = alloc(c, "a", [P, NT]), alloc(c, "b", [P, NT])
            flat_ = lambda x: x.rearrange("(p t) -> p t", p=P)

            @block.sync
            def _(sp):
                sp.dma_start(v[:, :], flat_(w2_in)).then_inc(ld, 16)
                sp.dma_start(s_c[:, :], flat_(src_in)).then_inc(ld, 16)
                sp.dma_start(d_c[:, :], flat_(dst_in[1:EP + 1])).then_inc(ld, 16)
                sp.dma_start(w_c[:, :], flat_(w_in)).then_inc(ld, 16)
                sp.wait_ge(pr, 1)
                sp.dma_start(flat_(base_in), w_c[:, :]).then_inc(wr, 16)
                sp.wait_ge(wr, 16)

            @block.vector
            def _(dve):
                link = linker(dve, "dve")
                dve.wait_ge(ld, 64)
                link(dve.tensor_scalar(v[:, :], v[:, :], co[:, 0:1], co[:, 1:2], ALU.mult, ALU.add))
                link(dve.tensor_scalar(a[:, :], v[:, :], -1.0, None, ALU.mult))
                link(dve.tensor_tensor(a[:, :], a[:, :], v[:, :], ALU.min))
                dve.sem_inc(ax, 1)
                link(dve.tensor_scalar(b[:, :], v[:, :], 0.0, None, ALU.max))
                dve.wait_ge(ax, 2)
                link(dve.tensor_tensor(b[:, :], b[:, :], a[:, :], ALU.add))
                link(dve.tensor_tensor(v[:, :], s_c[:, :], d_c[:, :], ALU.not_equal))
                link(dve.tensor_tensor(b[:, :], b[:, :], v[:, :], ALU.mult))
                link(dve.tensor_tensor(w_c[:, :], b[:, :], w_c[:, :], ALU.mult))
                dve.sem_inc(pr, 1)

            @block.scalar
            def _(act):
                link = linker(act, "act")
                act.wait_ge(ax, 1)
                link(act.activation(a[:, :], a[:, :], ACT.Exp))
                link(act.activation(a[:, :], a[:, :], ACT.Ln, bias=1.0))
                act.sem_inc(ax, 1)

    @phase
    def unpack_sorted():
        ld, pr, wr = sem("rec_loaded"), sem("rec_ready"), sem("rec_written")
        with ExitStack() as c, nc.Block() as block:
            r = alloc(c, "r", [P, NT, 3], I32)
            s_c, d_c = alloc(c, "s_c", [P, NT], I32), alloc(c, "d_c", [P, NT], I32)
            w_c = alloc(c, "w_c", [P, NT])
            end = alloc(c, "end", [1, 2], I32)

            @block.sync
            def _(sp):
                sp.dma_start(r[:, :, :], rec.rearrange("(p t) f -> p t f", p=P)).then_inc(ld, 16)
                sp.wait_ge(pr, 1)
                sp.dma_start(skey[1:EP + 1].rearrange("(p t) -> p t", p=P), s_c[:, :]).then_inc(wr, 16)
                sp.wait_ge(pr, 2)
                sp.dma_start(skey[0:1].rearrange("(a n) -> a n", a=1), end[:, 0:1]).then_inc(wr, 16)
                sp.dma_start(skey[EP + 1:EP + 2].rearrange("(a n) -> a n", a=1), end[:, 1:2]).then_inc(wr, 16)
                sp.wait_ge(pr, 3)
                sp.dma_start(sdst.rearrange("(p t) -> p t", p=P), d_c[:, :]).then_inc(wr, 16)
                sp.wait_ge(pr, 4)
                sp.dma_start(sbase.rearrange("(p t) -> p t", p=P), w_c[:, :]).then_inc(wr, 16)
                sp.wait_ge(wr, 80)

            @block.vector
            def _(dve):
                dve.wait_ge(ld, 16)
                dve.tensor_copy(s_c[:, :], r[:, :, 0]).then_inc(pr, 1)
                dve.memset(end[:, :], -1).then_inc(pr, 1)
                dve.tensor_copy(d_c[:, :], r[:, :, 1]).then_inc(pr, 1)
                dve.tensor_copy(w_c[:, :], r[:, :, 2].bitcast(F32)).then_inc(pr, 1)

    @phase
    def masks(o, keys):
        ld, tr, bc = sem(f"mask_{o}_in"), sem(f"mask_{o}_T"), sem(f"mask_{o}_b")
        with ExitStack() as c, nc.Block() as block:
            k = [alloc(c, f"k{n}", [P, NT], I32) for n in range(3)]
            nx, col = alloc(c, "nx", [P, NT]), alloc(c, "col", [P, NT], I32)
            colf = alloc(c, "colf", [P, NT])
            rowb, rowf = alloc(c, "rowb", [P, 1], I32), alloc(c, "rowf", [P, 1])
            m = alloc(c, "m", [P, 1])
            ab = alloc(c, "ab", [P, F])
            pt = ps(c, "pt", [F, P])
            io = sem(f"mask_{o}_iota")

            @block.sync
            def _(sp):
                for n in range(3):
                    sp.dma_start(k[n][:, :], keys[n:n + EP].rearrange("(p t) -> p t", p=P)).then_inc(ld, 16)

            @block.gpsimd
            def _(pool):
                pool.iota(col[:, :], pattern=[[1, NT]], base=0, channel_multiplier=0).then_inc(io, 1)
                pool.iota(rowb[:, :], pattern=[[0, 1]], base=0, channel_multiplier=NT).then_inc(io, 1)

            @block.vector
            def _(dve):
                link = linker(dve, "dve")
                dve.wait_ge(ld, 48)
                dve.wait_ge(io, 2)
                kp = keep[o]
                link(dve.tensor_tensor(kp[:, :], k[1][:, :], k[0][:, :], ALU.is_equal))
                link(dve.tensor_tensor(nx[:, :], k[1][:, :], k[2][:, :], ALU.is_equal))
                link(dve.tensor_copy(fk[o][:, :], kp[:, 0:1]))
                link(dve.tensor_reduce(out=m[:, :], in_=kp[:, :], op=ALU.min, axis=AX.X))
                link(dve.memset(ab[:, :], 0.0))
                link(dve.tensor_scalar(ab[:, :], ab[:, :], m[:, 0:1], None, ALU.add))
                dve.sem_inc(bc, 1)
                link(dve.memset(kp[:, 0:1], 0.0))
                if o == "d":
                    link(dve.tensor_scalar(neg[:, :], nx[:, :], 1.0, BIG, ALU.subtract, ALU.mult))
                link(dve.tensor_copy(colf[:, :], col[:, :]))
                link(dve.tensor_scalar(nx[:, :], nx[:, :], NOROW, None, ALU.mult))
                link(dve.tensor_tensor(nx[:, :], nx[:, :], colf[:, :], ALU.add))
                link(dve.tensor_reduce(out=m[:, :], in_=nx[:, :], op=ALU.min, axis=AX.X))
                link(dve.tensor_copy(rowf[:, :], rowb[:, :]))
                link(dve.tensor_tensor(m[:, :], m[:, :], rowf[:, :], ALU.add))
                link(dve.tensor_copy(end0[o][:, :], m[:, :]))
                dve.wait_ge(tr, 1)
                link(dve.tensor_copy(aT[o][:, :], pt[:, :]))

            @block.tensor
            def _(pe):
                pe.wait_ge(bc, 1)
                pe.transpose(pt[:, :], ab[:, :], ident[:, :]).then_inc(tr, 1)

    def gathers(pool, table, idx, rows, idx_in, rows_in, free, go, w, n):
        def gather(i, b):
            if not isinstance(i, int) or i:
                free(pool, i, b)
            pool.wait_ge(idx_in[b], (i + 1) * 16)
            pool.sem_inc(go, 1)
            for j in range(w):
                pool.indirect_dma_start(rows[b][:, j, :], None, table,
                                        bass.IndirectOffsetOnAxis(ap=idx[b][:, j:j + 1], axis=0)).then_inc(rows_in[b], 16)
        pairs(pool, gather, n)

    def pairs(eng, step, n=NCH):
        step(0, 0)
        step(0, 1)
        with eng.Fori(1, n // 2) as i:
            step(i, 0)
            step(i, 1)

    DW = 16
    QUARTER = NT // 4
    dist_w = alloc(top, "dist_w", [F + 1, DW * F])
    dist_b2 = alloc(top, "dist_b2", [1, 4 * P])
    dist_v = {n: alloc(top, f"dist_{n}", [P, F]) for n in ("g1", "b1", "g2", "b2")}
    ones_row = alloc(top, "ones_row", [1, P])

    class Distances:

        def __init__(self, c, q):
            S = lambda n: sem(f"dist{q}_{n}")
            self.first = q * QUARTER
            self.a3_in, self.a3_T, self.a3_s, self.y1, self.y1_s = S("a3_in"), S("a3_T"), S("a3_s"), S("y1"), S("y1_s")
            self.sq, self.ln, self.ge, self.tr, self.ts, self.y2, self.y2_s = (S(n) for n in ("sq", "ln", "ge", "tr", "ts", "y2", "y2_s"))
            self.k, self.stored, self.var, self.sd = S("dve"), S("stored"), S("var"), S("sd")
            self.a3 = alloc(c, "a3", [P, P])
            self.a3T = alloc(c, "a3T", [F + 1, P])
            self.Y, self.SQ = alloc(c, "Y", [P, DW, F]), alloc(c, "SQ", [P, DW, F])
            self.yT = alloc(c, "yT", [P, 4, P])
            self.ss = alloc(c, "ss", [P, DW])
            self.pa, self.p1 = ps(c, "pa", [P, P]), ps(c, "p1", [P, DW, F])
            self.pt, self.p2 = ps(c, "pt", [P, 4, P]), ps(c, "p2", [P, 4, P])

        def start(self, dve):
            dve.memset(self.a3[:, :], 0.0).then_inc(self.k, 1)
            dve.memset(self.a3T[:, :], 1.0).then_inc(self.k, 1)

        def load(self, sp, i, b):
            ch = i * 2 + b
            if isinstance(ch, int) and ch == 0:
                sp.wait_ge(self.k, 2)
            else:
                sp.wait_ge(self.a3_T, ch)
            src = attr3_in.rearrange("(p t) f -> p (t f)", p=P)[:, bass.ds(ch * DW * 3 + self.first * 3, DW * 3)]
            sp.dma_start(self.a3[:, 0:DW * 3], src).then_inc(self.a3_in, 16)

        def store(self, sp, i, b):
            ch = i * 2 + b
            sp.wait_ge(self.ge, ch * 2 + 2)
            sp.dma_start(cols(dists, ch, DW, self.first), self.Y[:, :, :]).then_inc(self.stored, 16)

        def pe_first(self, pe, i, b):
            ch = i * 2 + b
            pe.wait_ge(self.a3_in, ch * 16 + 16)
            pe.transpose(self.pa[:, :], self.a3[:, :], ident[:, :]).then_inc(self.a3_T, 1)
            pe.wait_ge(self.a3_s, ch + 1)
            for h in range(2):
                t = pe.matmul(self.p1[:, 8 * h:8 * h + 8, :].rearrange("p a f -> p (a f)"), self.a3T[:, :],
                              dist_w[:, h * 512:(h + 1) * 512], start=True, stop=True)
            t.then_inc(self.y1, 1)

        def pe_second(self, pe, i, b):
            ch = i * 2 + b
            first = isinstance(ch, int) and ch == 0
            pe.wait_ge(self.ge, ch * 2 + 1)
            for g in range(2):
                for h in range(4):
                    r = self.Y[:, 8 * g + 2 * h:8 * g + 2 * h + 2, :].rearrange("p a f -> p (a f)")
                    t = pe.transpose(self.pt[:, h, :], r, ident[:, :])
                t.then_inc(self.tr, 1)
                pe.wait_ge(self.ts, ch * 2 + g + 1)
                if g or not first:
                    pe.wait_ge(self.y2_s, ch * 2 + g)
                pe.matmul(self.p2[:, :, :].rearrange("p a f -> p (a f)"), ones_row[:, :], dist_b2[:, :], start=True, stop=False)
                for h in range(4):
                    t = pe.matmul(self.p2[:, h, :], self.yT[:, h, :], bd["d2"][:, :], start=False, stop=h == 3)
                t.then_inc(self.y2, 1)

        def act(self, act, i, b):
            ch = i * 2 + b
            act.wait_ge(self.a3_T, ch + 1)
            act.activation(self.a3T[0:F, :], self.pa[0:F, :], ACT.Copy).then_inc(self.a3_s, 1)
            act.wait_ge(self.y1, ch + 1)
            if not (isinstance(ch, int) and ch == 0):
                act.wait_ge(self.stored, ch * 16)
            flat_ = lambda t: t[:, :, :].rearrange("p a f -> p (a f)")
            act.activation(flat_(self.Y), flat_(self.p1), ACT.Copy).then_inc(self.y1_s, 1)
            act.wait_ge(self.y1_s, ch + 1)
            act.activation(self.SQ[:, :, :], self.Y[:, :, :], ACT.Square).then_inc(self.sq, 1)
            act.wait_ge(self.var, ch * 2 + 1)
            act.activation(self.ss[:, :], self.ss[:, :], ACT.Sqrt).then_inc(self.sd, 1)
            act.wait_ge(self.ln, ch * 2 + 1)
            act.activation(self.Y[:, :, :], self.Y[:, :, :], ACT.Gelu).then_inc(self.ge, 1)
            for g in range(2):
                act.wait_ge(self.tr, ch * 2 + g + 1)
                act.activation(self.yT[:, :, :], self.pt[:, :, :], ACT.Copy).then_inc(self.ts, 1)
                act.wait_ge(self.y2, ch * 2 + g + 1)
                act.activation(self.Y[:, 8 * g:8 * g + 8, :].rearrange("p a f -> p (a f)"),
                               self.p2[:, :, :].rearrange("p a f -> p (a f)"), ACT.Copy).then_inc(self.y2_s, 1)
            act.wait_ge(self.y2_s, ch * 2 + 2)
            act.activation(self.SQ[:, :, :], self.Y[:, :, :], ACT.Square).then_inc(self.sq, 1)
            act.wait_ge(self.var, ch * 2 + 2)
            act.activation(self.ss[:, :], self.ss[:, :], ACT.Sqrt).then_inc(self.sd, 1)
            act.wait_ge(self.ln, ch * 2 + 2)
            act.activation(self.Y[:, :, :], self.Y[:, :, :], ACT.Gelu).then_inc(self.ge, 1)

        def dve(self, dve, i, b, h):
            ch = i * 2 + b
            k = [ch * 12 + 6 * h + 2]

            def link(ins):
                ins.then_inc(self.k, 1)
                k[0] = k[0] + 1
                dve.wait_ge(self.k, k[0])
            Y, ss = self.Y, self.ss
            dve.wait_ge(self.sq, ch * 2 + h + 1)
            link(dve.reduce_sum(ss[:, :], self.SQ[:, :, :], axis=AX.X))
            link(dve.tensor_scalar(ss[:, :], ss[:, :], 1.0 / F, EPS, ALU.mult, ALU.add))
            dve.sem_inc(self.var, 1)
            dve.wait_ge(self.sd, ch * 2 + h + 1)
            link(dve.reciprocal(ss[:, :], ss[:, :]))
            link(dve.tensor_tensor(Y[:, :, :], Y[:, :, :], ss[:, :].unsqueeze(2).to_broadcast([P, DW, F]), ALU.mult))
            g, bb = dist_v[f"g{h + 1}"], dist_v[f"b{h + 1}"]
            link(dve.tensor_tensor(Y[:, :, :], Y[:, :, :], g[:, :].unsqueeze(1).to_broadcast([P, DW, F]), ALU.mult))
            link(dve.tensor_tensor(Y[:, :, :], Y[:, :, :], bb[:, :].unsqueeze(1).to_broadcast([P, DW, F]), ALU.add))
            dve.sem_inc(self.ln, 1)

    @phase
    def sum_pass(name, o, idx_arr, table, last, quarter, hist=None):
        S = lambda n: [sem(f"{name}_{n}{b}") for b in range(2)]
        idx_in, rows_in, stored = S("idx"), S("rows"), S("stored")
        scanned, carried, go = sem(f"{name}_scanned"), sem(f"{name}_carried"), sem(f"{name}_go")
        with ExitStack() as c, nc.Block() as block:
            idx = [alloc(c, f"idx{b}", [P, T], I32) for b in range(2)]
            rows = [alloc(c, f"rows{b}", [P, T, F]) for b in range(2)]
            dist = Distances(c, quarter)
            cnt = Counting(c, hist) if hist else None

            @block.sync
            def _(sp):
                def load(i, b):
                    if not isinstance(i, int) or i:
                        sp.wait_ge(rows_in[b], i * 16 * T)
                    sp.dma_start(idx[b][:, :], cols(idx_arr, i * 2 + b)).then_inc(idx_in[b], 16)
                    dist.load(sp, i, b)

                def step(i, b):
                    load(i, b)
                    if not isinstance(i, int) or i or b:
                        bb, ii = (1, i - 1) if b == 0 else (0, i)
                        store(ii, bb)

                def store(i, b):
                    sp.wait_ge(scanned, (i * 2 + b + 1) * F)
                    sp.dma_start(cols(sums[0:EP, :], i * 2 + b), rows[b][:, :, :]).then_inc(stored[b], 16)
                    dist.store(sp, i, b)
                if cnt:
                    cnt.load(sp)
                pairs(sp, step)
                store(NCH // 2 - 1, 1)
                for b in range(2):
                    sp.wait_ge(stored[b], NCH // 2 * 16)
                sp.wait_ge(dist.stored, NCH * 16)

            @block.gpsimd
            def _(pool):
                if cnt:
                    cnt.consts(pool)
                gathers(pool, table, idx, rows, idx_in, rows_in, lambda e, i, b: e.wait_ge(stored[b], i * 16), go, T, NCH)

            @block.tensor
            def _(pe):
                def step(i, b):
                    dist.pe_first(pe, i, b)
                    if cnt:
                        cnt.pe(pe, i, b)
                    dist.pe_second(pe, i, b)
                if cnt:
                    cnt.pe_begin(pe)
                pairs(pe, step)
                if cnt:
                    cnt.pe_end(pe)

            @block.scalar
            def _(act):
                pairs(act, lambda i, b: dist.act(act, i, b))

            @block.vector
            def _(dve):
                dist.start(dve)
                dve.memset(last[:, :], 0.0).then_inc(carried, 1)

                def scan(i, b):
                    ch = i * 2 + b
                    dist.dve(dve, i, b, 0)
                    if cnt:
                        cnt.dve(dve, i, b)
                    dve.wait_ge(rows_in[b], (i + 1) * 16 * T)
                    dve.wait_ge(carried, ch + 1)
                    k = keep[o][:, bass.ds(ch * T, T)]
                    for f in range(F):
                        dve.tensor_tensor_scan(rows[b][:, :, f], k, rows[b][:, :, f], last[:, f:f + 1],
                                               ALU.mult, ALU.add).then_inc(scanned, 1)
                    dve.wait_ge(scanned, (ch + 1) * F)
                    dve.tensor_copy(last[:, :], rows[b][:, T - 1, :]).then_inc(carried, 1)
                    dist.dve(dve, i, b, 1)
                link = linker(dve, "dve")
                if cnt:
                    cnt.digits(dve, link)
                pairs(dve, scan)
                if cnt:
                    cnt.dve_end(dve, link)

    TS = 52

    @phase
    def softmax_pass(name, idx_arr, table, last, lastmax):
        NC = NT // TS
        one = name == "L1"
        W_ = F if one else 2 * F
        S = lambda n: [sem(f"{name}_{n}{b}") for b in range(2)]
        q = lambda n: sem(f"{name}_{n}")
        idx_in, rows_in = S("idx"), S("rows")
        go, side_in, maxed, dk, faded, valued, summed, carried, mstored, sstored = (q(n) for n in (
            "go", "side_in", "maxed", "steps", "faded", "valued", "summed", "carried", "mstored", "sstored"))
        hs, ml, ml2, cp = q("hscan"), q("logit"), q("weighted"), q("copy")
        tr, ts, lg, ls, t1 = q("tr"), q("ts"), q("lg"), q("ls"), q("act")
        GR = [(4 * g, min(4, TS // 2 - 4 * g)) for g in range(-(-TS // 8))]
        NGR = len(GR)
        with ExitStack() as c, nc.Block() as block:
            idx = [alloc(c, f"idx{b}", [P, TS], I32) for b in range(2)]
            rows = [alloc(c, f"rows{b}", [P, TS, W_]) for b in range(2)]
            side = alloc(c, "side", [P, TS, F])
            L1b = alloc(c, "logits", [P, TS, F]) if one else None
            Hh = alloc(c, "H", [P, TS + 1, F])
            XB, PB = alloc(c, "XB", [P, TS, F]), alloc(c, "PB", [P, TS, F])
            DN = alloc(c, "DN", [P, TS, 2 * F])
            if one:
                aT_ = [alloc(c, f"attrT{n}", [P, 4, P]) for n in range(2)]
                pt = [ps(c, f"pt{n}", [P, 4, P]) for n in range(2)]
                pl = [ps(c, f"pl{n}", [P, 4, P]) for n in range(2)]

            def lg_of(b):
                return L1b[:, :, :] if one else rows[b][:, :, 0:F]

            def val_of(b):
                return rows[b][:, :, :] if one else rows[b][:, :, F:2 * F]

            @block.sync
            def _(sp):
                def step(i, b):
                    ch = i * 2 + b
                    if not isinstance(i, int) or i:
                        sp.wait_ge(rows_in[b], i * 16 * TS)
                    sp.dma_start(idx[b][:, :], cols(idx_arr, ch, TS)).then_inc(idx_in[b], 16)
                    if not isinstance(i, int) or i or b:
                        if one:
                            sp.wait_ge(tr, ch * NGR)
                        else:
                            sp.wait_ge(valued, ch)
                    sp.dma_start(side[:, :, :], cols(attr64_in if one else dists, ch, TS)).then_inc(side_in, 16)
                    if not isinstance(i, int) or i or b:
                        store(ch - 1)

                def store(ch):
                    sp.wait_ge(maxed, ch + 1)
                    sp.dma_start(cols(maxes, ch, TS), Hh[:, 0:TS, :]).then_inc(mstored, 16)
                    sp.wait_ge(summed, (ch + 1) * 2 * F)
                    sp.dma_start(cols(sums2[0:EP, :], ch, TS), DN[:, :, :]).then_inc(sstored, 16)
                pairs(sp, step, NC)
                store(NC - 1)
                sp.wait_ge(mstored, NC * 16)
                sp.wait_ge(sstored, NC * 16)

            @block.gpsimd
            def _(pool):
                gathers(pool, table, idx, rows, idx_in, rows_in,
                        lambda e, i, b: e.wait_ge(summed, (i * 2 + b - 1) * 2 * F), go, TS, NC)

            @block.tensor
            def _(pe):
                def step(i, b):
                    ch = i * 2 + b
                    pe.wait_ge(side_in, ch * 16 + 16)
                    for g, (h0, n) in enumerate(GR):
                        z = (b * NGR + g) % 2
                        first = (isinstance(i, int) and i == 0) and b * NGR + g < 2
                        if not first:
                            pe.wait_ge(ts, ch * NGR + g - 1)
                        for h in range(n):
                            r = side[:, 2 * (h0 + h):2 * (h0 + h) + 2, :].rearrange("p a f -> p (a f)")
                            t = pe.transpose(pt[z][:, h, :], r, ident[:, :])
                        t.then_inc(tr, 1)
                        pe.wait_ge(ts, ch * NGR + g + 1)
                        if not first:
                            pe.wait_ge(ls, ch * NGR + g - 1)
                        for h in range(n):
                            t = pe.matmul(pl[z][:, h, :], aT_[z][:, h, :], bd["fcr"][:, :], start=True, stop=True)
                        t.then_inc(lg, 1)
                if one:
                    pairs(pe, step, NC)

            @block.scalar
            def _(act):
                def logits(i, b):
                    ch = i * 2 + b
                    for g, (h0, n) in enumerate(GR):
                        z = (b * NGR + g) % 2
                        act.wait_ge(tr, ch * NGR + g + 1)
                        if not ((isinstance(i, int) and i == 0) and b * NGR + g < 2):
                            act.wait_ge(lg, ch * NGR + g - 1)
                        act.activation(aT_[z][:, 0:n, :], pt[z][:, 0:n, :], ACT.Copy).then_inc(ts, 1)
                        act.wait_ge(lg, ch * NGR + g + 1)
                        if g == 0 and not (isinstance(i, int) and i == 0 and b == 0):
                            act.wait_ge(valued, ch)
                        act.activation(L1b[:, 2 * h0:2 * (h0 + n), :].rearrange("p a f -> p (a f)"),
                                       pl[z][:, 0:n, :].rearrange("p a f -> p (a f)"), ACT.Copy).then_inc(ls, 1)

                def fades(i, b):
                    ch = i * 2 + b
                    act.wait_ge(dk, ch + 1)
                    if not (isinstance(i, int) and i == 0 and b == 0):
                        act.wait_ge(summed, ch * 2 * F)
                    act.activation(PB[:, :, :], XB[:, :, :], ACT.Relu, scale=-1.0).then_inc(t1, 1)
                    act.wait_ge(t1, ch * 2 + 1)
                    act.activation(XB[:, :, :], XB[:, :, :], ACT.Relu).then_inc(t1, 1)
                    act.activation(PB[:, :, :], PB[:, :, :], ACT.Exp, scale=-1.0).then_inc(faded, 1)
                    act.wait_ge(t1, ch * 2 + 2)
                    act.activation(XB[:, :, :], XB[:, :, :], ACT.Exp, scale=-1.0).then_inc(faded, 1)
                if one:
                    logits(0, 0)
                    fades(0, 0)
                    logits(0, 1)
                    fades(0, 1)
                    with act.Fori(1, NC // 2) as i:
                        logits(i, 0)
                        fades(i, 0)
                        logits(i, 1)
                        fades(i, 1)
                else:
                    pairs(act, fades, NC)

            @block.vector
            def _(dve):
                dve.memset(last[:, :], 0.0).then_inc(carried, 1)
                dve.memset(Hh[:, TS, :], -BIG).then_inc(cp, 1)

                def step(i, b):
                    ch = i * 2 + b
                    first = isinstance(i, int) and i == 0 and b == 0
                    l, v = lg_of(b), val_of(b)
                    dve.wait_ge(cp, ch * 2 + 1)
                    if not first:
                        dve.wait_ge(mstored, ch * 16)
                    dve.tensor_copy(Hh[:, 0, :], Hh[:, TS, :]).then_inc(cp, 1)
                    if one:
                        dve.wait_ge(ls, (ch + 1) * NGR)
                    else:
                        dve.wait_ge(side_in, ch * 16 + 16)
                        dve.wait_ge(rows_in[b], (i + 1) * 16 * TS)
                        dve.tensor_tensor(l, side[:, :, :], l, ALU.subtract).then_inc(ml, 1)
                        dve.wait_ge(ml, ch + 1)
                    dve.wait_ge(cp, ch * 2 + 2)
                    k = neg[:, bass.ds(ch * TS, TS)]
                    for f in range(F):
                        dve.tensor_tensor_scan(Hh[:, 1:TS + 1, f], l[:, :, f], k, Hh[:, 0, f:f + 1],
                                               ALU.max, ALU.add).then_inc(hs, 1)
                    dve.wait_ge(hs, (ch + 1) * F)
                    if not first:
                        dve.wait_ge(summed, ch * 2 * F)
                    dve.tensor_tensor(XB[:, :, :], l, Hh[:, 0:TS, :], ALU.subtract).then_inc(dk, 1)
                    dve.wait_ge(dk, ch + 1)
                    dve.tensor_tensor(Hh[:, 0:TS, :], Hh[:, 0:TS, :], l, ALU.max).then_inc(maxed, 1)
                    if one:
                        dve.wait_ge(rows_in[b], (i + 1) * 16 * TS)
                        dve.tensor_tensor(v, v, l, ALU.add).then_inc(valued, 1)
                    else:
                        dve.tensor_tensor(v, v, side[:, :, :], ALU.add).then_inc(valued, 1)
                    dve.wait_ge(valued, ch + 1)
                    dve.wait_ge(maxed, ch + 1)
                    dve.tensor_copy(lastmax[:, :], Hh[:, TS - 1, :]).then_inc(cp, 1)
                    dve.wait_ge(faded, ch * 2 + 2)
                    dve.tensor_tensor(v, v, PB[:, :, :], ALU.mult).then_inc(ml2, 1)
                    dve.wait_ge(ml2, ch + 1)
                    dve.wait_ge(carried, ch + 1)
                    if not first:
                        dve.wait_ge(sstored, ch * 16)
                    for s_, a in enumerate((PB[:, :, :], v)):
                        for f in range(F):
                            dve.tensor_tensor_scan(DN[:, :, s_ * F + f], XB[:, :, f], a[:, :, f],
                                                   last[:, s_ * F + f:s_ * F + f + 1], ALU.mult, ALU.add).then_inc(summed, 1)
                    dve.wait_ge(summed, (ch + 1) * 2 * F)
                    dve.tensor_copy(last[:, :], DN[:, TS - 1, :]).then_inc(carried, 1)
                pairs(dve, step, NC)

    @phase
    def fix_and_fetch(name, o, src, last, lastmax, node_rows):
        W_ = 2 * F if lastmax is not None else F
        soft = lastmax is not None
        tr, tb, up, fx = sem(f"{name}_T"), sem(f"{name}_carryT"), sem(f"{name}_carry"), sem(f"{name}_first")
        f_in, f_out, n_in = sem(f"{name}_first_in"), sem(f"{name}_first_out"), sem(f"{name}_nodes")
        ex = sem(f"{name}_exps")
        nk = 3 if soft else 1
        with ExitStack() as c, nc.Block() as block:
            pT = [ps(c, f"pT{n}", [F, P]) for n in range(nk)]
            pB = [ps(c, f"pB{n}", [P, F]) for n in range(nk)]
            lT = [alloc(c, f"lT{n}", [F, P]) for n in range(nk)]
            cT = [alloc(c, f"cT{n}", [F, P + 1]) for n in range(nk)]
            nT, dT, eT = (alloc(c, f"xT{n}", [F, P]) for n in range(3))
            cin = alloc(c, "cin", [P, nk * F])
            row, mrow = alloc(c, "row", [P, W_]), alloc(c, "mrow", [P, F])
            M, e1, e2 = (alloc(c, f"e{n}", [P, F]) for n in range(3))
            parts = [lastmax[:, :], last[:, 0:F], last[:, F:2 * F]] if soft else [last[:, :]]

            @block.tensor
            def _(pe):
                for n, part in enumerate(parts):
                    t = pe.transpose(pT[n][:, :], part, ident[:, :])
                t.then_inc(tr, 1)
                pe.wait_ge(tb, 1)
                for n in range(nk):
                    t = pe.transpose(pB[n][:, :], cT[n][:, 0:P], ident[0:F, 0:F])
                t.then_inc(up, 1)

            @block.scalar
            def _(act):
                if soft:
                    link = linker(act, "act")
                    for k in (1, 3):
                        act.wait_ge(ex, k)
                        a, b_ = (dT, eT) if k == 1 else (e1, e2)
                        link(act.activation(a[:, :], a[:, :], ACT.Exp))
                        link(act.activation(b_[:, :], b_[:, :], ACT.Exp))
                        act.sem_inc(ex, 1)

            @block.vector
            def _(dve):
                link = linker(dve, "dve")
                dve.wait_ge(tr, 1)
                for n in range(nk):
                    link(dve.tensor_copy(lT[n][:, :], pT[n][:, :]))
                    link(dve.memset(cT[n][:, :], -BIG if soft and n == 0 else 0.0))
                if soft:
                    link(dve.tensor_scalar(nT[:, :], aT[o][:, :], 1.0, BIG, ALU.subtract, ALU.mult))
                    link(dve.tensor_tensor_scan(cT[0][:, 1:P + 1], nT[:, :], lT[0][:, :], -BIG, ALU.add, ALU.max))
                    link(dve.tensor_tensor(dT[:, :], cT[0][:, 0:P], cT[0][:, 1:P + 1], ALU.subtract))
                    link(dve.tensor_scalar(dT[:, :], dT[:, :], 0.0, None, ALU.min))
                    link(dve.tensor_tensor(eT[:, :], lT[0][:, :], cT[0][:, 1:P + 1], ALU.subtract))
                    dve.sem_inc(ex, 1)
                    dve.wait_ge(ex, 2)
                    link(dve.tensor_tensor(dT[:, :], dT[:, :], aT[o][:, :], ALU.mult))
                    for n in (1, 2):
                        link(dve.tensor_tensor(lT[n][:, :], lT[n][:, :], eT[:, :], ALU.mult))
                        link(dve.tensor_tensor_scan(cT[n][:, 1:P + 1], dT[:, :], lT[n][:, :], 0.0, ALU.mult, ALU.add))
                else:
                    link(dve.tensor_tensor_scan(cT[0][:, 1:P + 1], aT[o][:, :], lT[0][:, :], 0.0, ALU.mult, ALU.add))
                dve.sem_inc(tb, 1)
                dve.wait_ge(up, 1)
                for n in range(nk):
                    link(dve.tensor_copy(cin[:, n * F:(n + 1) * F], pB[n][:, :]))
                dve.wait_ge(f_in, (2 if soft else 1) * 16)
                if soft:
                    link(dve.tensor_scalar(cin[:, 0:3 * F], cin[:, 0:3 * F], fk[o][:, 0:1], None, ALU.mult))
                    link(dve.tensor_scalar(M[:, 0:1], fk[o][:, 0:1], 1.0, BIG, ALU.subtract, ALU.mult))
                    link(dve.tensor_scalar(e1[:, :], cin[:, 0:F], M[:, 0:1], None, ALU.add))
                    link(dve.tensor_tensor(M[:, :], e1[:, :], mrow[:, :], ALU.max))
                    link(dve.tensor_tensor(e1[:, :], e1[:, :], M[:, :], ALU.subtract))
                    link(dve.tensor_tensor(e2[:, :], mrow[:, :], M[:, :], ALU.subtract))
                    dve.sem_inc(ex, 1)
                    dve.wait_ge(ex, 4)
                    for n in range(2):
                        a, b_ = row[:, n * F:(n + 1) * F], cin[:, (n + 1) * F:(n + 2) * F]
                        link(dve.tensor_tensor(a, a, e2[:, :], ALU.mult))
                        link(dve.tensor_tensor(b_, b_, e1[:, :], ALU.mult))
                        link(dve.tensor_tensor(a, a, b_, ALU.add))
                else:
                    link(dve.scalar_tensor_tensor(row[:, :], cin[:, :], fk[o][:, 0:1], row[:, :], ALU.mult, ALU.add))
                dve.sem_inc(fx, 1)

            @block.gpsimd
            def _(pool):
                link = linker(pool, "pool")
                link(pool.memset(row[:, :], 0.0))
                link(pool.memset(mrow[:, :], 0.0))
                off = lambda: bass.IndirectOffsetOnAxis(ap=end0[o][:, 0:1], axis=0)
                pool.indirect_dma_start(row[:, :], None, src[0:EP, :], off(), bounds_check=EP - 1, oob_is_err=False).then_inc(f_in, 16)
                if soft:
                    pool.indirect_dma_start(mrow[:, :], None, maxes, off(), bounds_check=EP - 1, oob_is_err=False).then_inc(f_in, 16)
                pool.wait_ge(fx, 1)
                pool.indirect_dma_start(src[0:EP, :], off(), row[:, :], None, bounds_check=EP - 1, oob_is_err=False).then_inc(f_out, 16)
                pool.wait_ge(f_out, 16)
                for j in range(NJ):
                    pool.indirect_dma_start(node_rows[:, j, 0:W_], None, src,
                                            bass.IndirectOffsetOnAxis(ap=endp[o][:, j:j + 1], axis=0)).then_inc(n_in, 16)
                pool.wait_ge(n_in, 16 * NJ)

    pj = [Counter(lasting(n)) for n in ("proj_in", "proj_T", "proj_lhs", "proj_out", "proj_stored")]

    def project(src, weight, dst):
        s_in, s_T, s_l, s_o, s_d = pj
        B = [s.base for s in pj]
        with ExitStack() as c, nc.Block() as block:
            xin, xT = alloc(c, "xin", [P, G, F]), alloc(c, "xT", [P, G // 2, P])
            pT, pO = ps(c, "pTp", [P, 8, P]), ps(c, "pOp", [P, 8, P])
            H = G // 2

            @block.vector
            def _(dve):
                with dve.Fori(0, NG) as i:
                    dve.wait_ge(s_o.sem, i + B[3])
                    dve.tensor_copy(xin[:, :, :], src[:, bass.ds(i * G, G), :]).then_inc(s_in.sem, 1)
                    dve.wait_ge(s_o.sem, i + B[3] + 1)
                    dve.tensor_copy(dst[:, bass.ds(i * G, G), :],
                                    pO[:, 0:H, :].rearrange("p h (a f) -> p (h a) f", f=F)).then_inc(s_d.sem, 1)

            @block.tensor
            def _(pe):
                with pe.Fori(0, NG) as i:
                    pe.wait_ge(s_in.sem, i + B[0] + 1)
                    for h in range(H):
                        t = pe.transpose(pT[:, h, :], xin[:, 2 * h:2 * h + 2, :].rearrange("p a f -> p (a f)"), ident[:, :])
                    t.then_inc(s_T.sem, 1)
                    pe.wait_ge(s_l.sem, i + B[2] + 1)
                    pe.wait_ge(s_d.sem, i + B[4])
                    for h in range(H):
                        t = pe.matmul(pO[:, h, :], xT[:, h, :], weight[:, :], start=True, stop=True)
                    t.then_inc(s_o.sem, 1)

            @block.scalar
            def _(act):
                with act.Fori(0, NG) as i:
                    act.wait_ge(s_T.sem, i + B[1] + 1)
                    act.activation(xT[:, :, :], pT[:, 0:H, :], ACT.Copy).then_inc(s_l.sem, 1)
        for s in pj:
            s.base += NG

    def bias_tile(c, n, vec):
        t = alloc(c, f"bias_{n}", [P, F])
        return t, vec.rearrange("(a n) -> a n", a=1).to_broadcast([P, F])

    def bc(t):
        return t[:, :].unsqueeze(1).to_broadcast([P, NJ, F])

    def pc(t):
        return t.unsqueeze(2).to_broadcast([P, NJ, F])

    nd = {n: lasting(n) for n in ("vec_in", "table_out")}
    ndb = {"vec_in": 0, "table_out": 0}

    def nodes(dve_work, vectors=(), tables=(), act_work=None):
        done = Counter_done
        with ExitStack() as c, nc.Block() as block:
            vt = [alloc(c, f"vec{n}", [P, F]) for n in range(len(vectors))]
            tmp = alloc(c, "tmp_n", [P, NJ, F])
            small = [alloc(c, f"small{n}", [P, NJ]) for n in range(3)]
            b_in, b_out, b_done = ndb["vec_in"], ndb["table_out"], done.base

            @block.sync
            def _(sp):
                for t, v in zip(vt, vectors):
                    sp.dma_start(t[:, :], v.rearrange("(a n) -> a n", a=1).to_broadcast([P, F])).then_inc(nd["vec_in"], 16)
                if tables:
                    sp.wait_ge(done.sem, b_done + 1)
                    for dst, s in tables:
                        sp.dma_start(dst.rearrange("(p j) f -> p j f", p=P), s).then_inc(nd["table_out"], 16)
                    sp.wait_ge(nd["table_out"], b_out + 16 * len(tables))

            @block.vector
            def _(dve):
                if vectors:
                    dve.wait_ge(nd["vec_in"], b_in + 16 * len(vectors))
                dve_work(dve, linker(dve, "dve"), vt, tmp, small)
                dve.sem_inc(done.sem, 1)

            @block.scalar
            def _(act):
                for t in pending:
                    act.wait_ge(root_in.sem, root_in.base)
                    act.activation(t[:, :], t[:, :], ACT.Sqrt).then_inc(root_out.sem, 1)
                pending.clear()
            ndb["vec_in"] += 16 * len(vectors)
            ndb["table_out"] += 16 * len(tables)
            done.base += 1
    root_in, root_out = Counter(lasting("root_in")), Counter(lasting("root_out"))

    def roots(dve, t):
        root_in.base += 1
        root_out.base += 1
        pending.append(t)
        dve.sem_inc(root_in.sem, 1)
        dve.wait_ge(root_out.sem, root_out.base)
    pending = []

    Counter_done = Counter(lasting("nodes_done"))

    def layernorm(dve, link, x, tmp, small):
        mean, var = small[0], small[1]
        link(dve.reduce_sum(mean[:, :], x[:, :, :], axis=AX.X))
        link(dve.tensor_scalar(mean[:, :], mean[:, :], 1.0 / F, None, ALU.mult))
        link(dve.tensor_tensor(x[:, :, :], x[:, :, :], pc(mean[:, :]), ALU.subtract))
        link(dve.tensor_tensor(tmp[:, :, :], x[:, :, :], x[:, :, :], ALU.mult))
        link(dve.reduce_sum(var[:, :], tmp[:, :, :], axis=AX.X))
        link(dve.tensor_scalar(var[:, :], var[:, :], 1.0 / F, EPS, ALU.mult, ALU.add))
        roots(dve, var)
        link(dve.reciprocal(var[:, :], var[:, :]))
        link(dve.tensor_tensor(x[:, :, :], x[:, :, :], pc(var[:, :]), ALU.mult))

    @phase
    def similarity_pass(last):
        W_ = F + 1
        S = lambda n: [sem(f"L2_{n}{b}") for b in range(2)]
        q = lambda n: sem(f"L2_{n}")
        idx_in, rows_in, side_in = S("idx"), S("rows"), S("side")
        go, filled, prod, steps, msg, scanned, carried, stored = (q(n) for n in (
            "go", "filled", "prod", "steps", "msg", "scanned", "carried", "stored"))
        with ExitStack() as c, nc.Block() as block:
            idx = [alloc(c, f"idx{b}", [P, T], I32) for b in range(2)]
            rows = [alloc(c, f"rows{b}", [P, T, W_]) for b in range(2)]
            own = [alloc(c, f"own{b}", [P, T, W_]) for b in range(2)]
            base = [alloc(c, f"base{b}", [P, T]) for b in range(2)]
            tmp = alloc(c, "tmp", [P, T, F])
            lastu = alloc(c, "lastu", [P, W_])
            dot, nn, a, b2 = (alloc(c, f"s{n}", [P, T]) for n in range(4))

            @block.sync
            def _(sp):
                def step(i, b):
                    ch = i * 2 + b
                    if not isinstance(i, int) or i:
                        sp.wait_ge(rows_in[b], i * 16 * T)
                        sp.wait_ge(msg, ch - 1)
                    sp.dma_start(idx[b][:, :], cols(sdst, ch)).then_inc(idx_in[b], 16)
                    sp.dma_start(own[b][:, :, :], cols(spread, ch)).then_inc(side_in[b], 16)
                    sp.dma_start(base[b][:, :], cols(sbase, ch)).then_inc(side_in[b], 16)
                    if not isinstance(i, int) or i or b:
                        store(ch - 1)

                def store(ch):
                    sp.wait_ge(scanned, (ch + 1) * F)
                    sp.dma_start(cols(sums[0:EP, :], ch), tmp[:, :, :]).then_inc(stored, 16)
                pairs(sp, step)
                store(NCH - 1)
                sp.wait_ge(stored, NCH * 16)

            @block.gpsimd
            def _(pool):
                gathers(pool, tab65, idx, rows, idx_in, rows_in, lambda e, i, b: e.wait_ge(msg, i * 2 + b - 1), go, T, NCH)

            @block.vector
            def _(dve):
                dve.memset(last[:, :], 0.0).then_inc(carried, 1)
                dve.memset(lastu[:, :], 0.0).then_inc(carried, 1)
                NS = 10

                def step(i, b):
                    ch = i * 2 + b
                    first = isinstance(i, int) and i == 0 and b == 0
                    k = keep["s"][:, bass.ds(ch * T, T)]
                    dve.wait_ge(side_in[b], (i + 1) * 32)
                    dve.wait_ge(carried, ch * 2 + 2)
                    u, g = own[b], rows[b]
                    for f in range(W_):
                        dve.tensor_tensor_scan(u[:, :, f], k, u[:, :, f], lastu[:, f:f + 1], ALU.mult, ALU.add).then_inc(filled, 1)
                    dve.wait_ge(filled, (ch + 1) * W_)
                    dve.tensor_copy(lastu[:, :], u[:, T - 1, :]).then_inc(carried, 1)
                    dve.wait_ge(rows_in[b], (i + 1) * 16 * T)
                    if not first:
                        dve.wait_ge(stored, ch * 16)
                    n = [0]

                    def link(ins):
                        n[0] += 1
                        ins.then_inc(steps, 1)
                        dve.wait_ge(steps, ch * NS + n[0])
                    link(dve.tensor_tensor(tmp[:, :, :], u[:, :, 0:F], g[:, :, 0:F], ALU.mult))
                    link(dve.reduce_sum(dot[:, :], tmp[:, :, :], axis=AX.X))
                    link(dve.tensor_tensor(nn[:, :], u[:, :, F], g[:, :, F], ALU.mult))
                    link(dve.tensor_scalar(nn[:, :], nn[:, :], 1e-8, None, ALU.max))
                    link(dve.reciprocal(a[:, :], nn[:, :]))
                    link(dve.tensor_tensor(dot[:, :], dot[:, :], a[:, :], ALU.mult))
                    link(dve.tensor_scalar(a[:, :], dot[:, :], 0.0, co[:, 4:5], ALU.max, ALU.mult))
                    link(dve.tensor_scalar(b2[:, :], dot[:, :], 0.0, co[:, 5:6], ALU.min, ALU.mult))
                    link(dve.tensor_tensor(a[:, :], a[:, :], b2[:, :], ALU.add))
                    link(dve.tensor_tensor(a[:, :], a[:, :], base[b][:, :], ALU.mult))
                    dve.tensor_tensor(tmp[:, :, :], g[:, :, 0:F], a[:, :].unsqueeze(2).to_broadcast([P, T, F]), ALU.mult).then_inc(msg, 1)
                    dve.wait_ge(msg, ch + 1)
                    for f in range(F):
                        dve.tensor_tensor_scan(tmp[:, :, f], k, tmp[:, :, f], last[:, f:f + 1], ALU.mult, ALU.add).then_inc(scanned, 1)
                    dve.wait_ge(scanned, (ch + 1) * F)
                    dve.tensor_copy(last[:, :], tmp[:, T - 1, :]).then_inc(carried, 1)
                pairs(dve, step)

    @phase
    def spread_rows(wh):
        sc, kin, fin, fst = sem("spread_nodes"), sem("spread_key"), sem("spread_first_in"), sem("spread_first")
        with ExitStack() as c, nc.Block() as block:
            key0 = alloc(c, "key0", [P, 2], I32)
            row = alloc(c, "row0", [P, F + 1])

            @block.sync
            def _(sp):
                sp.dma_start(key0[:, :], skey[1:EP + 1].rearrange("(p t) -> p t", p=P)[:, 0:2]).then_inc(kin, 16)
                sp.wait_ge(fin, 16)
                sp.wait_ge(sc, 16 * NJ)
                sp.dma_start(spread.rearrange("(p t) f -> p t f", p=P)[:, 0, :], row[:, :]).then_inc(fst, 16)
                sp.wait_ge(fst, 16)

            @block.gpsimd
            def _(pool):
                pool.wait_ge(kin, 16)
                pool.indirect_dma_start(row[:, :], None, tab65, bass.IndirectOffsetOnAxis(ap=key0[:, 0:1], axis=0)).then_inc(fin, 16)
                for j in range(NJ):
                    pool.indirect_dma_start(spread, bass.IndirectOffsetOnAxis(ap=startp[:, j:j + 1], axis=0),
                                            wh[:, j, :], None, bounds_check=EP - 1, oob_is_err=False).then_inc(sc, 16)
                pool.wait_ge(sc, 16 * NJ)

    @phase
    def zero_scratch():
        z, zd = sem("zeros"), sem("zeroed")
        with ExitStack() as c, nc.Block() as block:
            zt = alloc(c, "zt", [P, 2 * T, F + 1])

            @block.vector
            def _(dve):
                dve.memset(zt[:, :, :], 0.0).then_inc(z, 1)

            @block.sync
            def _(sp):
                sp.wait_ge(z, 1)
                with sp.Fori(0, NCH // 2) as i:
                    sp.dma_start(cols(spread, i, 2 * T), zt[:, :, :]).then_inc(zd, 16)
                sp.dma_start(sums[EP:ROWS, :], zt[0:1, 0, 0:F]).then_inc(zd, 16)
                sp.dma_start(sums2[EP:ROWS, :], zt[0:1, 0:2, 0:F]).then_inc(zd, 16)
                sp.wait_ge(zd, 16 * (NCH // 2 + 2))

    @phase
    def distance_weights():
        ld, ce, st, rd = sem("dw_loaded"), sem("dw_centred"), sem("dw_stored"), sem("dw_back")
        centred = dram("centred", [5, F])
        with ExitStack() as c, nc.Block() as block:
            w = alloc(c, "w5", [5, F])
            m = alloc(c, "m5", [5, 1])
            zs = sem("dw_zeroed")

            @block.sync
            def _(sp):
                sp.dma_start(w[0:3, :], W["L3_gnn_Wd1"]).then_inc(ld, 16)
                sp.dma_start(w[3:4, :], W["L3_gnn_bd1"].rearrange("(a n) -> a n", a=1)).then_inc(ld, 16)
                sp.dma_start(w[4:5, :], W["L3_gnn_bd2"].rearrange("(a n) -> a n", a=1)).then_inc(ld, 16)
                for n in ("g1", "b1", "g2", "b2"):
                    sp.dma_start(dist_v[n][:, :], W[f"L3_gnn_{n}"].rearrange("(a n) -> a n", a=1).to_broadcast([P, F])).then_inc(ld, 16)
                sp.wait_ge(ce, 1)
                sp.dma_start(centred, w[:, :]).then_inc(st, 16)
                sp.wait_ge(st, 16)
                sp.wait_ge(zs, 2)
                for t in range(DW):
                    sp.dma_start(dist_w[3 * t:3 * t + 3, t * F:(t + 1) * F], centred[0:3, :]).then_inc(rd, 16)
                    sp.dma_start(dist_w[F:F + 1, t * F:(t + 1) * F], centred[3:4, :]).then_inc(rd, 16)
                for t in range(8):
                    sp.dma_start(dist_b2[:, t * F:(t + 1) * F], centred[4:5, :]).then_inc(rd, 16)
                sp.wait_ge(rd, 16 * (2 * DW + 8))

            @block.vector
            def _(dve):
                link = linker(dve, "dve")
                dve.memset(dist_w[:, :], 0.0).then_inc(zs, 1)
                dve.memset(ones_row[:, :], 1.0).then_inc(zs, 1)
                dve.sem_inc(pj[3].sem, 1)
                dve.sem_inc(pj[4].sem, 1)
                pj[3].base = pj[4].base = 1
                dve.wait_ge(ld, 16 * 7)
                link(dve.reduce_sum(m[:, :], w[:, :], axis=AX.X))
                link(dve.tensor_scalar(m[:, :], m[:, :], 1.0 / F, None, ALU.mult))
                link(dve.tensor_scalar(w[:, :], w[:, :], m[:, 0:1], None, ALU.subtract))
                dve.sem_inc(ce, 1)

    constants()
    distance_weights()
    zero_scratch()
    edge_weights()
    masks("d", dst_in)

    with ExitStack() as c:
        A = alloc(c, "A", [P, NJ, F])
        project(X, bd["a1"], A)
        nodes(lambda dve, link, v, tmp, small: None, tables=[(tab, A[:, :, :])])
    quarter = 0
    for conv, (bias, nxt) in enumerate((("L0_gnn_b1", "a2"), ("L0_gnn_b2", None))):
        for o, keys in (("d", src_in), ("s", sdst)):
            with ExitStack() as c:
                last = alloc(c, "last", [P, F])
                first_pass = quarter == 0
                if first_pass:
                    hist = {k: alloc(c, f"hist_{k}", [P, P]) for k in "ds"}
                    first_row = alloc(c, "first_row", [P, P])
                sum_pass(f"conv{conv}{o}", o, keys, tab, last, quarter, hist if first_pass else None)
                quarter += 1
                if first_pass:
                    pointers(hist, first_row)
                with ExitStack() as cc:
                    R = alloc(cc, "node_rows", [P, NJ, F])
                    fix_and_fetch(f"conv{conv}{o}", o, sums, last, None, R)
                    if o == "d":
                        nodes(lambda dve, link, v, tmp, small:
                              link(dve.tensor_tensor(R[:, :, :], R[:, :, :], pc(inv["d"][:, :]), ALU.mult)), tables=[(tab, R[:, :, :])])
                    else:
                        def finish(dve, link, v, tmp, small):
                            link(dve.tensor_tensor(R[:, :, :], R[:, :, :], pc(inv["s"][:, :]), ALU.mult))
                            link(dve.tensor_tensor(R[:, :, :], R[:, :, :], bc(v[0]), ALU.add))
                            if conv == 0:
                                link(dve.tensor_scalar(R[:, :, :], R[:, :, :], 0.0, None, ALU.max))
                            else:
                                link(dve.tensor_tensor(X[:, :, :], X[:, :, :], R[:, :, :], ALU.add))
                                layernorm(dve, link, X, tmp, small)
                        nodes(finish, vectors=[W[bias]])
                        if nxt:
                            A = alloc(cc, "A", [P, NJ, F])
                            project(R, bd[nxt], A)
                            nodes(lambda dve, link, v, tmp, small: None, tables=[(tab, A[:, :, :])])
                if first_pass:
                    sort_edges(first_row)
                    unpack_sorted()
                    masks("s", skey)

    with ExitStack() as c:
        A = alloc(c, "A", [P, NJ, F])
        project(X, bd["fc"], A)
        nodes(lambda dve, link, v, tmp, small: None, tables=[(tab, A[:, :, :])])
    with ExitStack() as c:
        last, lastmax = alloc(c, "last", [P, 2 * F]), alloc(c, "lastmax", [P, F])
        softmax_pass("L1", src_in, tab, last, lastmax)
        R = alloc(c, "node_rows", [P, NJ, 2 * F])
        fix_and_fetch("L1", "d", sums2, last, lastmax, R)
        Hn = alloc(c, "Hn", [P, NJ, F])
        B_ = R[:, :, 0:F]
        num = R[:, :, F:2 * F]

        def attend(dve, link, v, tmp, small):
            link(dve.tensor_scalar(B_, B_, 1e-30, None, ALU.max))
            link(dve.reciprocal(tmp[:, :, :], B_))
            link(dve.tensor_tensor(num, num, tmp[:, :, :], ALU.mult))
        nodes(attend)
        project(X, bd["fc"], Hn)
        L_ = R[:, :, 0:F]
        project(Hn, bd["loop"], L_)

        def merge(dve, link, v, tmp, small):
            has = small[2]
            link(dve.tensor_scalar(has[:, :], inv["d"][:, :], 0.0, None, ALU.is_gt))
            link(dve.tensor_tensor(num, num, L_, ALU.add))
            link(dve.tensor_tensor(num, num, pc(has[:, :]), ALU.mult))
            link(dve.tensor_scalar(has[:, :], has[:, :], -1.0, 1.0, ALU.mult, ALU.add))
            link(dve.tensor_tensor(Hn[:, :, :], Hn[:, :, :], pc(has[:, :]), ALU.mult))
            link(dve.tensor_tensor(num, num, Hn[:, :, :], ALU.add))
            link(dve.tensor_scalar(num, num, 0.0, None, ALU.max))
            link(dve.tensor_tensor(X[:, :, :], X[:, :, :], num, ALU.add))
            layernorm(dve, link, X, tmp, small)
        nodes(merge)

    with ExitStack() as c:
        WH = alloc(c, "WH", [P, NJ, F + 1])
        project(X, bd["w2l"], WH[:, :, 0:F])

        def norms(dve, link, v, tmp, small):
            wh = WH[:, :, 0:F]
            link(dve.tensor_tensor(wh, wh, bc(v[0]), ALU.add))
            link(dve.tensor_tensor(tmp[:, :, :], wh, wh, ALU.mult))
            link(dve.reduce_sum(small[0][:, :], tmp[:, :, :], axis=AX.X))
            roots(dve, small[0])
            link(dve.tensor_copy(WH[:, :, F], small[0][:, :]))
        nodes(norms, vectors=[W["L2_gnn_b"]], tables=[(tab65, WH[:, :, :])])
        spread_rows(WH)
    with ExitStack() as c:
        last = alloc(c, "last", [P, F])
        similarity_pass(last)
        R = alloc(c, "node_rows", [P, NJ, F])
        fix_and_fetch("L2", "s", sums, last, None, R)
        A = alloc(c, "A", [P, NJ, F])
        project(X, bd["w2l"], A)

        def propagate(dve, link, v, tmp, small):
            link(dve.tensor_tensor(A[:, :, :], A[:, :, :], bc(v[0]), ALU.add))
            link(dve.tensor_scalar(A[:, :, :], A[:, :, :], co[:, 6:7], None, ALU.mult))
            link(dve.tensor_tensor(R[:, :, :], R[:, :, :], A[:, :, :], ALU.add))
            link(dve.tensor_tensor(X[:, :, :], X[:, :, :], R[:, :, :], ALU.add))
            layernorm(dve, link, X, tmp, small)
        nodes(propagate, vectors=[W["L2_gnn_b"]])

    with ExitStack() as c:
        Q = alloc(c, "Q", [P, NJ, 2 * F])
        project(X, bd["q2"], Q[:, :, 0:F])
        project(X, bd["q3"], Q[:, :, F:2 * F])
        nodes(lambda dve, link, v, tmp, small: None, tables=[(tab128, Q[:, :, :])])
    with ExitStack() as c:
        last, lastmax = alloc(c, "last", [P, 2 * F]), alloc(c, "lastmax", [P, F])
        softmax_pass("L3", src_in, tab128, last, lastmax)
        R = alloc(c, "node_rows", [P, NJ, 2 * F])
        fix_and_fetch("L3", "d", sums2, last, lastmax, R)
        B_ = R[:, :, 0:F]
        num = R[:, :, F:2 * F]

        def final(dve, link, v, tmp, small):
            link(dve.tensor_scalar(B_, B_, 1e-30, None, ALU.max))
            link(dve.reciprocal(tmp[:, :, :], B_))
            link(dve.tensor_tensor(num, num, tmp[:, :, :], ALU.mult))
            link(dve.tensor_tensor(X[:, :, :], X[:, :, :], num, ALU.add))
            layernorm(dve, link, X, tmp, small)
        nodes(final, tables=[(out, X[:, :, :])])
    top.close()


_WEIGHTS = ["L0_gnn_W1", "L0_gnn_b1", "L0_gnn_W2", "L0_gnn_b2", "L1_gnn_W_fc", "L1_gnn_W_fcr", "L1_gnn_loop_W",
            "L2_gnn_W", "L2_gnn_b", "L2_gnn_deg_coeff", "L2_gnn_coeff_param", "L2_gnn_scale_param",
            "L3_gnn_Wd1", "L3_gnn_bd1", "L3_gnn_g1", "L3_gnn_b1", "L3_gnn_Wd2", "L3_gnn_bd2", "L3_gnn_g2", "L3_gnn_b2",
            "L3_gnn_W1", "L3_gnn_W2", "L3_gnn_W3"]


def kernel(**inputs):
    import numpy as _np
    import concourse.bacc as _bacc
    from concourse import mybir as _mybir
    from concourse.bass_utils import run_bass_kernel_spmd as _run

    def padded(a, n, value=0, before=0):
        a = _np.asarray(a)
        o = _np.full((n,) + a.shape[1:], value, a.dtype)
        o[before:before + a.shape[0]] = a
        return o

    arrays = {
        "x": padded(inputs["x"], NP),
        "src": padded(inputs["src"], EP, N),
        "dst": _np.concatenate([_np.full(1, -1, _np.int32), padded(inputs["dst"], EP, N), _np.full(1, -1, _np.int32)]),
        "attr3": padded(inputs["edge_attr_3"], EP),
        "attr64": padded(inputs["edge_attr_64"], EP),
        "w": padded(inputs["edge_weight"], EP),
        "w2": padded(inputs["edge_weight_n2"], EP),
    }
    for name in _WEIGHTS:
        arrays[name] = _np.ascontiguousarray(inputs[name])
    nc = _bacc.Bacc("TRN2", target_bir_lowering=False, num_devices=1)
    arrays = {f"in_{k}": _np.ascontiguousarray(v) for k, v in arrays.items()}
    ap = {k: nc.dram_tensor(k, v.shape, _mybir.dt.from_np(v.dtype), kind="ExternalInput").ap() for k, v in arrays.items()}
    out = nc.dram_tensor("out_0", (NP, F), _mybir.dt.float32, kind="ExternalOutput").ap()
    gnn_resnorm(nc, ap["in_x"], ap["in_src"], ap["in_dst"], ap["in_attr3"], ap["in_attr64"], ap["in_w"], ap["in_w2"],
                {n: ap[f"in_{n}"] for n in _WEIGHTS}, out)
    r = _run(nc, [arrays], core_ids=[0])
    return r.results[0]["out_0"][:N]
```

```python
import concourse.bass as bass
from concourse import mybir
from contextlib import ExitStack

F32 = mybir.dt.float32
I32 = mybir.dt.int32
BF16 = mybir.dt.bfloat16
ALU = mybir.AluOpType
ACT = mybir.ActivationFunctionType
AX = mybir.AxisListType

P = 128
F = 64
N = 12500
E = 212500
NJ = -(-(N + 1) // P)
NP = NJ * P
HI = NJ
T = 64
NT = -(-E // (P * 2 * T)) * 2 * T
NCH = NT // T
EP = P * NT
ROWS = EP + 1
BIG = 1.0e38
NOROW = float(1 << 21)
EPS = 1e-5
G = 14
NG = NJ // G


def gnn_resnorm(nc, x_in, src_0, dst_0, attr3_0, attr64_0, w_0, w2_0, W, out):
    top = ExitStack()

    unique = [0]

    def alloc(ctx, name, shape, dt=F32):
        unique[0] += 1
        return ctx.enter_context(nc.sbuf_tensor(f"{name}_{unique[0]}", shape, dt))

    def ps(ctx, name, shape, dt=F32):
        unique[0] += 1
        return ctx.enter_context(nc.psum_tensor(f"{name}_{unique[0]}", shape, dt))

    phase_sems = []

    def sem(name):
        unique[0] += 1
        phase_sems.append(nc.alloc_semaphore(name=f"{name}_{unique[0]}"))
        return phase_sems[-1]

    def phase(build):
        def run(*args, **kw):
            build(*args, **kw)
            nc.clear_and_free_semaphores(list(phase_sems))
            phase_sems.clear()
            nc.all_engine_barrier()
        return run

    def dram(name, shape, dt=F32):
        return nc.dram_tensor(name, shape, dt).ap()

    src_in, dst_in = dram("src_d", [EP], I32), dram("dst_d", [EP + 2], I32)
    attr3_in, attr64_s = dram("attr3_d", [EP, 3]), dram("attr64_d", [EP, F])
    w_in, w2_in = dram("w_d", [EP]), dram("w2_d", [EP])
    number, perm = dram("number", [EP], I32), dram("perm", [EP], I32)

    tab = dram("tab", [NP, F])
    tab65 = dram("tab65", [NP, F + 1])
    tab128 = dram("tab128", [NP, 2 * F])
    sums = dram("sums", [ROWS, F])
    sums2 = dram("sums2", [ROWS, 2 * F])
    maxes = dram("maxes", [EP, F])
    dists = dram("dists", [EP, F])
    spread = dram("spread", [EP, F + 1])
    rec = dram("rec", [EP, 3], I32)
    base_in = dram("base", [EP])
    skey = dram("skey", [EP + 2], I32)
    sdst = dram("sdst", [EP], I32)
    sbase = dram("sbase", [EP])
    flat = {n: dram(n, [NP], I32) for n in ("end_d", "end_s", "start_s")}
    flatf = {n: dram(n, [NP]) for n in ("cnt_d", "cnt_s")}

    def cols(ap, c, w=T, first=0):
        if len(ap.shape) == 1:
            return ap.rearrange("(p t) -> p t", p=P)[:, bass.ds(c * w + first, w)]
        return ap.rearrange("(p t) f -> p t f", p=P)[:, bass.ds(c * w + first, w), :]

    X = alloc(top, "X", [P, NJ, F])
    ident = alloc(top, "ident", [P, P])
    keep = {o: alloc(top, f"keep_{o}", [P, NT]) for o in "ds"}
    neg = alloc(top, "neg_d", [P, NT])
    fk = {o: alloc(top, f"fk_{o}", [P, 1]) for o in "ds"}
    aT = {o: alloc(top, f"aT_{o}", [F, P]) for o in "ds"}
    end0 = {o: alloc(top, f"end0_{o}", [P, 1], I32) for o in "ds"}
    endp = {o: alloc(top, f"endp_{o}", [P, NJ], I32) for o in "ds"}
    startp = alloc(top, "startp", [P, NJ], I32)
    inv = {o: alloc(top, f"inv_{o}", [P, NJ]) for o in "ds"}
    co = alloc(top, "co", [P, 16])
    sorted_p = alloc(top, "sorted_p", [1, 1], I32)
    bd = {n: alloc(top, f"bd_{n}", [P, P]) for n in ("a1", "a2", "fc", "fcr", "loop", "w2l", "d2", "q2", "q3")}

    def linker(eng, which):
        done, count = sem(f"chain_{which}"), [0]

        def link(ins):
            count[0] += 1
            ins.then_inc(done, 1)
            eng.wait_ge(done, count[0])
        return link

    @phase
    def constants():
        loaded, made = sem("w_loaded"), sem("ident_made")
        zeroed = sem("bd_zeroed")
        copied, keys_in, ordered, counted = sem("edges_copied"), sem("keys_in"), sem("order_seen"), sem("order_counted")
        tr_ready, tr_done = sem("wt_ready"), sem("wt_done")
        order = {"a1": "L0_gnn_W1", "a2": "L0_gnn_W2", "fc": "L1_gnn_W_fc", "fcr": "L1_gnn_W_fcr",
                 "loop": "L1_gnn_loop_W", "w2l": "L2_gnn_W", "d2": "L3_gnn_Wd2",
                 "q2": "L3_gnn_W2", "q3": "L3_gnn_W3"}
        with ExitStack() as c, nc.Block() as block:
            tp = ps(c, "wt_ps", [P, P])
            mean = alloc(c, "mean_d2", [P, 1])
            st = alloc(c, "soft", [P, 8])
            key, key_next = alloc(c, "key", [P, NT], I32), alloc(c, "key_next", [P, NT], I32)
            rising, all_rise, ones = alloc(c, "rising", [P, NT]), alloc(c, "all_rise", [P, 1]), alloc(c, "ones_o", [P, 1])
            po = ps(c, "order_ps", [1, 1])

            @block.gpsimd
            def _(pool):
                pool.memset(ident[:, :], 0.0).then_inc(made, 1)
                pool.wait_ge(made, 1)
                pool.affine_select(out=ident[:, :], in_=ident[:, :], compare_op=ALU.not_equal, fill=1.0, base=0,
                                   pattern=[[-1, P]], channel_multiplier=1).then_inc(made, 1)

            @block.sync
            def _(sp):
                for n, t in enumerate((key, key_next)):
                    sp.dma_start(t[:, :], dst_0[n:n + EP].rearrange("(p t) -> p t", p=P)).then_inc(keys_in, 16)
                sp.wait_ge(zeroed, len(order) + 1)
                for n, full in order.items():
                    for h in (0, F):
                        sp.dma_start(bd[n][h:h + F, h:h + F], W[full]).then_inc(loaded, 16)
                sp.dma_start(X[:, :, :], x_in.rearrange("(p j) f -> p j f", p=P)).then_inc(loaded, 16)
                for k, (n, w) in enumerate((("L2_gnn_deg_coeff", 2), ("L2_gnn_coeff_param", 3), ("L2_gnn_scale_param", 1))):
                    v = W[n].rearrange("(a n) -> a n", a=1).to_broadcast([P, w])
                    sp.dma_start(co[:, 4 * k:4 * k + w], v).then_inc(loaded, 16)

            @block.vector
            def _(dve):
                link = linker(dve, "dve")
                for n in order:
                    dve.memset(bd[n][:, :], 0.0).then_inc(zeroed, 1)
                dve.memset(co[:, :], 0.0).then_inc(zeroed, 1)
                link(dve.memset(ones[:, :], 1.0))
                dve.wait_ge(keys_in, 32)
                link(dve.tensor_tensor(rising[:, :], key[:, :], key_next[:, :], ALU.is_le))
                link(dve.tensor_reduce(out=all_rise[:, :], in_=rising[:, :], op=ALU.min, axis=AX.X))
                dve.sem_inc(ordered, 1)
                dve.wait_ge(counted, 1)
                link(dve.tensor_copy(sorted_p[:, :], po[:, :]))
                dve.wait_ge(loaded, 16 * (2 * len(order) + 4))
                for k, n in enumerate(("fc", "fcr")):
                    dve.wait_ge(tr_ready, k + 1)
                    dve.tensor_copy(bd[n][:, :], tp[:, :]).then_inc(tr_done, 1)
                link(dve.reduce_sum(mean[:, :], bd["d2"][:, :], axis=AX.X))
                link(dve.tensor_scalar(mean[:, :], mean[:, :], 1.0 / F, None, ALU.mult))
                for h in (0, F):
                    link(dve.tensor_scalar(bd["d2"][h:h + F, h:h + F], bd["d2"][h:h + F, h:h + F],
                                           mean[h:h + F, 0:1], None, ALU.subtract))
                link(dve.reduce_max(st[:, 0:1], co[:, 4:7], axis=AX.X))
                link(dve.tensor_scalar(co[:, 4:7], co[:, 4:7], st[:, 0:1], None, ALU.subtract))
                link(dve.tensor_scalar(st[:, 1:2], co[:, 8:9], -1.0, None, ALU.mult))
                link(dve.tensor_tensor(st[:, 1:2], st[:, 1:2], co[:, 8:9], ALU.min))
                dve.sem_inc(tr_done, 1)
                dve.wait_ge(tr_ready, 3)
                link(dve.reduce_sum(st[:, 2:3], co[:, 4:7], axis=AX.X))
                link(dve.reciprocal(st[:, 3:4], st[:, 2:3]))
                link(dve.tensor_scalar(co[:, 4:7], co[:, 4:7], st[:, 3:4], None, ALU.mult))
                link(dve.tensor_scalar(st[:, 4:5], co[:, 8:9], 0.0, None, ALU.max))
                link(dve.tensor_tensor(co[:, 8:9], st[:, 4:5], st[:, 1:2], ALU.add))
                link(dve.tensor_scalar(co[:, 4:7], co[:, 4:7], co[:, 8:9], None, ALU.mult))

            @block.scalar
            def _(act):
                link = linker(act, "act")
                rows_of = lambda a: a.rearrange("(p t) -> p t", p=P)
                for a, b in ((src_in, src_0), (w_in, w_0), (w2_in, w2_0), (dst_in[1:EP + 1], dst_0[1:EP + 1])):
                    act.dma_start(rows_of(a), rows_of(b)).then_inc(copied, 16)
                for n in (0, EP + 1):
                    act.dma_start(dst_in[n:n + 1].rearrange("(a n) -> a n", a=1),
                                  dst_0[n:n + 1].rearrange("(a n) -> a n", a=1)).then_inc(copied, 16)
                act.dma_start(attr3_in.rearrange("(p t) f -> p (t f)", p=P),
                              attr3_0.rearrange("(p t) f -> p (t f)", p=P)).then_inc(copied, 16)
                act.wait_ge(tr_done, 3)
                link(act.activation(co[:, 4:7], co[:, 4:7], ACT.Exp))
                link(act.activation(st[:, 1:2], st[:, 1:2], ACT.Exp))
                act.activation(st[:, 1:2], st[:, 1:2], ACT.Ln, bias=1.0).then_inc(tr_ready, 1)
                act.wait_ge(copied, 7 * 16)

            @block.tensor
            def _(pe):
                pe.wait_ge(ordered, 1)
                pe.matmul(po[:, :], all_rise[:, :], ones[:, :], start=True, stop=True).then_inc(counted, 1)
                pe.wait_ge(made, 2)
                pe.wait_ge(loaded, 16 * (2 * len(order) + 4))
                for k, n in enumerate(("fc", "fcr")):
                    if k:
                        pe.wait_ge(tr_done, k)
                    pe.transpose(tp[:, :], bd[n][:, :], ident[:, :]).then_inc(tr_ready, 1)

    KC = 16

    class Counting:

        def __init__(self, c, hist):
            self.keys_in, self.const = sem("keys_in"), sem("count_consts")
            self.ready, self.used, self.done = sem("onehots"), sem("onehots_used"), sem("counted")
            self.hist = hist
            self.raw = {o: alloc(c, f"keys_{o}", [P, NT], I32) for o in "ds"}
            self.tmp = alloc(c, "key_tmp", [P, NT], I32)
            self.dig = {d: alloc(c, f"dig_{d}", [P, NT], BF16) for d in ("dl", "dh", "sl", "sh")}
            self.oh = [{d: alloc(c, f"oh_{d}{z}", [P, KC, P if d[1] == "l" else HI], BF16) for d in self.dig} for z in range(2)]
            self.iota_i, self.iota = alloc(c, "iota_i", [P, P], I32), alloc(c, "iota", [P, P], BF16)
            self.H = {o: ps(c, f"H_{o}", [P, P]) for o in "ds"}
            self.zb = alloc(c, "zb", [P, P], BF16)

        def load(self, act, src, dst):
            act.dma_start(self.raw["d"][:, :], dst[1:EP + 1].rearrange("(p t) -> p t", p=P)).then_inc(self.keys_in, 16)
            act.dma_start(self.raw["s"][:, :], src.rearrange("(p t) -> p t", p=P)).then_inc(self.keys_in, 16)

        def consts(self, pool):
            pool.memset(self.zb[:, :], 0.0).then_inc(self.const, 1)
            pool.iota(self.iota_i[:, :], pattern=[[1, P]], base=0, channel_multiplier=0).then_inc(self.const, 1)

        def digits(self, dve, link):
            dve.wait_ge(self.const, 2)
            dve.wait_ge(self.keys_in, 32)
            link(dve.tensor_copy(self.iota[:, :], self.iota_i[:, :]))
            for o in "ds":
                link(dve.tensor_scalar(self.tmp[:, :], self.raw[o][:, :], P - 1, None, ALU.bitwise_and))
                link(dve.tensor_copy(self.dig[o + "l"][:, :], self.tmp[:, :]))
                link(dve.tensor_scalar(self.tmp[:, :], self.raw[o][:, :], 7, None, ALU.logical_shift_right))
                link(dve.tensor_copy(self.dig[o + "h"][:, :], self.tmp[:, :]))

        def dve(self, dve, i, b):
            for k in range(T // KC):
                n = (i * 2 + b) * (T // KC) + k
                if not (isinstance(n, int) and n < 2):
                    dve.wait_ge(self.used, n - 1)
                for d, oh in self.oh[k % 2].items():
                    w = oh.shape[2]
                    v = self.dig[d][:, bass.ds(n * KC, KC)].unsqueeze(2).to_broadcast([P, KC, w])
                    u = self.iota[:, 0:w].unsqueeze(1).to_broadcast([P, KC, w])
                    dve.tensor_tensor(oh[:, :, :], v, u, ALU.is_equal).then_inc(self.ready, 1)

        def pe_begin(self, pe):
            pe.wait_ge(self.const, 2)
            for o in "ds":
                pe.matmul(self.H[o][:, :], self.zb[:, :], self.zb[:, :], start=True, stop=False)

        def pe(self, pe, i, b):
            for k in range(T // KC):
                n = (i * 2 + b) * (T // KC) + k
                pe.wait_ge(self.ready, (n + 1) * 4)
                for t in range(KC):
                    for o in "ds":
                        oh = self.oh[k % 2]
                        last = pe.matmul(self.H[o][0:HI, :], oh[o + "h"][:, t, :], oh[o + "l"][:, t, :],
                                         start=False, stop=False)
                last.then_inc(self.used, 1)

        def pe_end(self, pe):
            for o in "ds":
                last = pe.matmul(self.H[o][:, :], self.zb[:, :], self.zb[:, :], start=False, stop=True)
            last.then_inc(self.done, 1)

        def dve_end(self, dve, link):
            dve.wait_ge(self.done, 1)
            for o in "ds":
                link(dve.tensor_copy(self.hist[o][:, :], self.H[o][:, :]))

    @phase
    def count_edges(src, dst, hist):
        with ExitStack() as c, nc.Block() as block:
            cnt = Counting(c, hist)

            @block.scalar
            def _(act):
                cnt.load(act, src, dst)

            @block.gpsimd
            def _(pool):
                cnt.consts(pool)

            @block.tensor
            def _(pe):
                cnt.pe_begin(pe)
                pairs(pe, lambda i, b: cnt.pe(pe, i, b))
                cnt.pe_end(pe)

            @block.vector
            def _(dve):
                link = linker(dve, "dve")
                cnt.digits(dve, link)
                pairs(dve, lambda i, b: cnt.dve(dve, i, b))
                cnt.dve_end(dve, link)

    @phase
    def pointers(hist, first_row, order):
        post, pre, const = sem("hist_sums"), sem("hist_scanned"), sem("ptr_consts")
        stored, back = sem("ptr_stored"), sem("ptr_back")
        with ExitStack() as c, nc.Block() as block:
            ones = alloc(c, "ones_c", [P, P])
            upper = alloc(c, "upper_c", [P, P])
            before = {o: ps(c, f"before_{o}", [P, 1]) for o in "ds"}
            cum = {o: alloc(c, f"cum_{o}", [P, P]) for o in "ds"}
            has, tmp = alloc(c, "has", [P, P]), alloc(c, "tmp_c", [P, P])
            pi = {n: alloc(c, f"pi_{n}", [P, P], I32) for n in flat}
            cb = {o: alloc(c, f"cb_{o}", [P, NJ]) for o in "ds"}
            cm = alloc(c, "cm", [P, NJ])

            @block.gpsimd
            def _(pool):
                pool.memset(ones[:, :], 1.0).then_inc(const, 1)
                pool.wait_ge(const, 1)
                pool.affine_select(out=upper[:, :], in_=ones[:, :], compare_op=ALU.is_gt, fill=0.0, base=0,
                                   pattern=[[1, P]], channel_multiplier=-1).then_inc(const, 1)

            @block.sync
            def _(sp):
                for o in "ds":
                    sp.dma_start(flatf[f"cnt_{o}"].rearrange("(h l) -> h l", l=P), hist[o][0:HI, :]).then_inc(stored, 16)
                sp.wait_ge(post, 2)
                for n in flat:
                    sp.dma_start(flat[n].rearrange("(h l) -> h l", l=P), pi[n][0:HI, :]).then_inc(stored, 16)
                sp.wait_ge(stored, 80)
                for o in "ds":
                    sp.dma_start(cb[o][:, :], flatf[f"cnt_{o}"].rearrange("(p j) -> p j", p=P)).then_inc(back, 16)
                    sp.dma_start(endp[o][:, :], flat[f"end_{o}"].rearrange("(p j) -> p j", p=P)).then_inc(back, 16)
                sp.dma_start(startp[:, :], flat["start_s"].rearrange("(p j) -> p j", p=P)).then_inc(back, 16)

            @block.tensor
            def _(pe):
                pe.wait_ge(const, 2)
                pe.wait_ge(pre, 1)
                for o in "ds":
                    last = pe.matmul(before[o][:, :], upper[:, :], cum[o][:, P - 1:P], start=True, stop=True)
                last.then_inc(post, 1)

            @block.vector
            def _(dve):
                link = linker(dve, "dve")
                dve.wait_ge(const, 2)
                for o in "ds":
                    link(dve.tensor_tensor_scan(cum[o][:, :], ones[:, :], hist[o][:, :], 0.0, ALU.mult, ALU.add))
                dve.sem_inc(pre, 1)
                dve.wait_ge(post, 1)
                for o in "ds":
                    link(dve.tensor_scalar(cum[o][:, :], cum[o][:, :], before[o][:, 0:1], None, ALU.add))
                    link(dve.tensor_scalar(has[:, :], hist[o][:, :], 1.0, None, ALU.min))
                    if o == order:
                        link(dve.tensor_tensor(first_row[:, :], cum[o][:, :], hist[o][:, :], ALU.subtract))
                    if o == "s":
                        link(dve.tensor_tensor(tmp[:, :], cum[o][:, :], hist[o][:, :], ALU.subtract))
                        link(dve.tensor_scalar(tmp[:, :], tmp[:, :], -NOROW, None, ALU.add))
                        link(dve.tensor_tensor(tmp[:, :], tmp[:, :], has[:, :], ALU.mult))
                        link(dve.tensor_scalar(tmp[:, :], tmp[:, :], NOROW, None, ALU.add))
                        link(dve.tensor_copy(pi["start_s"][:, :], tmp[:, :]))
                    link(dve.tensor_scalar(cum[o][:, :], cum[o][:, :], -1.0 - EP, None, ALU.add))
                    link(dve.tensor_tensor(cum[o][:, :], cum[o][:, :], has[:, :], ALU.mult))
                    link(dve.tensor_scalar(cum[o][:, :], cum[o][:, :], float(EP), None, ALU.add))
                    link(dve.tensor_copy(pi[f"end_{o}"][:, :], cum[o][:, :]))
                dve.sem_inc(post, 1)
                dve.wait_ge(back, 80)
                for o in "ds":
                    link(dve.tensor_scalar(cm[:, :], cb[o][:, :], 1.0, None, ALU.max))
                    link(dve.reciprocal(inv[o][:, :], cm[:, :]))
                    link(dve.tensor_scalar(cm[:, :], cb[o][:, :], 1.0, None, ALU.min))
                    link(dve.tensor_tensor(inv[o][:, :], inv[o][:, :], cm[:, :], ALU.mult))

    @phase
    def sort_edges(first_row, key, second, third):
        NP2 = T // 2
        NGP = T // 4
        loaded = [sem(f"sort_in{b}") for b in range(2)]
        moved = [sem(f"sort_out{b}") for b in range(2)]
        q = lambda n: sem(f"sort_{n}")
        const, started, copied, packed, dg, ohr, idx_r = (q(n) for n in (
            "consts", "started", "columns", "packed", "digits", "onehots", "idx"))
        tr, tev, eqr, msk, look, placed, pev, rk = (q(n) for n in (
            "turned", "turned_copied", "same", "masked", "looked_up", "placed", "place_copied", "ranked"))
        with ExitStack() as c, nc.Block() as block:
            recs = [alloc(c, f"recs{b}", [P, T, 3], I32) for b in range(2)]
            raw = [alloc(c, f"raw{b}", [P, 3, T], I32) for b in range(2)]
            di, lo, hi = alloc(c, "di", [P, 2, T], I32), alloc(c, "lo", [P, T], BF16), alloc(c, "hi", [P, T], BF16)
            ohl = [alloc(c, f"ohl{b}", [P, T, P], BF16) for b in range(2)]
            ohh = [alloc(c, f"ohh{b}", [P, T, HI], BF16) for b in range(2)]
            ohT = [alloc(c, f"ohT{z}", [P, 4, P]) for z in range(2)]
            same = [[alloc(c, f"same{z}{h}", [P, 3, P], BF16) for h in range(2)] for z in range(2)]
            mask = alloc(c, "mask", [P, 3, P])
            place = alloc(c, "place", [P, HI])
            junk = alloc(c, "junk", [P, HI])
            pos = alloc(c, "pos", [P, T])
            idx = [alloc(c, f"sidx{b}", [P, T], I32) for b in range(2)]
            iota_i, iota = alloc(c, "iota_i", [P, P], I32), alloc(c, "iota", [P, P], BF16)
            identb = alloc(c, "identb", [P, P], BF16)
            pT = [ps(c, f"pT{z}", [P, 4, P], BF16) for z in range(2)]
            pE = [ps(c, f"pE{h}", [P, 3, P]) for h in range(2)]
            pV = [ps(c, f"pV{h}", [P, 2, P]) for h in range(2)]
            pP = ps(c, "pP", [P, HI])
            zeros, zm, zd = alloc(c, "zeros", [P, T, F + 1]), sem("zeros"), sem("zeroed")

            def zero(n):
                return isinstance(n, int) and n == 0

            @block.sync
            def _(sp):
                def load(i, b):
                    if not zero(i):
                        sp.wait_ge(packed, i * 2 + b - 1)
                    for n, a in enumerate((key, second, third)):
                        d = raw[b][:, n, :]
                        sp.dma_start(d.bitcast(a.dtype), cols(a, i * 2 + b)).then_inc(loaded[b], 16)
                    sp.dma_start(cols(spread, i * 2 + b), zeros[:, :, :]).then_inc(zd, 16)
                sp.wait_ge(zm, 1)
                pairs(sp, load)
                sp.dma_start(sums2[EP:ROWS, :], zeros[0:1, 0:2, 0:F]).then_inc(zd, 16)
                sp.wait_ge(zd, 16 * (NCH + 1))

            @block.gpsimd
            def _(pool):
                pool.iota(iota_i[:, :], pattern=[[1, P]], base=0, channel_multiplier=0).then_inc(const, 1)
                pool.memset(mask[:, :, :], 1.0).then_inc(const, 1)
                pool.memset(zeros[:, :, :], 0.0).then_inc(zm, 1)
                pool.wait_ge(const, 2)
                for n in (0, 2):
                    pool.affine_select(out=mask[:, n, :], in_=mask[:, n, :], compare_op=ALU.is_gt, fill=0.0, base=0,
                                       pattern=[[1, P]], channel_multiplier=-1).then_inc(const, 1)

                def scatter(i, b):
                    pool.wait_ge(packed, i * 2 + b + 1)
                    for j in range(T):
                        if j % (T // 4) == 0:
                            pool.wait_ge(idx_r, (i * 2 + b) * 4 + j // (T // 4) + 1)
                            pool.sem_inc(started, 1)
                        pool.indirect_dma_start(rec, bass.IndirectOffsetOnAxis(ap=idx[b][:, j:j + 1], axis=0),
                                                recs[b][:, j, :], None).then_inc(moved[b], 16)
                with pool.Fori(0, NCH // 2) as i:
                    scatter(i, 0)
                    scatter(i, 1)
                for b in range(2):
                    pool.wait_ge(moved[b], NCH // 2 * 16 * T)

            @block.scalar
            def _(act):
                def pack(i, b):
                    act.wait_ge(loaded[b], (i + 1) * 48)
                    if not zero(i):
                        act.wait_ge(moved[b], i * 16 * T)
                    for n in range(3):
                        s, d = raw[b][:, n, :], recs[b][:, :, n]
                        if n == 2:
                            s, d = s.bitcast(third.dtype), d.bitcast(third.dtype)
                        act.activation(d, s, ACT.Copy).then_inc(copied, 1)
                    act.wait_ge(copied, (i * 2 + b + 1) * 3)
                    act.sem_inc(packed, 1)

                def turned(ch, g, z):
                    act.wait_ge(tr, ch * NGP + g + 1)
                    if not (zero(ch) and g < 2):
                        act.wait_ge(look, ch * NP2 + 2 * g - 2)
                    act.activation(ohT[z][:, :, :], pT[z][:, :, :], ACT.Copy).then_inc(tev, 1)

                def step(i, b):
                    ch = i * 2 + b
                    turned(ch, 0, 0)
                    for g in range(NGP):
                        if g + 1 < NGP:
                            turned(ch, g + 1, (g + 1) % 2)
                        for h in range(2):
                            act.wait_ge(placed, ch * NP2 + 2 * g + h + 2)
                            act.activation(place[:, :], pP[:, :], ACT.Copy).then_inc(pev, 1)
                        if g == (0 if zero(ch) else 3 * NGP // 4):
                            pack(i, b)
                act.wait_ge(placed, 1)
                act.activation(place[:, :], pP[:, :], ACT.Copy).then_inc(pev, 1)
                pairs(act, step)

            @block.vector
            def _(dve):
                link = linker(dve, "dve")
                dve.wait_ge(const, 4)
                link(dve.tensor_copy(iota[:, :], iota_i[:, :]))
                link(dve.tensor_copy(identb[:, :], ident[:, :]))
                dve.sem_inc(const, 1)

                def digits(i, b):
                    ch = i * 2 + b
                    dve.wait_ge(loaded[b], (i + 1) * 48)
                    if not zero(ch):
                        dve.wait_ge(ohr, ch * 2 * NGP)
                    dve.tensor_scalar(di[:, 0, :], raw[b][:, 0, :], P - 1, None, ALU.bitwise_and).then_inc(dg, 1)
                    dve.tensor_scalar(di[:, 1, :], raw[b][:, 0, :], 7, None, ALU.logical_shift_right).then_inc(dg, 1)
                    dve.wait_ge(dg, ch * 4 + 2)
                    dve.tensor_copy(lo[:, :], di[:, 0, :]).then_inc(dg, 1)
                    dve.tensor_copy(hi[:, :], di[:, 1, :]).then_inc(dg, 1)
                    dve.wait_ge(dg, ch * 4 + 4)

                def onehots(ch, b, g):
                    for src, dst, w in ((lo, ohl, P), (hi, ohh, HI)):
                        v = src[:, 4 * g:4 * g + 4].unsqueeze(2).to_broadcast([P, 4, w])
                        u = iota[:, 0:w].unsqueeze(1).to_broadcast([P, 4, w])
                        dve.tensor_tensor(dst[b][:, 4 * g:4 * g + 4, :], v, u, ALU.is_equal).then_inc(ohr, 1)

                def masks_(ch, g):
                    for h in range(2):
                        dve.wait_ge(eqr, ch * NP2 + 2 * g + h + 1)
                        if not (zero(ch) and g < 2):
                            dve.wait_ge(look, ch * NP2 + 2 * g + h - 3)
                        dve.tensor_tensor(same[g % 2][h][:, :, :], pE[h][:, :, :], mask[:, :, :], ALU.mult).then_inc(msk, 1)

                def ranks(ch, g, h, b):
                    dve.wait_ge(look, ch * NP2 + 2 * g + h + 1)
                    for k in range(2):
                        t = 4 * g + 2 * h + k
                        if not (zero(ch) and t == 0):
                            dve.wait_ge(rk, ch * T + t)
                        dve.tensor_tensor_reduce(out=junk[:, :], in0=pV[h][:, k, 0:HI], in1=ohh[b][:, t, :], scale=1.0, scalar=0.0,
                                                 op0=ALU.mult, op1=ALU.add, accum_out=pos[:, t:t + 1]).then_inc(rk, 1)

                def step(i, b, last=False):
                    ch = i * 2 + b
                    if not last:
                        digits(*((i, 1) if b == 0 else (i + 1, 0)))
                    masks_(ch, 0)
                    for g in range(NGP):
                        ranks(ch, g, 0, b)
                        if g + 1 < NGP:
                            masks_(ch, g + 1)
                        ranks(ch, g, 1, b)
                        if not last:
                            onehots(ch + 1, 1 - b, g)
                        if g % 4 == 3:
                            n = g // 4
                            dve.wait_ge(rk, ch * T + (n + 1) * 16)
                            if n == 0 and not zero(i):
                                dve.wait_ge(moved[b], i * 16 * T)
                            dve.tensor_copy(idx[b][:, 16 * n:16 * n + 16], pos[:, 16 * n:16 * n + 16]).then_inc(idx_r, 1)
                    dve.wait_ge(idx_r, ch * 4 + 4)
                digits(0, 0)
                for g in range(NGP):
                    onehots(0, 0, g)
                step(0, 0)
                step(0, 1)
                with dve.Fori(1, NCH // 2 - 1) as i:
                    step(i, 0)
                    step(i, 1)
                step(NCH // 2 - 1, 0)
                step(NCH // 2 - 1, 1, last=True)

            @block.tensor
            def _(pe):
                pe.wait_ge(const, 5)
                pe.matmul(pP[:, :], first_row[:, :], ident[:, 0:HI], start=True, stop=True).then_inc(placed, 1)

                def turn(ch, g, b):
                    if not (zero(ch) and g < 2):
                        pe.wait_ge(tev, ch * NGP + g - 1)
                    pe.wait_ge(ohr, (ch * NGP + g + 1) * 2)
                    for t in range(4):
                        last = pe.transpose(pT[g % 2][:, t, :], ohl[b][:, 4 * g + t, :], identb[:, :])
                    last.then_inc(tr, 1)

                def equal(ch, g):
                    pe.wait_ge(tev, ch * NGP + g + 1)
                    o = ohT[g % 2]
                    for h in range(2):
                        if not (zero(ch) and g == 0):
                            pe.wait_ge(msk, ch * NP2 + 2 * g + h - 1)
                        pe.matmul(pE[h][:, 0:2, :].rearrange("p a e -> p (a e)"), o[:, 2 * h, :],
                                  o[:, 2 * h:2 * h + 2, :].rearrange("p a e -> p (a e)"), start=True, stop=True)
                        pe.matmul(pE[h][:, 2, :], o[:, 2 * h + 1, :], o[:, 2 * h + 1, :],
                                  start=True, stop=True).then_inc(eqr, 1)

                def rows_of(ch, g, h, b):
                    n = ch * NP2 + 2 * g + h
                    o, s, t = ohT[g % 2], same[g % 2][h], 4 * g + 2 * h
                    pe.wait_ge(msk, n + 1)
                    pe.wait_ge(pev, n + 1)
                    if not (zero(ch) and g == 0):
                        pe.wait_ge(rk, 2 * n - 2)
                    pe.matmul(pV[h][:, 0, 0:HI], o[:, 2 * h, :], place[:, :], start=True, stop=False)
                    pe.matmul(pV[h][:, 0, 0:HI], s[:, 0, :], ohh[b][:, t, :], start=False, stop=True)
                    pe.matmul(pV[h][:, 1, 0:HI], o[:, 2 * h + 1, :], place[:, :], start=True, stop=False)
                    pe.matmul(pV[h][:, 1, 0:HI], s[:, 1, :], ohh[b][:, t, :], start=False, stop=False)
                    pe.matmul(pV[h][:, 1, 0:HI], s[:, 2, :], ohh[b][:, t + 1, :], start=False, stop=True).then_inc(look, 1)
                    for k in range(2):
                        last = pe.matmul(pP[:, :], ohl[b][:, t + k, :], ohh[b][:, t + k, :], start=False, stop=k == 1,
                                         skip_group_check=True)
                    last.then_inc(placed, 1)

                def step(i, b):
                    ch = i * 2 + b
                    turn(ch, 0, b)
                    equal(ch, 0)
                    for g in range(NGP):
                        if g + 1 < NGP:
                            turn(ch, g + 1, b)
                        rows_of(ch, g, 0, b)
                        if g + 1 < NGP:
                            equal(ch, g + 1)
                        rows_of(ch, g, 1, b)
                pairs(pe, step)

    def edge_weights(c, block):
        ld, pr, wr, ax = sem("weights_loaded"), sem("weights_ready"), sem("weights_written"), sem("softplus_ready")
        s_c, d_c = alloc(c, "s_c", [P, NT], I32), alloc(c, "d_c", [P, NT], I32)
        w_c, v = alloc(c, "w_c", [P, NT]), alloc(c, "v", [P, NT])
        a, b = alloc(c, "a", [P, NT]), alloc(c, "b", [P, NT])
        flat_ = lambda x: x.rearrange("(p t) -> p t", p=P)

        @block.gpsimd
        def _(pool):
            pool.dma_start(v[:, :], flat_(w2_in)).then_inc(ld, 16)
            pool.dma_start(s_c[:, :], flat_(src_in)).then_inc(ld, 16)
            pool.dma_start(d_c[:, :], flat_(dst_in[1:EP + 1])).then_inc(ld, 16)
            pool.dma_start(w_c[:, :], flat_(w_in)).then_inc(ld, 16)
            pool.wait_ge(pr, 1)
            pool.dma_start(flat_(base_in), w_c[:, :]).then_inc(wr, 16)
            pool.wait_ge(wr, 16)

        @block.vector
        def _(dve):
            link = linker(dve, "dve")
            dve.wait_ge(ld, 64)
            link(dve.tensor_scalar(v[:, :], v[:, :], co[:, 0:1], co[:, 1:2], ALU.mult, ALU.add))
            link(dve.tensor_scalar(a[:, :], v[:, :], -1.0, None, ALU.mult))
            link(dve.tensor_tensor(a[:, :], a[:, :], v[:, :], ALU.min))
            dve.sem_inc(ax, 1)
            link(dve.tensor_scalar(b[:, :], v[:, :], 0.0, None, ALU.max))
            dve.wait_ge(ax, 2)
            link(dve.tensor_tensor(b[:, :], b[:, :], a[:, :], ALU.add))
            link(dve.tensor_tensor(v[:, :], s_c[:, :], d_c[:, :], ALU.not_equal))
            link(dve.tensor_tensor(b[:, :], b[:, :], v[:, :], ALU.mult))
            link(dve.tensor_tensor(w_c[:, :], b[:, :], w_c[:, :], ALU.mult))
            dve.sem_inc(pr, 1)

        @block.scalar
        def _(act):
            link = linker(act, "act")
            act.wait_ge(ax, 1)
            link(act.activation(a[:, :], a[:, :], ACT.Exp))
            link(act.activation(a[:, :], a[:, :], ACT.Ln, bias=1.0))
            act.sem_inc(ax, 1)

    @phase
    def unpack_sorted(key, second, third):
        ld, pr, wr = sem("rec_loaded"), sem("rec_ready"), sem("rec_written")
        with ExitStack() as c, nc.Block() as block:
            r = alloc(c, "r", [P, NT, 3], I32)
            s_c, d_c = alloc(c, "s_c", [P, NT], I32), alloc(c, "d_c", [P, NT], I32)
            w_c = alloc(c, "w_c", [P, NT], third.dtype)
            end = alloc(c, "end", [1, 2], I32)

            @block.sync
            def _(sp):
                sp.dma_start(r[:, :, :], rec.rearrange("(p t) f -> p t f", p=P)).then_inc(ld, 16)
                sp.wait_ge(pr, 1)
                sp.dma_start(key[1:EP + 1].rearrange("(p t) -> p t", p=P), s_c[:, :]).then_inc(wr, 16)
                sp.wait_ge(pr, 2)
                sp.dma_start(key[0:1].rearrange("(a n) -> a n", a=1), end[:, 0:1]).then_inc(wr, 16)
                sp.dma_start(key[EP + 1:EP + 2].rearrange("(a n) -> a n", a=1), end[:, 1:2]).then_inc(wr, 16)
                sp.wait_ge(pr, 3)
                sp.dma_start(second.rearrange("(p t) -> p t", p=P), d_c[:, :]).then_inc(wr, 16)
                sp.wait_ge(pr, 4)
                sp.dma_start(third.rearrange("(p t) -> p t", p=P), w_c[:, :]).then_inc(wr, 16)
                sp.wait_ge(wr, 80)

            @block.vector
            def _(dve):
                dve.wait_ge(ld, 16)
                dve.tensor_copy(s_c[:, :], r[:, :, 0]).then_inc(pr, 1)
                dve.memset(end[:, :], -1).then_inc(pr, 1)
                dve.tensor_copy(d_c[:, :], r[:, :, 1]).then_inc(pr, 1)
                dve.tensor_copy(w_c[:, :], r[:, :, 2].bitcast(third.dtype)).then_inc(pr, 1)

    def masks(o, keys, c, block):
        ld, tr, bc = sem(f"mask_{o}_in"), sem(f"mask_{o}_T"), sem(f"mask_{o}_b")
        k = [alloc(c, f"k{n}", [P, NT], I32) for n in range(3)]
        nx, col = alloc(c, "nx", [P, NT]), alloc(c, "col", [P, NT], I32)
        rowb, rowf = alloc(c, "rowb", [P, 1], I32), alloc(c, "rowf", [P, 1])
        m = alloc(c, "m", [P, 1])
        ab = alloc(c, "ab", [P, F])
        pt = ps(c, "pt", [F, P])
        io = sem(f"mask_{o}_iota")

        @block.scalar
        def _(act):
            for n in range(3):
                act.dma_start(k[n][:, :], keys[n:n + EP].rearrange("(p t) -> p t", p=P)).then_inc(ld, 16)

        @block.gpsimd
        def _(pool):
            pool.iota(col[:, :], pattern=[[1, NT]], base=0, channel_multiplier=0).then_inc(io, 1)
            pool.iota(rowb[:, :], pattern=[[0, 1]], base=0, channel_multiplier=NT).then_inc(io, 1)

        @block.vector
        def _(dve):
            link = linker(dve, "dve")
            dve.wait_ge(ld, 48)
            dve.wait_ge(io, 2)
            kp = keep[o]
            link(dve.tensor_tensor(kp[:, :], k[1][:, :], k[0][:, :], ALU.is_equal))
            link(dve.tensor_tensor(nx[:, :], k[1][:, :], k[2][:, :], ALU.is_equal))
            link(dve.tensor_copy(fk[o][:, :], kp[:, 0:1]))
            link(dve.tensor_reduce(out=m[:, :], in_=kp[:, :], op=ALU.min, axis=AX.X))
            link(dve.memset(ab[:, :], 0.0))
            link(dve.tensor_scalar(ab[:, :], ab[:, :], m[:, 0:1], None, ALU.add))
            dve.sem_inc(bc, 1)
            link(dve.memset(kp[:, 0:1], 0.0))
            if o == "d":
                link(dve.tensor_scalar(neg[:, :], nx[:, :], 1.0, BIG, ALU.subtract, ALU.mult))
            link(dve.tensor_scalar(nx[:, :], nx[:, :], NOROW, None, ALU.mult))
            link(dve.tensor_tensor(nx[:, :], nx[:, :], col[:, :], ALU.add))
            link(dve.tensor_reduce(out=m[:, :], in_=nx[:, :], op=ALU.min, axis=AX.X))
            link(dve.tensor_copy(rowf[:, :], rowb[:, :]))
            link(dve.tensor_tensor(m[:, :], m[:, :], rowf[:, :], ALU.add))
            link(dve.tensor_copy(end0[o][:, :], m[:, :]))
            dve.wait_ge(tr, 1)
            link(dve.tensor_copy(aT[o][:, :], pt[:, :]))

        @block.tensor
        def _(pe):
            pe.wait_ge(bc, 1)
            pe.transpose(pt[:, :], ab[:, :], ident[:, :]).then_inc(tr, 1)

    def gathers(pool, table, idx, rows, idx_in, rows_in, free, go, w, n):
        def gather(i, b):
            if not isinstance(i, int) or i:
                free(pool, i, b)
            pool.wait_ge(idx_in[b], (i + 1) * 16)
            pool.sem_inc(go, 1)
            for j in range(w):
                pool.indirect_dma_start(rows[b][:, j, :], None, table,
                                        bass.IndirectOffsetOnAxis(ap=idx[b][:, j:j + 1], axis=0)).then_inc(rows_in[b], 16)
        pairs(pool, gather, n)

    def pairs(eng, step, n=NCH):
        step(0, 0)
        step(0, 1)
        with eng.Fori(1, n // 2) as i:
            step(i, 0)
            step(i, 1)

    DW = 16
    QUARTER = NT // 4
    dist_w = alloc(top, "dist_w", [F + 1, DW * F])
    dist_b2 = alloc(top, "dist_b2", [1, 4 * P])
    dist_v = {n: alloc(top, f"dist_{n}", [P, F]) for n in ("g1", "b1", "g2", "b2")}
    ones_row = alloc(top, "ones_row", [1, P])

    class Distances:

        def __init__(self, c, q):
            S = lambda n: sem(f"dist{q}_{n}")
            self.first = q * QUARTER
            self.a3_in, self.a3_T, self.a3_s, self.y1, self.y1_s = S("a3_in"), S("a3_T"), S("a3_s"), S("y1"), S("y1_s")
            self.sq, self.ln, self.ge, self.tr, self.ts, self.y2, self.y2_s = (S(n) for n in ("sq", "ln", "ge", "tr", "ts", "y2", "y2_s"))
            self.k, self.stored, self.var, self.sd = S("dve"), S("stored"), S("var"), S("sd")
            self.a3 = alloc(c, "a3", [P, P])
            self.a3T = alloc(c, "a3T", [F + 1, P])
            self.Y, self.SQ = alloc(c, "Y", [P, DW, F]), alloc(c, "SQ", [P, DW, F])
            self.yT = alloc(c, "yT", [P, 4, P])
            self.ss = alloc(c, "ss", [P, DW])
            self.pa, self.p1 = ps(c, "pa", [P, P]), ps(c, "p1", [P, DW, F])
            self.pt, self.p2 = ps(c, "pt", [P, 4, P]), ps(c, "p2", [P, 4, P])

        def start(self, dve):
            dve.memset(self.a3[:, :], 0.0).then_inc(self.k, 1)
            dve.memset(self.a3T[:, :], 1.0).then_inc(self.k, 1)

        def load(self, sp, i, b):
            ch = i * 2 + b
            if isinstance(ch, int) and ch == 0:
                sp.wait_ge(self.k, 2)
            else:
                sp.wait_ge(self.a3_T, ch)
            src = attr3_in.rearrange("(p t) f -> p (t f)", p=P)[:, bass.ds(ch * DW * 3 + self.first * 3, DW * 3)]
            sp.dma_start(self.a3[:, 0:DW * 3], src).then_inc(self.a3_in, 16)

        def store(self, sp, i, b):
            ch = i * 2 + b
            sp.wait_ge(self.ge, ch * 2 + 2)
            sp.dma_start(cols(dists, ch, DW, self.first), self.Y[:, :, :]).then_inc(self.stored, 16)

        def pe_first(self, pe, i, b):
            ch = i * 2 + b
            pe.wait_ge(self.a3_in, ch * 16 + 16)
            pe.transpose(self.pa[:, :], self.a3[:, :], ident[:, :]).then_inc(self.a3_T, 1)
            pe.wait_ge(self.a3_s, ch + 1)
            for h in range(2):
                t = pe.matmul(self.p1[:, 8 * h:8 * h + 8, :].rearrange("p a f -> p (a f)"), self.a3T[:, :],
                              dist_w[:, h * 512:(h + 1) * 512], start=True, stop=True)
            t.then_inc(self.y1, 1)

        def pe_second(self, pe, i, b):
            ch = i * 2 + b
            first = isinstance(ch, int) and ch == 0
            pe.wait_ge(self.ge, ch * 2 + 1)
            for g in range(2):
                for h in range(4):
                    r = self.Y[:, 8 * g + 2 * h:8 * g + 2 * h + 2, :].rearrange("p a f -> p (a f)")
                    t = pe.transpose(self.pt[:, h, :], r, ident[:, :])
                t.then_inc(self.tr, 1)
                pe.wait_ge(self.ts, ch * 2 + g + 1)
                if g or not first:
                    pe.wait_ge(self.y2_s, ch * 2 + g)
                pe.matmul(self.p2[:, :, :].rearrange("p a f -> p (a f)"), ones_row[:, :], dist_b2[:, :], start=True, stop=False)
                for h in range(4):
                    t = pe.matmul(self.p2[:, h, :], self.yT[:, h, :], bd["d2"][:, :], start=False, stop=h == 3)
                t.then_inc(self.y2, 1)

        def act(self, act, i, b):
            ch = i * 2 + b
            act.wait_ge(self.a3_T, ch + 1)
            act.activation(self.a3T[0:F, :], self.pa[0:F, :], ACT.Copy).then_inc(self.a3_s, 1)
            act.wait_ge(self.y1, ch + 1)
            if not (isinstance(ch, int) and ch == 0):
                act.wait_ge(self.stored, ch * 16)
            flat_ = lambda t: t[:, :, :].rearrange("p a f -> p (a f)")
            act.activation(flat_(self.Y), flat_(self.p1), ACT.Copy).then_inc(self.y1_s, 1)
            act.wait_ge(self.y1_s, ch + 1)
            act.activation(self.SQ[:, :, :], self.Y[:, :, :], ACT.Square).then_inc(self.sq, 1)
            act.wait_ge(self.var, ch * 2 + 1)
            act.activation(self.ss[:, :], self.ss[:, :], ACT.Sqrt).then_inc(self.sd, 1)
            act.wait_ge(self.ln, ch * 2 + 1)
            act.activation(self.Y[:, :, :], self.Y[:, :, :], ACT.Gelu).then_inc(self.ge, 1)
            for g in range(2):
                act.wait_ge(self.tr, ch * 2 + g + 1)
                act.activation(self.yT[:, :, :], self.pt[:, :, :], ACT.Copy).then_inc(self.ts, 1)
                act.wait_ge(self.y2, ch * 2 + g + 1)
                act.activation(self.Y[:, 8 * g:8 * g + 8, :].rearrange("p a f -> p (a f)"),
                               self.p2[:, :, :].rearrange("p a f -> p (a f)"), ACT.Copy).then_inc(self.y2_s, 1)
            act.wait_ge(self.y2_s, ch * 2 + 2)
            act.activation(self.SQ[:, :, :], self.Y[:, :, :], ACT.Square).then_inc(self.sq, 1)
            act.wait_ge(self.var, ch * 2 + 2)
            act.activation(self.ss[:, :], self.ss[:, :], ACT.Sqrt).then_inc(self.sd, 1)
            act.wait_ge(self.ln, ch * 2 + 2)
            act.activation(self.Y[:, :, :], self.Y[:, :, :], ACT.Gelu).then_inc(self.ge, 1)

        def dve(self, dve, i, b, h):
            ch = i * 2 + b
            k = [ch * 12 + 6 * h + 2]

            def link(ins):
                ins.then_inc(self.k, 1)
                k[0] = k[0] + 1
                dve.wait_ge(self.k, k[0])
            Y, ss = self.Y, self.ss
            dve.wait_ge(self.sq, ch * 2 + h + 1)
            link(dve.reduce_sum(ss[:, :], self.SQ[:, :, :], axis=AX.X))
            link(dve.tensor_scalar(ss[:, :], ss[:, :], 1.0 / F, EPS, ALU.mult, ALU.add))
            dve.sem_inc(self.var, 1)
            dve.wait_ge(self.sd, ch * 2 + h + 1)
            link(dve.reciprocal(ss[:, :], ss[:, :]))
            link(dve.tensor_tensor(Y[:, :, :], Y[:, :, :], ss[:, :].unsqueeze(2).to_broadcast([P, DW, F]), ALU.mult))
            g, bb = dist_v[f"g{h + 1}"], dist_v[f"b{h + 1}"]
            link(dve.tensor_tensor(Y[:, :, :], Y[:, :, :], g[:, :].unsqueeze(1).to_broadcast([P, DW, F]), ALU.mult))
            link(dve.tensor_tensor(Y[:, :, :], Y[:, :, :], bb[:, :].unsqueeze(1).to_broadcast([P, DW, F]), ALU.add))
            dve.sem_inc(self.ln, 1)

    @phase
    def number_edges():
        made, st = sem("numbers"), sem("numbers_out")
        with ExitStack() as c, nc.Block() as block:
            t = alloc(c, "numbers", [P, NT], I32)

            @block.gpsimd
            def _(pool):
                pool.iota(t[:, :], pattern=[[1, NT]], base=0, channel_multiplier=NT).then_inc(made, 1)

            @block.sync
            def _(sp):
                sp.wait_ge(made, 1)
                sp.dma_start(number.rearrange("(p t) -> p t", p=P), t[:, :]).then_inc(st, 16)
                sp.wait_ge(st, 16)

    @phase
    def permute(name, table, to):
        w = table.shape[1]
        idx_in, rows_in, stored = ([sem(f"perm_{name}_{n}{b}") for b in range(2)] for n in ("idx", "rows", "out"))
        go = sem(f"perm_{name}_go")
        with ExitStack() as c, nc.Block() as block:
            idx = [alloc(c, f"idx{b}", [P, T], I32) for b in range(2)]
            rows = [alloc(c, f"rows{b}", [P, T, w]) for b in range(2)]

            @block.sync
            def _(sp):
                def step(i, b):
                    if not isinstance(i, int) or i:
                        sp.wait_ge(rows_in[b], i * 16 * T)
                    sp.dma_start(idx[b][:, :], cols(perm, i * 2 + b)).then_inc(idx_in[b], 16)
                    if not isinstance(i, int) or i or b:
                        store(*((i - 1, 1) if b == 0 else (i, 0)))

                def store(i, b):
                    sp.wait_ge(rows_in[b], (i + 1) * 16 * T)
                    sp.dma_start(cols(to, i * 2 + b), rows[b][:, :, :]).then_inc(stored[b], 16)
                pairs(sp, step)
                store(NCH // 2 - 1, 1)
                for b in range(2):
                    sp.wait_ge(stored[b], NCH // 2 * 16)

            @block.gpsimd
            def _(pool):
                gathers(pool, table, idx, rows, idx_in, rows_in, lambda e, i, b: e.wait_ge(stored[b], i * 16), go, T, NCH)

    def sort_by_dst():
        number_edges()
        with ExitStack() as c:
            hist = {k: alloc(c, f"hist_{k}", [P, P]) for k in "ds"}
            first_row = alloc(c, "first_row", [P, P])
            count_edges(src_0, dst_0, hist)
            pointers(hist, first_row, "d")
            sort_edges(first_row, dst_0[1:EP + 1], src_0, number)
            unpack_sorted(dst_in, src_in, perm)
        for name, table, to in (("w", w_0, w_in), ("w2", w2_0, w2_in)):
            column = lambda a: a.rearrange("(e a) -> e a", a=1)
            permute(name, column(table), column(to))
        permute("attr3", attr3_0, attr3_in)
        permute("attr64", attr64_0, attr64_s)

    @phase
    def sum_pass(name, o, idx_arr, table, last, quarter, hist=None, beside=()):
        S = lambda n: [sem(f"{name}_{n}{b}") for b in range(2)]
        idx_in, rows_in, stored = S("idx"), S("rows"), S("stored")
        scanned, carried, go = sem(f"{name}_scanned"), sem(f"{name}_carried"), sem(f"{name}_go")
        with ExitStack() as c, nc.Block() as block:
            idx = [alloc(c, f"idx{b}", [P, T], I32) for b in range(2)]
            rows = [alloc(c, f"rows{b}", [P, T, F]) for b in range(2)]
            dist = Distances(c, quarter)
            cnt = Counting(c, hist) if hist else None
            for part in beside:
                part(c, block)

            @block.sync
            def _(sp):
                def load(i, b):
                    if not isinstance(i, int) or i:
                        sp.wait_ge(rows_in[b], i * 16 * T)
                    sp.dma_start(idx[b][:, :], cols(idx_arr, i * 2 + b)).then_inc(idx_in[b], 16)
                    dist.load(sp, i, b)

                def step(i, b):
                    load(i, b)
                    if not isinstance(i, int) or i or b:
                        bb, ii = (1, i - 1) if b == 0 else (0, i)
                        store(ii, bb)

                def store(i, b):
                    sp.wait_ge(scanned, (i * 2 + b + 1) * F)
                    sp.dma_start(cols(sums[0:EP, :], i * 2 + b), rows[b][:, :, :]).then_inc(stored[b], 16)
                    dist.store(sp, i, b)
                pairs(sp, step)
                store(NCH // 2 - 1, 1)
                for b in range(2):
                    sp.wait_ge(stored[b], NCH // 2 * 16)
                sp.wait_ge(dist.stored, NCH * 16)

            @block.gpsimd
            def _(pool):
                if cnt:
                    cnt.consts(pool)
                gathers(pool, table, idx, rows, idx_in, rows_in, lambda e, i, b: e.wait_ge(stored[b], i * 16), go, T, NCH)

            @block.tensor
            def _(pe):
                def step(i, b):
                    dist.pe_first(pe, i, b)
                    if cnt:
                        cnt.pe(pe, i, b)
                    dist.pe_second(pe, i, b)
                if cnt:
                    cnt.pe_begin(pe)
                pairs(pe, step)
                if cnt:
                    cnt.pe_end(pe)

            @block.scalar
            def _(act):
                if cnt:
                    cnt.load(act, src_in, dst_in)
                pairs(act, lambda i, b: dist.act(act, i, b))

            @block.vector
            def _(dve):
                dist.start(dve)
                dve.memset(last[:, :], 0.0).then_inc(carried, 1)

                def scan(i, b):
                    ch = i * 2 + b
                    dist.dve(dve, i, b, 0)
                    if cnt:
                        cnt.dve(dve, i, b)
                    dve.wait_ge(rows_in[b], (i + 1) * 16 * T)
                    dve.wait_ge(carried, ch + 1)
                    k = keep[o][:, bass.ds(ch * T, T)]
                    for f in range(F):
                        dve.tensor_tensor_scan(rows[b][:, :, f], k, rows[b][:, :, f], last[:, f:f + 1],
                                               ALU.mult, ALU.add).then_inc(scanned, 1)
                    dve.wait_ge(scanned, (ch + 1) * F)
                    dve.tensor_copy(last[:, :], rows[b][:, T - 1, :]).then_inc(carried, 1)
                    dist.dve(dve, i, b, 1)
                link = linker(dve, "dve")
                if cnt:
                    cnt.digits(dve, link)
                pairs(dve, scan)
                if cnt:
                    cnt.dve_end(dve, link)

    TS = 52

    @phase
    def softmax_pass(name, idx_arr, table, last, lastmax):
        NC = NT // TS
        one = name == "L1"
        W_ = F if one else 2 * F
        S = lambda n: [sem(f"{name}_{n}{b}") for b in range(2)]
        q = lambda n: sem(f"{name}_{n}")
        idx_in, rows_in = S("idx"), S("rows")
        go, side_in, maxed, dk, faded, valued, summed, carried, mstored, sstored = (q(n) for n in (
            "go", "side_in", "maxed", "steps", "faded", "valued", "summed", "carried", "mstored", "sstored"))
        hs, ml, ml2, cp = q("hscan"), q("logit"), q("weighted"), q("copy")
        tr, ts, lg, ls, t1 = q("tr"), q("ts"), q("lg"), q("ls"), q("act")
        GR = [(4 * g, min(4, TS // 2 - 4 * g)) for g in range(-(-TS // 8))]
        NGR = len(GR)
        with ExitStack() as c, nc.Block() as block:
            idx = [alloc(c, f"idx{b}", [P, TS], I32) for b in range(2)]
            rows = [alloc(c, f"rows{b}", [P, TS, W_]) for b in range(2)]
            side = alloc(c, "side", [P, TS, F])
            L1b = alloc(c, "logits", [P, TS, F]) if one else None
            Hh = alloc(c, "H", [P, TS + 1, F])
            XB, PB = alloc(c, "XB", [P, TS, F]), alloc(c, "PB", [P, TS, F])
            VB = alloc(c, "VB", [P, TS, F])
            DN = alloc(c, "DN", [P, TS, 2 * F])
            if one:
                aT_ = [alloc(c, f"attrT{n}", [P, 4, P]) for n in range(2)]
                pt = [ps(c, f"pt{n}", [P, 4, P]) for n in range(2)]
                pl = [ps(c, f"pl{n}", [P, 4, P]) for n in range(2)]

            def lg_of(b):
                return L1b[:, :, :] if one else rows[b][:, :, 0:F]

            def val_of(b):
                return rows[b][:, :, :] if one else rows[b][:, :, F:2 * F]

            @block.sync
            def _(sp):
                def load_side(i, b, array):
                    ch = i * 2 + b
                    if not isinstance(i, int) or i or b:
                        if one:
                            sp.wait_ge(tr, ch * NGR)
                        else:
                            sp.wait_ge(valued, ch)
                    sp.dma_start(side[:, :, :], cols(array, ch, TS)).then_inc(side_in, 16)

                def load_indices(i, b):
                    if not isinstance(i, int) or i:
                        sp.wait_ge(rows_in[b], i * 16 * TS)
                    sp.dma_start(idx[b][:, :], cols(idx_arr, i * 2 + b, TS)).then_inc(idx_in[b], 16)

                def step(i, b, last=False):
                    ch = i * 2 + b
                    if one:
                        with sp.If(in_order > P - 1):
                            load_side(i, b, attr64_0)
                        with sp.Else():
                            load_side(i, b, attr64_s)
                        sp.end_ifs()
                    else:
                        load_side(i, b, dists)
                    if not last:
                        load_indices(*((i, 1) if b == 0 else (i + 1, 0)))
                    if not isinstance(i, int) or i or b:
                        store(ch - 1)

                def store(ch):
                    sp.wait_ge(maxed, ch + 1)
                    sp.dma_start(cols(maxes, ch, TS), Hh[:, 0:TS, :]).then_inc(mstored, 16)
                    sp.wait_ge(summed, (ch + 1) * 2 * F)
                    sp.dma_start(cols(sums2[0:EP, :], ch, TS), DN[:, :, :]).then_inc(sstored, 16)
                load_indices(0, 0)
                step(0, 0)
                step(0, 1)
                with sp.Fori(1, NC // 2 - 1) as i:
                    step(i, 0)
                    step(i, 1)
                step(NC // 2 - 1, 0)
                step(NC // 2 - 1, 1, last=True)
                store(NC - 1)
                sp.wait_ge(mstored, NC * 16)
                sp.wait_ge(sstored, NC * 16)

            @block.gpsimd
            def _(pool):
                gathers(pool, table, idx, rows, idx_in, rows_in,
                        lambda e, i, b: e.wait_ge(valued, i * 2 + b - 1), go, TS, NC)

            @block.tensor
            def _(pe):
                def step(i, b):
                    ch = i * 2 + b
                    pe.wait_ge(side_in, ch * 16 + 16)
                    for g, (h0, n) in enumerate(GR):
                        z = (b * NGR + g) % 2
                        first = (isinstance(i, int) and i == 0) and b * NGR + g < 2
                        if not first:
                            pe.wait_ge(ts, ch * NGR + g - 1)
                        for h in range(n):
                            r = side[:, 2 * (h0 + h):2 * (h0 + h) + 2, :].rearrange("p a f -> p (a f)")
                            t = pe.transpose(pt[z][:, h, :], r, ident[:, :])
                        t.then_inc(tr, 1)
                        pe.wait_ge(ts, ch * NGR + g + 1)
                        if not first:
                            pe.wait_ge(ls, ch * NGR + g - 1)
                        for h in range(n):
                            t = pe.matmul(pl[z][:, h, :], aT_[z][:, h, :], bd["fcr"][:, :], start=True, stop=True)
                        t.then_inc(lg, 1)
                if one:
                    pairs(pe, step, NC)

            @block.scalar
            def _(act):
                def logits(i, b):
                    ch = i * 2 + b
                    for g, (h0, n) in enumerate(GR):
                        z = (b * NGR + g) % 2
                        act.wait_ge(tr, ch * NGR + g + 1)
                        if not ((isinstance(i, int) and i == 0) and b * NGR + g < 2):
                            act.wait_ge(lg, ch * NGR + g - 1)
                        act.activation(aT_[z][:, 0:n, :], pt[z][:, 0:n, :], ACT.Copy).then_inc(ts, 1)
                        act.wait_ge(lg, ch * NGR + g + 1)
                        if g == 0 and not (isinstance(i, int) and i == 0 and b == 0):
                            act.wait_ge(valued, ch)
                        act.activation(L1b[:, 2 * h0:2 * (h0 + n), :].rearrange("p a f -> p (a f)"),
                                       pl[z][:, 0:n, :].rearrange("p a f -> p (a f)"), ACT.Copy).then_inc(ls, 1)

                def fades(i, b):
                    ch = i * 2 + b
                    act.wait_ge(dk, ch + 1)
                    if not (isinstance(i, int) and i == 0 and b == 0):
                        act.wait_ge(summed, ch * 2 * F)
                    act.activation(PB[:, :, :], XB[:, :, :], ACT.Relu, scale=-1.0).then_inc(t1, 1)
                    act.wait_ge(t1, ch * 2 + 1)
                    act.activation(PB[:, :, :], PB[:, :, :], ACT.Exp, scale=-1.0).then_inc(faded, 1)
                    act.activation(XB[:, :, :], XB[:, :, :], ACT.Relu).then_inc(t1, 1)
                    act.wait_ge(t1, ch * 2 + 2)
                    act.activation(XB[:, :, :], XB[:, :, :], ACT.Exp, scale=-1.0).then_inc(faded, 1)
                if one:
                    logits(0, 0)
                    fades(0, 0)
                    logits(0, 1)
                    fades(0, 1)
                    with act.Fori(1, NC // 2) as i:
                        logits(i, 0)
                        fades(i, 0)
                        logits(i, 1)
                        fades(i, 1)
                else:
                    pairs(act, fades, NC)

            @block.vector
            def _(dve):
                dve.memset(last[:, :], 0.0).then_inc(carried, 1)
                dve.memset(Hh[:, TS, :], -BIG).then_inc(cp, 1)

                def step(i, b):
                    ch = i * 2 + b
                    first = isinstance(i, int) and i == 0 and b == 0
                    l, v = lg_of(b), val_of(b)
                    dve.wait_ge(cp, ch * 2 + 1)
                    if not first:
                        dve.wait_ge(mstored, ch * 16)
                    dve.tensor_copy(Hh[:, 0, :], Hh[:, TS, :]).then_inc(cp, 1)
                    if one:
                        dve.wait_ge(ls, (ch + 1) * NGR)
                    else:
                        dve.wait_ge(side_in, ch * 16 + 16)
                        dve.wait_ge(rows_in[b], (i + 1) * 16 * TS)
                        dve.tensor_tensor(l, side[:, :, :], l, ALU.subtract).then_inc(ml, 1)
                        dve.wait_ge(ml, ch + 1)
                    dve.wait_ge(cp, ch * 2 + 2)
                    k = neg[:, bass.ds(ch * TS, TS)]
                    for f in range(F):
                        dve.tensor_tensor_scan(Hh[:, 1:TS + 1, f], l[:, :, f], k, Hh[:, 0, f:f + 1],
                                               ALU.max, ALU.add).then_inc(hs, 1)
                    dve.wait_ge(hs, (ch + 1) * F)
                    if not first:
                        dve.wait_ge(summed, ch * 2 * F)
                    dve.tensor_tensor(XB[:, :, :], l, Hh[:, 0:TS, :], ALU.subtract).then_inc(dk, 1)
                    dve.wait_ge(dk, ch + 1)
                    dve.tensor_tensor(Hh[:, 0:TS, :], Hh[:, 0:TS, :], l, ALU.max).then_inc(maxed, 1)
                    if one:
                        dve.wait_ge(rows_in[b], (i + 1) * 16 * TS)
                        dve.tensor_tensor(VB[:, :, :], v, l, ALU.add).then_inc(valued, 1)
                    else:
                        dve.tensor_tensor(VB[:, :, :], v, side[:, :, :], ALU.add).then_inc(valued, 1)
                    dve.wait_ge(valued, ch + 1)
                    dve.wait_ge(maxed, ch + 1)
                    dve.tensor_copy(lastmax[:, :], Hh[:, TS - 1, :]).then_inc(cp, 1)
                    dve.wait_ge(faded, ch * 2 + 1)
                    dve.tensor_tensor(VB[:, :, :], VB[:, :, :], PB[:, :, :], ALU.mult).then_inc(ml2, 1)
                    dve.wait_ge(faded, ch * 2 + 2)
                    dve.wait_ge(ml2, ch + 1)
                    dve.wait_ge(carried, ch + 1)
                    if not first:
                        dve.wait_ge(sstored, ch * 16)
                    for s_, a in enumerate((PB, VB)):
                        for f in range(F):
                            dve.tensor_tensor_scan(DN[:, :, s_ * F + f], XB[:, :, f], a[:, :, f],
                                                   last[:, s_ * F + f:s_ * F + f + 1], ALU.mult, ALU.add).then_inc(summed, 1)
                    dve.wait_ge(summed, (ch + 1) * 2 * F)
                    dve.tensor_copy(last[:, :], DN[:, TS - 1, :]).then_inc(carried, 1)
                pairs(dve, step, NC)

    @phase
    def carry(name, o, src, last, lastmax):
        W_ = 2 * F if lastmax is not None else F
        soft = lastmax is not None
        tr, tb, up, fx = sem(f"{name}_T"), sem(f"{name}_carryT"), sem(f"{name}_carry"), sem(f"{name}_first")
        f_in, f_out = sem(f"{name}_first_in"), sem(f"{name}_first_out")
        ex = sem(f"{name}_exps")
        nk = 3 if soft else 1
        with ExitStack() as c, nc.Block() as block:
            pT = [ps(c, f"pT{n}", [F, P]) for n in range(nk)]
            pB = [ps(c, f"pB{n}", [P, F]) for n in range(nk)]
            lT = [alloc(c, f"lT{n}", [F, P]) for n in range(nk)]
            cT = [alloc(c, f"cT{n}", [F, P + 1]) for n in range(nk)]
            nT, dT, eT = (alloc(c, f"xT{n}", [F, P]) for n in range(3))
            cin = alloc(c, "cin", [P, nk * F])
            row, mrow = alloc(c, "row", [P, W_]), alloc(c, "mrow", [P, F])
            M, e1, e2 = (alloc(c, f"e{n}", [P, F]) for n in range(3))
            parts = [lastmax[:, :], last[:, 0:F], last[:, F:2 * F]] if soft else [last[:, :]]

            @block.tensor
            def _(pe):
                for n, part in enumerate(parts):
                    t = pe.transpose(pT[n][:, :], part, ident[:, :])
                t.then_inc(tr, 1)
                pe.wait_ge(tb, 1)
                for n in range(nk):
                    t = pe.transpose(pB[n][:, :], cT[n][:, 0:P], ident[0:F, 0:F])
                t.then_inc(up, 1)

            @block.scalar
            def _(act):
                if soft:
                    link = linker(act, "act")
                    for k in (1, 3):
                        act.wait_ge(ex, k)
                        a, b_ = (dT, eT) if k == 1 else (e1, e2)
                        link(act.activation(a[:, :], a[:, :], ACT.Exp))
                        link(act.activation(b_[:, :], b_[:, :], ACT.Exp))
                        act.sem_inc(ex, 1)

            @block.vector
            def _(dve):
                link = linker(dve, "dve")
                dve.wait_ge(tr, 1)
                for n in range(nk):
                    link(dve.tensor_copy(lT[n][:, :], pT[n][:, :]))
                    link(dve.memset(cT[n][:, :], -BIG if soft and n == 0 else 0.0))
                if soft:
                    link(dve.tensor_scalar(nT[:, :], aT[o][:, :], 1.0, BIG, ALU.subtract, ALU.mult))
                    link(dve.tensor_tensor_scan(cT[0][:, 1:P + 1], nT[:, :], lT[0][:, :], -BIG, ALU.add, ALU.max))
                    link(dve.tensor_tensor(dT[:, :], cT[0][:, 0:P], cT[0][:, 1:P + 1], ALU.subtract))
                    link(dve.tensor_scalar(dT[:, :], dT[:, :], 0.0, None, ALU.min))
                    link(dve.tensor_tensor(eT[:, :], lT[0][:, :], cT[0][:, 1:P + 1], ALU.subtract))
                    dve.sem_inc(ex, 1)
                    dve.wait_ge(ex, 2)
                    link(dve.tensor_tensor(dT[:, :], dT[:, :], aT[o][:, :], ALU.mult))
                    for n in (1, 2):
                        link(dve.tensor_tensor(lT[n][:, :], lT[n][:, :], eT[:, :], ALU.mult))
                        link(dve.tensor_tensor_scan(cT[n][:, 1:P + 1], dT[:, :], lT[n][:, :], 0.0, ALU.mult, ALU.add))
                else:
                    link(dve.tensor_tensor_scan(cT[0][:, 1:P + 1], aT[o][:, :], lT[0][:, :], 0.0, ALU.mult, ALU.add))
                dve.sem_inc(tb, 1)
                dve.wait_ge(up, 1)
                for n in range(nk):
                    link(dve.tensor_copy(cin[:, n * F:(n + 1) * F], pB[n][:, :]))
                dve.wait_ge(f_in, (2 if soft else 1) * 16)
                if soft:
                    link(dve.tensor_scalar(cin[:, 0:3 * F], cin[:, 0:3 * F], fk[o][:, 0:1], None, ALU.mult))
                    link(dve.tensor_scalar(M[:, 0:1], fk[o][:, 0:1], 1.0, BIG, ALU.subtract, ALU.mult))
                    link(dve.tensor_scalar(e1[:, :], cin[:, 0:F], M[:, 0:1], None, ALU.add))
                    link(dve.tensor_tensor(M[:, :], e1[:, :], mrow[:, :], ALU.max))
                    link(dve.tensor_tensor(e1[:, :], e1[:, :], M[:, :], ALU.subtract))
                    link(dve.tensor_tensor(e2[:, :], mrow[:, :], M[:, :], ALU.subtract))
                    dve.sem_inc(ex, 1)
                    dve.wait_ge(ex, 4)
                    for n in range(2):
                        a, b_ = row[:, n * F:(n + 1) * F], cin[:, (n + 1) * F:(n + 2) * F]
                        link(dve.tensor_tensor(a, a, e2[:, :], ALU.mult))
                        link(dve.tensor_tensor(b_, b_, e1[:, :], ALU.mult))
                        link(dve.tensor_tensor(a, a, b_, ALU.add))
                else:
                    link(dve.scalar_tensor_tensor(row[:, :], cin[:, :], fk[o][:, 0:1], row[:, :], ALU.mult, ALU.add))
                dve.sem_inc(fx, 1)

            @block.gpsimd
            def _(pool):
                link = linker(pool, "pool")
                link(pool.memset(row[:, :], 0.0))
                link(pool.memset(mrow[:, :], 0.0))
                off = lambda: bass.IndirectOffsetOnAxis(ap=end0[o][:, 0:1], axis=0)
                pool.indirect_dma_start(row[:, :], None, src[0:EP, :], off(), bounds_check=EP - 1, oob_is_err=False).then_inc(f_in, 16)
                if soft:
                    pool.indirect_dma_start(mrow[:, :], None, maxes, off(), bounds_check=EP - 1, oob_is_err=False).then_inc(f_in, 16)
                pool.wait_ge(fx, 1)
                pool.indirect_dma_start(src[0:EP, :], off(), row[:, :], None, bounds_check=EP - 1, oob_is_err=False).then_inc(f_out, 16)
                pool.wait_ge(f_out, 16)

    def bc(t):
        return t[:, :].unsqueeze(1).to_broadcast([P, G, F])

    def pc(t):
        return t.unsqueeze(2).to_broadcast([P, G, F])

    @phase
    def node_phase(name, math, fetch=None, norm=False, weights=(), source=None, loop=None, vectors=(), stores=(),
                   finish=None, norms_to=None, spread_from=None, before=(), after=()):
        q = lambda n: sem(f"{name}_{n}")
        n_in = [q(f"rows{z}") for z in range(2)]
        used, vec_in, ready, turned, lhs, prod, evac, fin, stored = (q(n) for n in (
            "rows_used", "vectors", "ready", "turned", "lhs", "product", "product_out", "finished", "stored"))
        fvar, froot = q("squares"), q("norms")
        ex_in = [q(f"table_in{z}") for z in range(2)]
        var, root, lp, spr, keyin, first_in, first_out = (q(n) for n in (
            "var", "root", "loop_product", "spread", "first_key", "first_in", "first_out"))
        H = G // 2
        with ExitStack() as c, nc.Block() as block:
            W_ = fetch[2] if fetch else 0
            rows = [alloc(c, f"rows{z}", [P, G, W_]) for z in range(2)] if fetch else [None, None]
            vec = [alloc(c, f"vec{n}", [P, F]) for n in range(len(vectors))]
            small = [alloc(c, f"small{n}", [P, G]) for n in range(3)]
            sq = alloc(c, "sq", [P, G, F])
            if loop:
                ex = [alloc(c, f"ex{z}", [P, G, F]) for z in range(2)]
                pL = [ps(c, f"pL{z}", [P, 8, P]) for z in range(2)]
            if weights:
                pO = [ps(c, f"pO{z}", [P, 8, P]) for z in range(1 if loop else 2)]
            if loop or weights:
                pT, xT = ps(c, "pTn", [P, 8, P]), alloc(c, "xTn", [P, H, P])
            if spread_from is not None:
                key0, row0 = alloc(c, "key0", [P, 2], I32), alloc(c, "row0", [P, F + 1])
            nw = len(weights)
            turns = {"n": 0}
            for part in before:
                part(c, block)

            def uses(g, w=0):
                return g * nw + w

            @block.sync
            def _(sp):
                for t, v in zip(vec, vectors):
                    sp.dma_start(t[:, :], v.rearrange("(a n) -> a n", a=1).to_broadcast([P, F])).then_inc(vec_in, 16)
                if spread_from is not None:
                    sp.dma_start(key0[:, :], skey[1:EP + 1].rearrange("(p t) -> p t", p=P)[:, 0:2]).then_inc(keyin, 16)

                def load(g):
                    if g >= 2:
                        sp.wait_ge(used, g - 1)
                    sp.dma_start(ex[g % 2][:, :, :], loop[0].rearrange("(p j) f -> p j f", p=P)[:, g * G:(g + 1) * G, :]).then_inc(ex_in[g % 2], 16)
                if loop:
                    load(0)
                    load(1)
                for g in range(NG):
                    if loop and g + 2 < NG:
                        load(g + 2)
                    for dst, tile in stores:
                        if finish or not nw:
                            sp.wait_ge(fin, g + 1)
                        else:
                            sp.wait_ge(evac, uses(g + 1))
                        sp.dma_start(dst.rearrange("(p j) f -> p j f", p=P)[:, g * G:(g + 1) * G, :], tile(g)).then_inc(stored, 16)
                if stores:
                    sp.wait_ge(stored, 16 * NG * len(stores))
                if spread_from is not None:
                    sp.wait_ge(first_in, 16)
                    sp.wait_ge(spr, 16 * NJ)
                    sp.dma_start(spread.rearrange("(p t) f -> p t f", p=P)[:, 0, :], row0[:, :]).then_inc(first_out, 16)
                    sp.wait_ge(first_out, 16)

            @block.gpsimd
            def _(pool):
                def spread_group(g):
                    pool.wait_ge(fin, g + 1)
                    for j in range(g * G, (g + 1) * G):
                        pool.indirect_dma_start(spread, bass.IndirectOffsetOnAxis(ap=startp[:, j:j + 1], axis=0),
                                                spread_from[:, j, :], None, bounds_check=EP - 1, oob_is_err=False).then_inc(spr, 16)
                for g in range(NG):
                    if fetch:
                        if g >= 2:
                            pool.wait_ge(used, g - 1)
                        for j in range(G):
                            off = bass.IndirectOffsetOnAxis(ap=endp[fetch[0]][:, g * G + j:g * G + j + 1], axis=0)
                            pool.indirect_dma_start(rows[g % 2][:, j, :], None, fetch[1], off).then_inc(n_in[g % 2], 16)
                    if spread_from is not None and g >= 2:
                        spread_group(g - 2)
                if spread_from is not None:
                    spread_group(NG - 2)
                    spread_group(NG - 1)
                    pool.wait_ge(stored, 16 * NG * len(stores))
                    pool.wait_ge(keyin, 16)
                    pool.indirect_dma_start(row0[:, :], None, tab65, bass.IndirectOffsetOnAxis(ap=key0[:, 0:1], axis=0)).then_inc(first_in, 16)
                    pool.wait_ge(spr, 16 * NJ)

            @block.vector
            def _(dve):
                link = linker(dve, "dve")
                if vectors:
                    dve.wait_ge(vec_in, 16 * len(vectors))

                def finish_group(g):
                    dve.wait_ge(evac, uses(g + 1))
                    finish(dve, link, g, small[2], vec, sq)
                    dve.sem_inc(fvar, 1)
                    dve.wait_ge(froot, g + 1)
                    dve.sem_inc(fin, 1)
                for g in range(NG):
                    if fetch:
                        dve.wait_ge(n_in[g % 2], 16 * G * (g // 2 + 1))
                    if loop:
                        dve.wait_ge(lp, g + 1)
                    extra = (ex[g % 2], pL[g % 2]) if loop else None
                    if math:
                        math(dve, link, g, rows[g % 2], small, vec, extra)
                    if norm:
                        x = X[:, g * G:(g + 1) * G, :]
                        mean, v = small[0], small[1]
                        link(dve.reduce_sum(mean[:, :], x, axis=AX.X))
                        link(dve.tensor_scalar(mean[:, :], mean[:, :], 1.0 / F, None, ALU.mult))
                        link(dve.tensor_tensor(x, x, pc(mean[:, :]), ALU.subtract))
                        link(dve.tensor_tensor(sq[:, :, :], x, x, ALU.mult))
                        link(dve.reduce_sum(v[:, :], sq[:, :, :], axis=AX.X))
                        link(dve.tensor_scalar(v[:, :], v[:, :], 1.0 / F, EPS, ALU.mult, ALU.add))
                        dve.sem_inc(var, 1)
                        dve.wait_ge(root, g + 1)
                        link(dve.reciprocal(v[:, :], v[:, :]))
                        link(dve.tensor_tensor(x, x, pc(v[:, :]), ALU.mult))
                    dve.sem_inc(used, 1)
                    if nw:
                        dve.sem_inc(ready, 1)
                        if finish and g:
                            finish_group(g - 1)
                    else:
                        dve.sem_inc(fin, 1)
                if nw and finish:
                    finish_group(NG - 1)

            def turn(eng, src_of):
                k = turns["n"]
                if k:
                    eng.wait_ge(lhs, k)
                for h in range(H):
                    t = eng.transpose(pT[:, h, :], src_of[:, 2 * h:2 * h + 2, :].rearrange("p a f -> p (a f)"), ident[:, :])
                t.then_inc(turned, 1)
                eng.wait_ge(lhs, k + 1)
                turns["n"] += 1

            @block.tensor
            def _(pe):
                def loop_group(g):
                    pe.wait_ge(ex_in[g % 2], 16 * (g // 2 + 1))
                    turn(pe, ex[g % 2])
                    if g >= 2:
                        pe.wait_ge(used, g - 1)
                    for h in range(H):
                        t = pe.matmul(pL[g % 2][:, h, :], xT[:, h, :], loop[1][:, :], start=True, stop=True)
                    t.then_inc(lp, 1)
                if loop:
                    loop_group(0)
                for g in range(NG):
                    if loop and g + 1 < NG:
                        loop_group(g + 1)
                    if not nw:
                        continue
                    pe.wait_ge(ready, g + 1)
                    turn(pe, source(g, rows[g % 2]))
                    for w, (weight, dst) in enumerate(weights):
                        n = uses(g, w)
                        if n >= len(pO):
                            pe.wait_ge(evac, n - len(pO) + 1)
                        for h in range(H):
                            t = pe.matmul(pO[n % len(pO)][:, h, :], xT[:, h, :], weight[:, :], start=True, stop=True)
                        t.then_inc(prod, 1)

            @block.scalar
            def _(act):
                k = [0]

                def norm_column(g):
                    act.wait_ge(fvar, g + 1)
                    act.activation(norms_to[:, g * G:(g + 1) * G, F], small[2][:, :], ACT.Sqrt).then_inc(froot, 1)

                def copy_turn():
                    k[0] += 1
                    act.wait_ge(turned, k[0])
                    act.activation(xT[:, :, :], pT[:, 0:H, :], ACT.Copy).then_inc(lhs, 1)
                if loop:
                    copy_turn()
                for g in range(NG):
                    if loop and g + 1 < NG:
                        copy_turn()
                    if norm:
                        act.wait_ge(var, g + 1)
                        act.activation(small[1][:, :], small[1][:, :], ACT.Sqrt).then_inc(root, 1)
                    if nw:
                        copy_turn()
                        for w, (weight, dst) in enumerate(weights):
                            n = uses(g, w)
                            act.wait_ge(prod, n + 1)
                            act.activation(dst[:, g * G:(g + 1) * G, :],
                                           pO[n % len(pO)][:, 0:H, :].rearrange("p h (a f) -> p (h a) f", f=F), ACT.Copy).then_inc(evac, 1)
                        if finish and g:
                            norm_column(g - 1)
                if finish:
                    norm_column(NG - 1)
            for part in after:
                part(c, block)

    @phase
    def similarity_pass(last):
        W_ = F + 1
        S = lambda n: [sem(f"L2_{n}{b}") for b in range(2)]
        q = lambda n: sem(f"L2_{n}")
        idx_in, rows_in, side_in = S("idx"), S("rows"), S("side")
        go, filled, steps, msg, scanned, carried, stored = (q(n) for n in (
            "go", "filled", "steps", "msg", "scanned", "carried", "stored"))
        with ExitStack() as c, nc.Block() as block:
            idx = [alloc(c, f"idx{b}", [P, T], I32) for b in range(2)]
            rows = [alloc(c, f"rows{b}", [P, T, W_]) for b in range(2)]
            own = [alloc(c, f"own{b}", [P, T, W_]) for b in range(2)]
            base = [alloc(c, f"base{b}", [P, T]) for b in range(2)]
            tmp = alloc(c, "tmp", [P, T, F])
            lastu = alloc(c, "lastu", [P, W_])
            dot, nn, a, b2 = (alloc(c, f"s{n}", [P, T]) for n in range(4))

            @block.sync
            def _(sp):
                def load_indices(i, b):
                    if not isinstance(i, int) or i:
                        sp.wait_ge(rows_in[b], i * 16 * T)
                    sp.dma_start(idx[b][:, :], cols(sdst, i * 2 + b)).then_inc(idx_in[b], 16)

                def step(i, b, last=False):
                    ch = i * 2 + b
                    if not isinstance(i, int) or i:
                        sp.wait_ge(msg, ch - 1)
                    if not last:
                        load_indices(*((i, 1) if b == 0 else (i + 1, 0)))
                    sp.dma_start(own[b][:, :, :], cols(spread, ch)).then_inc(side_in[b], 16)
                    sp.dma_start(base[b][:, :], cols(sbase, ch)).then_inc(side_in[b], 16)
                    if not isinstance(i, int) or i or b:
                        store(ch - 1)

                def store(ch):
                    sp.wait_ge(scanned, (ch + 1) * F)
                    sp.dma_start(cols(sums[0:EP, :], ch), tmp[:, :, :]).then_inc(stored, 16)
                load_indices(0, 0)
                step(0, 0)
                step(0, 1)
                with sp.Fori(1, NCH // 2 - 1) as i:
                    step(i, 0)
                    step(i, 1)
                step(NCH // 2 - 1, 0)
                step(NCH // 2 - 1, 1, last=True)
                store(NCH - 1)
                sp.wait_ge(stored, NCH * 16)

            @block.gpsimd
            def _(pool):
                gathers(pool, tab65, idx, rows, idx_in, rows_in, lambda e, i, b: e.wait_ge(msg, i * 2 + b - 1), go, T, NCH)

            @block.vector
            def _(dve):
                dve.memset(last[:, :], 0.0).then_inc(carried, 1)
                dve.memset(lastu[:, :], 0.0).then_inc(carried, 1)
                NS = 10

                def step(i, b):
                    ch = i * 2 + b
                    first = isinstance(i, int) and i == 0 and b == 0
                    k = keep["s"][:, bass.ds(ch * T, T)]
                    dve.wait_ge(side_in[b], (i + 1) * 32)
                    dve.wait_ge(carried, ch * 2 + 2)
                    u, g = own[b], rows[b]
                    for f in range(W_):
                        dve.tensor_tensor_scan(u[:, :, f], k, u[:, :, f], lastu[:, f:f + 1], ALU.mult, ALU.add).then_inc(filled, 1)
                    dve.wait_ge(filled, (ch + 1) * W_)
                    dve.tensor_copy(lastu[:, :], u[:, T - 1, :]).then_inc(carried, 1)
                    dve.wait_ge(rows_in[b], (i + 1) * 16 * T)
                    if not first:
                        dve.wait_ge(stored, ch * 16)
                    n = [0]

                    def link(ins):
                        n[0] += 1
                        ins.then_inc(steps, 1)
                        dve.wait_ge(steps, ch * NS + n[0])
                    link(dve.tensor_tensor(tmp[:, :, :], u[:, :, 0:F], g[:, :, 0:F], ALU.mult))
                    link(dve.reduce_sum(dot[:, :], tmp[:, :, :], axis=AX.X))
                    link(dve.tensor_tensor(nn[:, :], u[:, :, F], g[:, :, F], ALU.mult))
                    link(dve.tensor_scalar(nn[:, :], nn[:, :], 1e-8, None, ALU.max))
                    link(dve.reciprocal(a[:, :], nn[:, :]))
                    link(dve.tensor_tensor(dot[:, :], dot[:, :], a[:, :], ALU.mult))
                    link(dve.tensor_scalar(a[:, :], dot[:, :], 0.0, co[:, 4:5], ALU.max, ALU.mult))
                    link(dve.tensor_scalar(b2[:, :], dot[:, :], 0.0, co[:, 5:6], ALU.min, ALU.mult))
                    link(dve.tensor_tensor(a[:, :], a[:, :], b2[:, :], ALU.add))
                    link(dve.tensor_tensor(a[:, :], a[:, :], base[b][:, :], ALU.mult))
                    dve.tensor_tensor(tmp[:, :, :], g[:, :, 0:F], a[:, :].unsqueeze(2).to_broadcast([P, T, F]), ALU.mult).then_inc(msg, 1)
                    dve.wait_ge(msg, ch + 1)
                    for f in range(F):
                        dve.tensor_tensor_scan(tmp[:, :, f], k, tmp[:, :, f], last[:, f:f + 1], ALU.mult, ALU.add).then_inc(scanned, 1)
                    dve.wait_ge(scanned, (ch + 1) * F)
                    dve.tensor_copy(last[:, :], tmp[:, T - 1, :]).then_inc(carried, 1)
                pairs(dve, step)

    def distance_weights(c, block):
        ld, ce, st, rd = sem("dw_loaded"), sem("dw_centred"), sem("dw_stored"), sem("dw_back")
        centred = dram("centred", [5, F])
        w = alloc(c, "w5", [5, F])
        m = alloc(c, "m5", [5, 1])
        zs = sem("dw_zeroed")

        @block.sync
        def _(sp):
            sp.dma_start(w[0:3, :], W["L3_gnn_Wd1"]).then_inc(ld, 16)
            sp.dma_start(w[3:4, :], W["L3_gnn_bd1"].rearrange("(a n) -> a n", a=1)).then_inc(ld, 16)
            sp.dma_start(w[4:5, :], W["L3_gnn_bd2"].rearrange("(a n) -> a n", a=1)).then_inc(ld, 16)
            for n in ("g1", "b1", "g2", "b2"):
                sp.dma_start(dist_v[n][:, :], W[f"L3_gnn_{n}"].rearrange("(a n) -> a n", a=1).to_broadcast([P, F])).then_inc(ld, 16)
            sp.wait_ge(ce, 1)
            sp.dma_start(centred, w[:, :]).then_inc(st, 16)
            sp.wait_ge(st, 16)
            sp.wait_ge(zs, 2)
            for t in range(DW):
                sp.dma_start(dist_w[3 * t:3 * t + 3, t * F:(t + 1) * F], centred[0:3, :]).then_inc(rd, 16)
            sp.dma_start(dist_w[F:F + 1, :].rearrange("a (t f) -> a t f", f=F),
                         centred[3:4, :].unsqueeze(1).to_broadcast([1, DW, F])).then_inc(rd, 16)
            sp.dma_start(dist_b2[:, :].rearrange("a (t f) -> a t f", f=F),
                         centred[4:5, :].unsqueeze(1).to_broadcast([1, 8, F])).then_inc(rd, 16)
            sp.dma_start(sums[EP:ROWS, :], dist_w[0:1, (DW - 1) * F:DW * F]).then_inc(rd, 16)
            sp.wait_ge(rd, 16 * (DW + 3))

        @block.vector
        def _(dve):
            link = linker(dve, "dve")
            dve.memset(dist_w[:, :], 0.0).then_inc(zs, 1)
            dve.memset(ones_row[:, :], 1.0).then_inc(zs, 1)
            dve.wait_ge(ld, 16 * 7)
            link(dve.reduce_sum(m[:, :], w[:, :], axis=AX.X))
            link(dve.tensor_scalar(m[:, :], m[:, :], 1.0 / F, None, ALU.mult))
            link(dve.tensor_scalar(w[:, :], w[:, :], m[:, 0:1], None, ALU.subtract))
            dve.sem_inc(ce, 1)

    constants()
    in_order = nc.values_load(sorted_p[0:1, 0:1], min_val=0, max_val=P)
    with nc.If(in_order < P):
        nc.all_engine_barrier()
        sort_by_dst()
    nc.end_ifs()

    def group(t):
        return lambda g: t[:, g * G:(g + 1) * G, :]

    def xg(g, rows):
        return X[:, g * G:(g + 1) * G, :]

    with ExitStack() as c:
        A = alloc(c, "A", [P, NJ, F])
        node_phase("x_W1", None, weights=[(bd["a1"], A)], source=xg, stores=[(tab, group(A))],
                   before=[distance_weights], after=[edge_weights])
    quarter = 0
    masks_of = {"d": lambda c, block: masks("d", dst_in, c, block), "s": lambda c, block: masks("s", skey, c, block)}
    for conv in range(2):
        for o, keys in (("d", src_in), ("s", sdst)):
            with ExitStack() as c:
                last = alloc(c, "last", [P, F])
                first_pass = quarter == 0
                if first_pass:
                    hist = {k: alloc(c, f"hist_{k}", [P, P]) for k in "ds"}
                    first_row = alloc(c, "first_row", [P, P])
                name = f"conv{conv}{o}"
                sum_pass(name, o, keys, tab, last, quarter, hist if first_pass else None,
                         beside=[masks_of[o]] if conv == 0 else [])
                quarter += 1
                if first_pass:
                    pointers(hist, first_row, "s")
                carry(name, o, sums, last, None)
                with ExitStack() as cc:
                    A = alloc(cc, "A", [P, NJ, F])
                    a_g = group(A)
                    if o == "d":
                        def mean_of_edges(dve, link, g, rows, small, vec, extra):
                            link(dve.tensor_tensor(a_g(g), rows[:, :, :], pc(inv["d"][:, g * G:(g + 1) * G]), ALU.mult))
                        node_phase(name + "n", mean_of_edges, fetch=("d", sums, F), stores=[(tab, a_g)])
                    elif conv == 0:
                        def hidden(dve, link, g, rows, small, vec, extra):
                            link(dve.tensor_tensor(rows[:, :, :], rows[:, :, :], pc(inv["s"][:, g * G:(g + 1) * G]), ALU.mult))
                            link(dve.tensor_tensor(rows[:, :, :], rows[:, :, :], bc(vec[0]), ALU.add))
                            link(dve.tensor_scalar(a_g(g), rows[:, :, :], 0.0, None, ALU.max))
                        A2 = alloc(cc, "A2", [P, NJ, F])
                        node_phase(name + "n", hidden, fetch=("s", sums, F), weights=[(bd["a2"], A2)],
                                   source=lambda g, rows: a_g(g), vectors=[W["L0_gnn_b1"]], stores=[(tab, group(A2))])
                    else:
                        def convolved(dve, link, g, rows, small, vec, extra):
                            link(dve.tensor_tensor(rows[:, :, :], rows[:, :, :], pc(inv["s"][:, g * G:(g + 1) * G]), ALU.mult))
                            link(dve.tensor_tensor(rows[:, :, :], rows[:, :, :], bc(vec[0]), ALU.add))
                            link(dve.tensor_tensor(xg(g, 0), xg(g, 0), rows[:, :, :], ALU.add))
                        node_phase(name + "n", convolved, fetch=("s", sums, F), norm=True, weights=[(bd["fc"], A)], source=xg,
                                   vectors=[W["L0_gnn_b2"]], stores=[(tab, a_g)])
                if first_pass:
                    sort_edges(first_row, src_in, dst_in[1:EP + 1], base_in)
                    unpack_sorted(skey, sdst, sbase)

    def mean_of_values(dve, link, rows):
        den, num = rows[:, :, 0:F], rows[:, :, F:2 * F]
        link(dve.tensor_scalar(den, den, 1e-30, None, ALU.max))
        link(dve.reciprocal(den, den))
        link(dve.tensor_tensor(num, num, den, ALU.mult))
        return num

    with ExitStack() as c1:
        last, lastmax = alloc(c1, "last", [P, 2 * F]), alloc(c1, "lastmax", [P, F])
        softmax_pass("L1", src_in, tab, last, lastmax)
        carry("L1", "d", sums2, last, lastmax)
        WH = alloc(c1, "WH", [P, NJ, F + 1])
        with ExitStack() as c:

            def attended(dve, link, g, rows, small, vec, extra):
                h, hl = extra
                num, has = mean_of_values(dve, link, rows), small[2]
                hl = hl[:, 0:G // 2, :].rearrange("p h (a f) -> p (h a) f", f=F)
                link(dve.tensor_tensor(num, num, hl, ALU.add))
                link(dve.tensor_scalar(has[:, :], inv["d"][:, g * G:(g + 1) * G], 0.0, None, ALU.is_gt))
                link(dve.tensor_tensor(num, num, pc(has[:, :]), ALU.mult))
                link(dve.tensor_scalar(has[:, :], has[:, :], -1.0, 1.0, ALU.mult, ALU.add))
                link(dve.tensor_tensor(h[:, :, :], h[:, :, :], pc(has[:, :]), ALU.mult))
                link(dve.tensor_tensor(num, num, h[:, :, :], ALU.add))
                link(dve.tensor_scalar(num, num, 0.0, None, ALU.max))
                link(dve.tensor_tensor(xg(g, 0), xg(g, 0), num, ALU.add))

            def norms(dve, link, g, squares, vec, sq):
                wh = WH[:, g * G:(g + 1) * G, 0:F]
                link(dve.tensor_tensor(wh, wh, bc(vec[0]), ALU.add))
                link(dve.tensor_tensor(sq[:, :, :], wh, wh, ALU.mult))
                link(dve.reduce_sum(squares[:, :], sq[:, :, :], axis=AX.X))
            node_phase("L1n", attended, fetch=("d", sums2, 2 * F), norm=True, weights=[(bd["w2l"], WH[:, :, 0:F])], source=xg,
                       loop=(tab, bd["loop"]), vectors=[W["L2_gnn_b"]], finish=norms, norms_to=WH,
                       stores=[(tab65, group(WH))], spread_from=WH)

        with ExitStack() as c:
            last = alloc(c, "last", [P, F])
            similarity_pass(last)
            carry("L2", "s", sums, last, None)
            Q = alloc(c, "Q", [P, NJ, 2 * F])

            def propagated(dve, link, g, rows, small, vec, extra):
                wh = WH[:, g * G:(g + 1) * G, 0:F]
                link(dve.scalar_tensor_tensor(rows[:, :, :], wh, co[:, 6:7], rows[:, :, :], ALU.mult, ALU.add))
                link(dve.tensor_tensor(xg(g, 0), xg(g, 0), rows[:, :, :], ALU.add))
            node_phase("L2n", propagated, fetch=("s", sums, F), norm=True, source=xg,
                       weights=[(bd["q2"], Q[:, :, 0:F]), (bd["q3"], Q[:, :, F:2 * F])], stores=[(tab128, group(Q))])

    with ExitStack() as c:
        last, lastmax = alloc(c, "last", [P, 2 * F]), alloc(c, "lastmax", [P, F])
        softmax_pass("L3", src_in, tab128, last, lastmax)
        carry("L3", "d", sums2, last, lastmax)

        def summed(dve, link, g, rows, small, vec, extra):
            link(dve.tensor_tensor(xg(g, 0), xg(g, 0), mean_of_values(dve, link, rows), ALU.add))
        node_phase("L3n", summed, fetch=("d", sums2, 2 * F), norm=True, stores=[(out, group(X))])
    top.close()


_WEIGHTS = ["L0_gnn_W1", "L0_gnn_b1", "L0_gnn_W2", "L0_gnn_b2", "L1_gnn_W_fc", "L1_gnn_W_fcr", "L1_gnn_loop_W",
            "L2_gnn_W", "L2_gnn_b", "L2_gnn_deg_coeff", "L2_gnn_coeff_param", "L2_gnn_scale_param",
            "L3_gnn_Wd1", "L3_gnn_bd1", "L3_gnn_g1", "L3_gnn_b1", "L3_gnn_Wd2", "L3_gnn_bd2", "L3_gnn_g2", "L3_gnn_b2",
            "L3_gnn_W2", "L3_gnn_W3"]


def kernel(**inputs):
    import numpy as _np
    import concourse.bacc as _bacc
    from concourse import mybir as _mybir
    from concourse.bass_utils import run_bass_kernel_spmd as _run

    def padded(a, n, value=0, before=0):
        a = _np.asarray(a)
        o = _np.full((n,) + a.shape[1:], value, a.dtype)
        o[before:before + a.shape[0]] = a
        return o

    arrays = {
        "x": padded(inputs["x"], NP),
        "src": padded(inputs["src"], EP, N),
        "dst": _np.concatenate([_np.full(1, -1, _np.int32), padded(inputs["dst"], EP, N), _np.full(1, -1, _np.int32)]),
        "attr3": padded(inputs["edge_attr_3"], EP),
        "attr64": padded(inputs["edge_attr_64"], EP),
        "w": padded(inputs["edge_weight"], EP),
        "w2": padded(inputs["edge_weight_n2"], EP),
    }
    for name in _WEIGHTS:
        arrays[name] = _np.ascontiguousarray(inputs[name])
    nc = _bacc.Bacc("TRN2", target_bir_lowering=False, num_devices=1)
    arrays = {f"in_{k}": _np.ascontiguousarray(v) for k, v in arrays.items()}
    ap = {k: nc.dram_tensor(k, v.shape, _mybir.dt.from_np(v.dtype), kind="ExternalInput").ap() for k, v in arrays.items()}
    out = nc.dram_tensor("out_0", (NP, F), _mybir.dt.float32, kind="ExternalOutput").ap()
    gnn_resnorm(nc, ap["in_x"], ap["in_src"], ap["in_dst"], ap["in_attr3"], ap["in_attr64"], ap["in_w"], ap["in_w2"],
                {n: ap[f"in_{n}"] for n in _WEIGHTS}, out)
    r = _run(nc, [arrays], core_ids=[0])
    return r.results[0]["out_0"][:N]
```
